# Optimizing a Trainium2 kernel written in Bass

```python
import numpy as np
import jax
import jax.numpy as jnp

def _softmax(x, axis=-1):
    return jax.nn.softmax(x, axis=axis)

def _gelu(x):
    return jax.nn.gelu(x, approximate=True)

def _silu(x):
    return jax.nn.silu(x)

def _sigmoid(x):
    return jax.nn.sigmoid(x)

def _layernorm(x, axis=-1, eps=1e-05):
    m = jnp.mean(x, axis=axis, keepdims=True)
    v = jnp.var(x, axis=axis, keepdims=True)
    return (x - m) / jnp.sqrt(v + eps)

def _scatter_add(tgt, idx, src, axis=0):
    return tgt.at[idx].add(src)

def _segment_sum(src, seg, n):
    return jax.ops.segment_sum(src, seg, n)
kernel_name = 'mk_perceiver_d1_seqx_r2_70e0b2'

def setup_inputs(seed: int=0):
    np.random.seed(seed)
    _w = jnp.asarray

    def _rec_inputs():
        import jax
        import jax.numpy as jnp
        _rk = jax.random.key(seed)
        x = 7.22e-05 + 1 * jax.random.normal(jax.random.fold_in(_rk, 1), (16, 64, 512), jnp.float32)
        _lenS = 64 - jax.random.randint(jax.random.fold_in(_rk, 7), (16,), 0, max(1, 64 // 4) + 1, jnp.int32)
        _lenS2 = 512 - jax.random.randint(jax.random.fold_in(_rk, 8), (16,), 0, max(1, 512 // 4) + 1, jnp.int32)
        _ctx_1024P = jax.random.normal(jax.random.fold_in(_rk, 11), (16, 16, 512), jnp.float32)
        _ctx_1024c = jax.random.dirichlet(jax.random.fold_in(_rk, 511), 0.3 * jnp.ones((16,), jnp.float32), (16, 512))
        _ctx_1024t = jnp.einsum('bsk,bkd->bsd', _ctx_1024c, _ctx_1024P)
        _ctx_1024t = _ctx_1024t * jax.lax.rsqrt(jnp.mean(jnp.square(_ctx_1024t)) + 1e-12) * 0.953939
        ctx_1024 = 4.13588e-05 + 0.999923 * (_ctx_1024t + 0.3 * jax.random.normal(jax.random.fold_in(_rk, 611), (16, 512, 512), jnp.float32))
        return (x, ctx_1024)
    x, ctx_1024 = _rec_inputs()

    def _L0_xattn_setup():
        import jax, jax.numpy as jnp
        import numpy as np
        D_MODEL = 512
        N_HEADS = 16
        D_HEAD = D_MODEL // N_HEADS

        def _split_heads(x):
            b, s, _ = x.shape
            return x.reshape(b, s, N_HEADS, D_HEAD).transpose(0, 2, 1, 3)
        key = jax.random.key(seed)
        ks = jax.random.split(key, 11)
        B, S = (4, 1024)
        scale = 1.0 / np.sqrt(D_MODEL)
        inp = {'query': jax.random.normal(ks[0], (B, S, D_MODEL), jnp.float32), 'key': jax.random.normal(ks[1], (B, S, D_MODEL), jnp.float32), 'value': jax.random.normal(ks[2], (B, S, D_MODEL), jnp.float32), 'Wq': jax.random.normal(ks[3], (D_MODEL, D_MODEL), jnp.float32) * scale, 'bq': jnp.zeros((D_MODEL,), jnp.float32), 'Wk': jax.random.normal(ks[4], (D_MODEL, D_MODEL), jnp.float32) * scale, 'bk': jnp.zeros((D_MODEL,), jnp.float32), 'Wv': jax.random.normal(ks[5], (D_MODEL, D_MODEL), jnp.float32) * scale, 'bv': jnp.zeros((D_MODEL,), jnp.float32), 'Wo': jax.random.normal(ks[6], (D_MODEL, D_MODEL), jnp.float32) * scale, 'bo': jnp.zeros((D_MODEL,), jnp.float32)}
        return inp
    _L0_xattn_all = _L0_xattn_setup()
    _L0_xattn_in = {k: v for k, v in _L0_xattn_all.items() if k in ('Wq', 'bq', 'Wk', 'bk', 'Wv', 'bv', 'Wo', 'bo')}
    del _L0_xattn_all

    def _L0_attn_setup():
        import jax, jax.numpy as jnp
        import numpy as np
        from jax import lax
        D_MODEL, D_STATE, D_CONV, D_INNER, DT_RANK = (512, 16, 4, 1024, 64)
        B_SZ, SEQ = (2, 512)

        def silu(v):
            return v * jax.nn.sigmoid(v)

        def _mamba_fwd(x, W_in, conv_w, conv_b, W_x, W_dt, b_dt, A_log, D, W_out):
            b, l, _ = x.shape
            xz = x @ W_in
            x_e, z = jnp.split(xz, 2, axis=-1)
            xc = lax.conv_general_dilated(x_e.transpose(0, 2, 1), conv_w, window_strides=(1,), padding=[(D_CONV - 1, 0)], dimension_numbers=('NCH', 'OIH', 'NCH'), feature_group_count=D_INNER)
            xc = (xc + conv_b[None, :, None]).transpose(0, 2, 1)
            xc = silu(xc)
            x_dbl = xc @ W_x
            delta_r = x_dbl[..., :DT_RANK]
            Bmat = x_dbl[..., DT_RANK:DT_RANK + D_STATE]
            Cmat = x_dbl[..., DT_RANK + D_STATE:]
            delta = jax.nn.softplus(delta_r @ W_dt + b_dt)
            A = -jnp.exp(A_log)
            deltaA = jnp.exp(delta[..., None] * A[None, None])
            deltaB_x = delta[..., None] * Bmat[:, :, None, :] * xc[..., None]

            def combine(left, right):
                a_l, b_l = left
                a_r, b_r = right
                return (a_r * a_l, a_r * b_l + b_r)
            _, H = lax.associative_scan(combine, (deltaA, deltaB_x), axis=1)
            y = jnp.einsum('bldn,bln->bld', H, Cmat) + xc * D[None, None, :]
            y = y * silu(z)
            return y @ W_out
        key = jax.random.key(seed)
        ks = jax.random.split(key, 10)
        s = lambda fan: 1.0 / np.sqrt(fan)
        x = jax.random.normal(ks[0], (B_SZ, SEQ, D_MODEL), jnp.float32)
        W_in = jax.random.normal(ks[1], (D_MODEL, 2 * D_INNER), jnp.float32) * s(D_MODEL)
        conv_w = jax.random.normal(ks[2], (D_INNER, 1, D_CONV), jnp.float32) * s(D_CONV)
        conv_b = jax.random.normal(ks[3], (D_INNER,), jnp.float32) * 0.01
        W_x = jax.random.normal(ks[4], (D_INNER, DT_RANK + 2 * D_STATE), jnp.float32) * s(D_INNER)
        W_dt = jax.random.normal(ks[5], (DT_RANK, D_INNER), jnp.float32) * s(DT_RANK)
        b_dt = jax.random.normal(ks[6], (D_INNER,), jnp.float32) * 0.01
        A_log = jnp.log(jnp.tile(jnp.arange(1, D_STATE + 1, dtype=jnp.float32), (D_INNER, 1)))
        Dparam = jnp.ones((D_INNER,), jnp.float32)
        W_out = jax.random.normal(ks[7], (D_INNER, D_MODEL), jnp.float32) * s(D_INNER)
        return {'x': x, 'W_in': W_in, 'conv_w': conv_w, 'conv_b': conv_b, 'W_x': W_x, 'W_dt': W_dt, 'b_dt': b_dt, 'A_log': A_log, 'D': Dparam, 'W_out': W_out}
    _L0_attn_all = _L0_attn_setup()
    _L0_attn_in = {k: v for k, v in _L0_attn_all.items() if k in ('W_in', 'conv_w', 'conv_b', 'W_x', 'W_dt', 'b_dt', 'A_log', 'D', 'W_out')}
    del _L0_attn_all

    def _L0_ffn_setup():
        import jax, jax.numpy as jnp
        import numpy as np
        B, T = (2, 1024)
        D_MODEL, D_HIDDEN = (512, 1024)
        N_EXPERTS, TOP_K = (8, 2)
        N_TOKENS = B * T
        CAPACITY = 2 * N_TOKENS * TOP_K // N_EXPERTS
        key = jax.random.key(seed)
        k_x, k_rw, k_w, k_v, k_o = jax.random.split(key, 5)
        x = jax.random.normal(k_x, (B, T, D_MODEL), jnp.float32)
        router_w = jax.random.normal(k_rw, (N_EXPERTS, D_MODEL), jnp.float32) * D_MODEL ** (-0.5)
        router_b = jnp.zeros((N_EXPERTS,), jnp.float32)
        W = jax.random.normal(k_w, (N_EXPERTS, D_MODEL, D_HIDDEN), jnp.float32) * D_MODEL ** (-0.5)
        V = jax.random.normal(k_v, (N_EXPERTS, D_MODEL, D_HIDDEN), jnp.float32) * D_MODEL ** (-0.5)
        W_out = jax.random.normal(k_o, (N_EXPERTS, D_HIDDEN, D_MODEL), jnp.float32) * D_HIDDEN ** (-0.5)
        return {'x': x, 'router_w': router_w, 'router_b': router_b, 'W': W, 'V': V, 'W_out': W_out}
    _L0_ffn_all = _L0_ffn_setup()
    _L0_ffn_in = {k: v for k, v in _L0_ffn_all.items() if k in ('router_w', 'router_b', 'W', 'V', 'W_out')}
    del _L0_ffn_all
    return {'x': x, 'ctx_1024': ctx_1024, 'L0_xattn_Wq': _L0_xattn_in['Wq'], 'L0_xattn_bq': _L0_xattn_in['bq'], 'L0_xattn_Wk': _L0_xattn_in['Wk'], 'L0_xattn_bk': _L0_xattn_in['bk'], 'L0_xattn_Wv': _L0_xattn_in['Wv'], 'L0_xattn_bv': _L0_xattn_in['bv'], 'L0_xattn_Wo': _L0_xattn_in['Wo'], 'L0_xattn_bo': _L0_xattn_in['bo'], 'L0_attn_W_in': _L0_attn_in['W_in'], 'L0_attn_conv_w': _L0_attn_in['conv_w'], 'L0_attn_conv_b': _L0_attn_in['conv_b'], 'L0_attn_W_x': _L0_attn_in['W_x'], 'L0_attn_W_dt': _L0_attn_in['W_dt'], 'L0_attn_b_dt': _L0_attn_in['b_dt'], 'L0_attn_A_log': _L0_attn_in['A_log'], 'L0_attn_D': _L0_attn_in['D'], 'L0_attn_W_out': _L0_attn_in['W_out'], 'L0_ffn_router_w': _L0_ffn_in['router_w'], 'L0_ffn_router_b': _L0_ffn_in['router_b'], 'L0_ffn_W': _L0_ffn_in['W'], 'L0_ffn_V': _L0_ffn_in['V'], 'L0_ffn_W_out': _L0_ffn_in['W_out']}

def reference(x, ctx_1024, L0_xattn_Wq, L0_xattn_bq, L0_xattn_Wk, L0_xattn_bk, L0_xattn_Wv, L0_xattn_bv, L0_xattn_Wo, L0_xattn_bo, L0_attn_W_in, L0_attn_conv_w, L0_attn_conv_b, L0_attn_W_x, L0_attn_W_dt, L0_attn_b_dt, L0_attn_A_log, L0_attn_D, L0_attn_W_out, L0_ffn_router_w, L0_ffn_router_b, L0_ffn_W, L0_ffn_V, L0_ffn_W_out):
    import jax
    import jax.numpy as jnp

    def _L0_xattn_ref(query, key, value, Wq, bq, Wk, bk, Wv, bv, Wo, bo):
        import jax, jax.numpy as jnp
        import numpy as np
        D_MODEL = 512
        N_HEADS = 16
        D_HEAD = D_MODEL // N_HEADS

        def _split_heads(x):
            b, s, _ = x.shape
            return x.reshape(b, s, N_HEADS, D_HEAD).transpose(0, 2, 1, 3)
        Q = _split_heads(query @ Wq + bq)
        K = _split_heads(key @ Wk + bk)
        V = _split_heads(value @ Wv + bv)
        scores = jnp.einsum('bhqd,bhkd->bhqk', Q, K) / jnp.sqrt(jnp.float32(D_HEAD))
        attn = jax.nn.softmax(scores, axis=-1)
        context = jnp.einsum('bhqk,bhkd->bhqd', attn, V)
        b, h, s, dh = context.shape
        context = context.transpose(0, 2, 1, 3).reshape(b, s, D_MODEL)
        return context @ Wo + bo

    def _L0_attn_ref(x, W_in, conv_w, conv_b, W_x, W_dt, b_dt, A_log, D, W_out):
        import jax, jax.numpy as jnp
        import numpy as np
        from jax import lax
        D_MODEL, D_STATE, D_CONV, D_INNER, DT_RANK = (512, 16, 4, 1024, 64)
        B_SZ, SEQ = (2, 512)

        def silu(v):
            return v * jax.nn.sigmoid(v)

        def _mamba_fwd(x, W_in, conv_w, conv_b, W_x, W_dt, b_dt, A_log, D, W_out):
            b, l, _ = x.shape
            xz = x @ W_in
            x_e, z = jnp.split(xz, 2, axis=-1)
            xc = lax.conv_general_dilated(x_e.transpose(0, 2, 1), conv_w, window_strides=(1,), padding=[(D_CONV - 1, 0)], dimension_numbers=('NCH', 'OIH', 'NCH'), feature_group_count=D_INNER)
            xc = (xc + conv_b[None, :, None]).transpose(0, 2, 1)
            xc = silu(xc)
            x_dbl = xc @ W_x
            delta_r = x_dbl[..., :DT_RANK]
            Bmat = x_dbl[..., DT_RANK:DT_RANK + D_STATE]
            Cmat = x_dbl[..., DT_RANK + D_STATE:]
            delta = jax.nn.softplus(delta_r @ W_dt + b_dt)
            A = -jnp.exp(A_log)
            deltaA = jnp.exp(delta[..., None] * A[None, None])
            deltaB_x = delta[..., None] * Bmat[:, :, None, :] * xc[..., None]

            def combine(left, right):
                a_l, b_l = left
                a_r, b_r = right
                return (a_r * a_l, a_r * b_l + b_r)
            _, H = lax.associative_scan(combine, (deltaA, deltaB_x), axis=1)
            y = jnp.einsum('bldn,bln->bld', H, Cmat) + xc * D[None, None, :]
            y = y * silu(z)
            return y @ W_out
        return _mamba_fwd(x, W_in, conv_w, conv_b, W_x, W_dt, b_dt, A_log, D, W_out)

    def _L0_ffn_ref(x, router_w, router_b, W, V, W_out):
        import jax, jax.numpy as jnp
        import numpy as np
        B, T = (2, 1024)
        D_MODEL, D_HIDDEN = (512, 1024)
        N_EXPERTS, TOP_K = (8, 2)
        N_TOKENS = B * T
        CAPACITY = 2 * N_TOKENS * TOP_K // N_EXPERTS
        Bq, Tq, D = x.shape
        N = Bq * Tq
        x_flat = x.reshape(N, D)
        router_logits = x_flat @ router_w.T + router_b
        top_vals, top_ids = jax.lax.top_k(router_logits, TOP_K)
        top_probs = jax.nn.softmax(top_vals, axis=-1)
        x_pad = jnp.concatenate([x_flat, jnp.zeros((1, D), x_flat.dtype)], axis=0)
        probs_pad = jnp.concatenate([top_probs, jnp.zeros((1, TOP_K), top_probs.dtype)], axis=0)
        out = jnp.zeros((N + 1, D), x_flat.dtype)
        for e in range(N_EXPERTS):
            tok, slot = jnp.nonzero(top_ids == e, size=CAPACITY, fill_value=(N, 0))
            w = probs_pad[tok, slot][:, None]
            xin = x_pad[tok]
            a = xin @ W[e]
            b = xin @ V[e]
            y = a * (b * jax.nn.sigmoid(b)) @ W_out[e]
            out = out.at[tok].add(y * w)
        return out[:N].reshape(Bq, Tq, D)
    x = x + _L0_xattn_ref(_layernorm(x, axis=-1), ctx_1024, ctx_1024, L0_xattn_Wq, L0_xattn_bq, L0_xattn_Wk, L0_xattn_bk, L0_xattn_Wv, L0_xattn_bv, L0_xattn_Wo, L0_xattn_bo)
    x = x + _L0_attn_ref(_layernorm(x, axis=-1), L0_attn_W_in, L0_attn_conv_w, L0_attn_conv_b, L0_attn_W_x, L0_attn_W_dt, L0_attn_b_dt, L0_attn_A_log, L0_attn_D, L0_attn_W_out)
    x = x + _L0_ffn_ref(_layernorm(x, axis=-1), L0_ffn_router_w, L0_ffn_router_b, L0_ffn_W, L0_ffn_V, L0_ffn_W_out)
    return x

_drawn_inputs = setup_inputs


def setup_inputs(seed=0):
    import zlib

    import numpy as np

    out = dict(_drawn_inputs(seed))
    spreads = {'L0_xattn_bq': (0.0, 0.1),
     'L0_xattn_bk': (0.0, 0.8),
     'L0_xattn_bv': (0.0, 0.1),
     'L0_xattn_bo': (0.0, 0.1),
     'L0_attn_D': (1.0, 0.2),
     'L0_ffn_router_b': (0.0, 0.1)}
    factors = {'L0_attn_conv_b': 2.969, 'L0_attn_b_dt': 6.943}
    for name, (base, spread) in spreads.items():
        noise = np.random.default_rng([zlib.crc32(name.encode()), seed]).standard_normal(out[name].shape)
        drawn = base * np.exp(spread * noise) if base else spread * noise
        out[name] = jnp.asarray(drawn.astype(out[name].dtype))
    for name, factor in factors.items():
        out[name] = (out[name] * factor).astype(out[name].dtype)
    return out
```

```python
from contextlib import ExitStack

import concourse.bass as bass
from concourse import mybir

F32 = mybir.dt.float32
I32 = mybir.dt.int32
U32 = mybir.dt.uint32
ALU = mybir.AluOpType
ACT = mybir.ActivationFunctionType
AX = mybir.AxisListType

P = 128
EPS = 1e-5
ds = bass.ds


class Chain:

    def __init__(self, eng, sem):
        self.eng, self.sem, self.base, self.k, self.outer = eng, sem, 0, 0, []

    def count(self, ins):
        ins.then_inc(self.sem, 1)
        self.k += 1
        return self.base + self.k

    def link(self, ins):
        self.eng.wait_ge(self.sem, self.count(ins))

    def enter(self, i, per):
        self.outer.append((self.base, self.k, per))
        self.base, self.k = self.base + self.k + i * per, 0

    def leave(self, times):
        base, k, per = self.outer.pop()
        assert self.k == per, (self.k, per)
        self.base, self.k = base, k + per * times


def build(nc, a, out, debug=None):
    x_d = a["x"].rearrange("b s d -> (b s) d")
    ctx_d = a["ctx_1024"]
    out_d = out.rearrange("b s d -> (b s) d")
    B, S, D = a["x"].shape
    CK = ctx_d.shape[1]
    KD = D // P
    KC = CK // P
    TOK = B * S
    NT = TOK // P
    H, DH = 16, 32
    NP = H // 2
    SCALE = float(DH) ** -0.5
    DI = a["L0_attn_D"].shape[0]
    JD = DI // P
    N = a["L0_attn_A_log"].shape[1]
    R = a["L0_attn_W_dt"].shape[0]
    HT = TOK // 2
    HB = B // 2
    E = a["L0_ffn_router_w"].shape[0]
    FH = a["L0_ffn_W"].shape[2]
    JF = FH // P
    NS = 2 * TOK // P + E - 1

    whole = ExitStack()

    def pool(stack):
        def sb(name, shape, dt=F32):
            return stack.enter_context(nc.sbuf_tensor(name, shape, dt))

        def ps(name, shape):
            return stack.enter_context(nc.psum_tensor(name, shape, F32))

        def sem(name):
            return stack.enter_context(nc.semaphore(name))
        return sb, ps, sem

    with whole:
        sb0, _, sem0 = pool(whole)
        xres = sb0("xres", [P, NT, D])
        xnT = sb0("xnT", [P, KD, TOK])
        ident = sb0("ident", [P, P])
        zeros = sb0("zeros", [P, D])
        xs_d = nc.dram_tensor("slot_rows_scratch", (NS * P, D), F32).ap()
        ys_d = nc.dram_tensor("slot_out_scratch", (NS * P, D), F32).ap()
        z_ok, xs_zero = sem0("zeros_ready"), sem0("slot_rows_zeroed")
        x_in, ident0, ident_ok = sem0("x_in"), sem0("ident_zeroed"), sem0("ident_ready")

        carried = sem0("waits_carried")

        def plain(eng):
            eng.sem_inc(carried, 1)

        with nc.Block() as block:
            @block.sync
            def _(sp):
                sp.dma_start(xres[:, :, :], x_d.rearrange("(t p) d -> p t d", p=P)).then_inc(x_in, 16)
                sp.wait_ge(z_ok, 1)
                sp.dma_start(xs_d.rearrange("(s p) d -> p s d", p=P),
                             zeros[:, :].unsqueeze(1).to_broadcast([P, NS, D])).then_inc(xs_zero, 16)
                sp.wait_ge(x_in, 16)

            @block.gpsimd
            def _(pl):
                pl.memset(zeros[:, :], 0.0).then_inc(z_ok, 1)
                pl.memset(ident[:, :], 0.0).then_inc(ident0, 1)
                pl.wait_ge(ident0, 1)
                pl.affine_select(out=ident[:, :], in_=ident[:, :], compare_op=ALU.not_equal, fill=1.0,
                                 base=0, pattern=[[-1, P]], channel_multiplier=1).then_inc(ident_ok, 1)
                pl.wait_ge(ident_ok, 1)

        def norm_phase(tag, keep=None):
            with ExitStack() as st:
                sb, ps, sem = pool(st)
                stats = sb(tag + "stats", [P, NT, nc.vector.BN_STATS_DIM])
                mv = sb(tag + "mv", [P, NT, nc.vector.BN_AGGR_DIM])
                veps, std, rstd = (sb(tag + n, [P, NT]) for n in ("var_eps", "std", "rstd"))
                var_ready, std_ready = sem(tag + "var_ready"), sem(tag + "std_ready")
                xn = sb(tag + "xn", [P, 2, D])
                bank = [ps(tag + f"bank{i}", [P, KD, P]) for i in range(2)]
                chain = sem(tag + "dve_chain")
                xn_ready = sem(tag + "xn_ready")
                turned = sem(tag + "xn_turned")
                copied = sem(tag + "xnT_copied")
                kept = sem(tag + "xn_kept")
                with nc.Block() as block:
                    @block.vector
                    def _(dve):
                        for t in range(NT):
                            dve.bn_stats(stats[:, t, :], xres[:, t, :]).then_inc(chain, 1)
                        dve.wait_ge(chain, NT)
                        for t in range(NT):
                            dve.bn_aggr(mv[:, t, :], stats[:, t, :]).then_inc(chain, 1)
                        dve.wait_ge(chain, 2 * NT)
                        dve.tensor_scalar(veps[:, :], mv[:, :, 1:2].rearrange("p t o -> p (t o)"), EPS, None,
                                          ALU.add).then_inc(var_ready, 1)
                        dve.wait_ge(std_ready, 1)
                        dve.reciprocal(rstd[:, :], std[:, :]).then_inc(chain, 1)
                        dve.wait_ge(chain, 2 * NT + 1)
                        for t in range(NT):
                            dve.wait_ge(turned, t + 1)
                            if keep is not None:
                                dve.wait_ge(kept, t + 1)
                            dve.tensor_scalar(xn[:, t % 2, :], xres[:, t, :], mv[:, t, 0:1], rstd[:, t:t + 1],
                                              ALU.subtract, ALU.mult).then_inc(xn_ready, 1)

                    @block.tensor
                    def _(pe):
                        pe.sem_inc(turned, 2)
                        with pe.Fori(0, NT // 2) as i:
                            for b in range(2):
                                t = 2 * i + b
                                pe.wait_ge(xn_ready, t + 1)
                                pe.wait_ge(copied, t + 1)
                                for k in range(KD):
                                    mm = pe.transpose(bank[b][:, k, :], xn[:, b, k * P:(k + 1) * P], ident[:, :])
                                mm.then_inc(turned, 1)

                    @block.scalar
                    def _(act):
                        act.sem_inc(copied, 2)
                        act.wait_ge(var_ready, 1)
                        act.activation(std[:, :], veps[:, :], ACT.Sqrt).then_inc(std_ready, 1)
                        with act.Fori(0, NT // 2) as i:
                            for b in range(2):
                                t = 2 * i + b
                                act.wait_ge(turned, 2 + t + 1)
                                act.activation(xnT[:, :, ds(t * P, P)], bank[b][:, :, :], ACT.Copy).then_inc(copied, 1)

                    if keep is not None:
                        @block.gpsimd
                        def _(pl):
                            pl.sem_inc(kept, 2)
                            with pl.Fori(0, NT // 2) as i:
                                for b in range(2):
                                    t = 2 * i + b
                                    pl.wait_ge(xn_ready, t + 1)
                                    pl.tensor_copy(keep[:, t, :], xn[:, b, :]).then_inc(kept, 1)

        norm_phase("n1_")

        with ExitStack() as st:
            sb, ps, sem = pool(st)
            Wk, Wv, Wo = (sb(n, [P, KD, D]) for n in ("Wk", "Wv", "Wo"))
            ctxs = sb("ctx_rows", [P, 2, KC, D])
            Wq = sb("Wq", [P, KD, D])
            ctxT = sb("ctxT", [P, 2, KD, CK])
            KT = sb("KT", [P, 2, KD, CK])
            V = sb("V", [P, 2, KC, D])
            QT = sb("QT", [P, KD, TOK])
            qbd = [sb(f"q_blocks{i}", [P, KD, P]) for i in range(2)]
            head_of = sb("head_parity", [P, 2])
            prob = sb("prob", [P, 2, CK])
            probT = sb("probT", [P, 2, KC, P])
            nmax = sb("neg_max", [P, 2, NP])
            rsum = sb("row_sum", [P, 2, NP])
            rinv = sb("row_inv", [P, 2, NP])
            cn = sb("context", [P, D])
            cnT = sb("contextT", [P, KD, P])
            bias = {n: sb(n, [P, KD]) for n in ("bq", "bk", "bv")}
            bqs = sb("bq_scaled", [P, KD])
            bo = sb("bo_rows", [P, D])
            bankT = ps("bankT", [P, KC, P])
            bankJ = [ps(f"bankJ{i}", [P, CK]) for i in range(2)]
            bankS = [ps(f"bankS{i}", [P, CK]) for i in range(2)]
            bankP = ps("bankP", [P, KC, P])
            bankO = ps("bankO", [P, NP, 2 * DH])
            bankX = ps("bankX", [P, D])

            wq_in, w_in, o_in, b_in = sem("wq_in"), sem("wkv_in"), sem("wo_in"), sem("b_in")
            ctx_in = [sem(f"ctx_in{i}") for i in range(2)]
            chain = sem("a_dve_chain")
            bqs_ok = sem("bqs_ready")
            q_mm, q_ok = sem("q_projected"), sem("qT_ready")
            mask_ok, qb = sem("head_mask_ready"), sem("q_blocks_ready")
            t_mm, t_cp = sem("ctx_turned"), sem("ctxT_copied")
            j_mm, j_cp = sem("kv_projected"), sem("kv_copied")
            s_mm, s_max = sem("scores_ready"), sem("max_ready")
            s_exp = sem("probs_ready")
            p_mm, p_cp = sem("probs_turned"), sem("probT_copied")
            o_mm = sem("pv_done")
            c_cp = sem("context_copied")
            ct_mm, ct_cp = sem("context_turned"), sem("contextT_copied")
            y_mm, y_add = sem("wo_done"), sem("x_added")
            xbo = sem("bo_added")

            with nc.Block() as block:
                @block.sync
                def _(sp):
                    sp.dma_start(Wq[:, :, :], a["L0_xattn_Wq"].rearrange("(k p) n -> p k n", p=P)).then_inc(wq_in, 16)
                    for g in range(2):
                        sp.dma_start(ctxs[:, g, :, :], ctx_d[g].rearrange("(k p) d -> p k d", p=P)).then_inc(ctx_in[g], 16)
                    for n, w in (("L0_xattn_Wk", Wk), ("L0_xattn_Wv", Wv)):
                        sp.dma_start(w[:, :, :], a[n].rearrange("(k p) n -> p k n", p=P)).then_inc(w_in, 16)
                    sp.dma_start(Wo[:, :, :], a["L0_xattn_Wo"].rearrange("(k p) n -> p k n", p=P)).then_inc(o_in, 16)
                    with sp.Fori(0, NT - 1) as t:
                        for b in range(2):
                            sp.wait_ge(t_mm, KD * (2 * t + b + 1))
                            sp.dma_start(ctxs[:, b, :, :], ctx_d[ds(2 * t + b + 2, 1)].rearrange(
                                "g (k p) d -> p (g k) d", p=P)).then_inc(ctx_in[b], 16)

                @block.gpsimd
                def _(pl):
                    for n in ("bq", "bk", "bv"):
                        with nc.allow_non_contiguous_dma("bias by channel"):
                            pl.dma_start(bias[n][:, :], a["L0_xattn_" + n].rearrange("(k p) -> p k", p=P)).then_inc(b_in, 16)
                    pl.dma_start(bo[:, :], a["L0_xattn_bo"].partition_broadcast(P)).then_inc(b_in, 16)

                    def place(g, b):
                        for e in range(2):
                            pl.tensor_tensor(qbd[b][:, :, e * S:e * S + S], QT[:, :, ds(g * S, S)],
                                             head_of[:, e:e + 1].unsqueeze(2).to_broadcast([P, KD, S]),
                                             ALU.mult).then_inc(qb, 1)
                    pl.wait_ge(mask_ok, 6)
                    pl.wait_ge(q_ok, 2 + KD * 2)
                    for b in range(2):
                        place(b, b)
                    pl.wait_ge(b_in, 64)
                    for t in range(NT):
                        pl.tensor_tensor(xres[:, t, :], xres[:, t, :], bo[:, :], ALU.add).then_inc(xbo, 1)
                    with pl.Fori(0, NT - 1) as t:
                        for b in range(2):
                            pl.wait_ge(s_mm, NP * (2 * t + b + 1))
                            place(2 * t + b + 2, b)

                @block.tensor
                def _(pe):
                    pe.sem_inc(p_mm, 2)
                    pe.sem_inc(o_mm, 2)
                    pe.wait_ge(wq_in, 16)
                    for n in range(2 * KD):
                        m, h = n % KD, n // KD
                        pe.wait_ge(q_ok, n + 1)
                        for k in range(KD):
                            mm = pe.matmul(bankJ[n % 2][:, :], Wq[:, k, m * P:(m + 1) * P],
                                           xnT[:, k, h * CK:(h + 1) * CK], start=(k == 0), stop=(k == KD - 1))
                        mm.then_inc(q_mm, 1)

                    def turn(g, b, j):
                        if j == 0:
                            pe.wait_ge(ctx_in[b], 16 * (g // 2 + 1) if isinstance(g, int) else g * 8 + (16 - 8 * b))
                        pe.wait_ge(t_cp, KD * g + j + 1)
                        for k in range(KC):
                            mm = pe.transpose(bankT[:, k, :], ctxs[:, b, k, j * P:(j + 1) * P], ident[:, :])
                        mm.then_inc(t_mm, 1)

                    def project(g, b, u):
                        if u == 0:
                            pe.wait_ge(t_cp, 1 + KD * (g + 1))
                        pe.wait_ge(j_cp, NP * g + u + 1)
                        for k in range(KD):
                            if u < KD:
                                l, r = Wk[:, k, u * P:(u + 1) * P], ctxT[:, b, k, :]
                            else:
                                l, r = ctxT[:, b, k, (u - KD) * P:(u - KD + 1) * P], Wv[:, k, :]
                            mm = pe.matmul(bankJ[u % 2][:, :], l, r, start=(k == 0), stop=(k == KD - 1))
                        mm.then_inc(j_mm, 1)

                    def scores(g, b, u):
                        if u == 0:
                            pe.wait_ge(qb, 2 * (g + 1))
                        pe.wait_ge(j_cp, 2 + NP * g + u // 2 + 1)
                        pe.wait_ge(s_exp, NP * g + u + 1)
                        r = slice(64 * (u % 2), 64 * (u % 2) + 64)
                        pe.matmul(bankS[u % 2][:, :], qbd[b][r, u // 2, :], KT[r, b, u // 2, :],
                                  start=True, stop=True).then_inc(s_mm, 1)

                    def turn_probs(g, u):
                        n = NP * g + u
                        pe.wait_ge(s_exp, 2 + n + 1)
                        pe.wait_ge(p_cp, n + 1)
                        for k in range(KC):
                            mm = pe.transpose(bankP[:, k, :], prob[:, u % 2, k * P:(k + 1) * P], ident[:, :])
                        mm.then_inc(p_mm, 1)

                    def values(g, b, u):
                        if u == 0:
                            pe.wait_ge(c_cp, 2 * g + 2)
                            pe.wait_ge(j_cp, 2 + NP * (g + 1))
                        pe.wait_ge(p_cp, 1 + NP * g + u + 1)
                        for k in range(KC):
                            mm = pe.matmul(bankO[:, u, :], probT[:, u % 2, k, :], V[:, b, k, 64 * u:64 * u + 64],
                                           start=(k == 0), stop=(k == KC - 1))
                        mm.then_inc(o_mm, 1)

                    def batch(g, b, nxt, nxt2):
                        scores(g, b, 0)
                        for u in range(NP):
                            if nxt:
                                project(g + 1, 1 - b, u)
                            if u + 1 < NP:
                                scores(g, b, u + 1)
                            if nxt2 and u % 2 == 0:
                                turn(g + 2, b, u // 2)
                            turn_probs(g, u)
                            if u:
                                values(g, b, u - 1)
                        values(g, b, NP - 1)

                    def finish(t):
                        pe.wait_ge(c_cp, 2 + 4 * (t + 1))
                        pe.wait_ge(y_add, t + 1)
                        for k in range(KD):
                            mm = pe.transpose(bankX[:, k * P:(k + 1) * P], cn[:, k * P:(k + 1) * P], ident[:, :])
                        mm.then_inc(ct_mm, 1)
                        pe.wait_ge(ct_cp, KD * (t + 1))
                        for k in range(KD):
                            mm = pe.matmul(bankX[:, :], cnT[:, k, :], Wo[:, k, :], start=(k == 0), stop=(k == KD - 1))
                        mm.then_inc(y_mm, 1)

                    for j in range(KD):
                        turn(0, 0, j)
                    pe.wait_ge(w_in, 32)
                    pe.wait_ge(q_ok, 2 + 2 * KD)
                    for u in range(NP):
                        project(0, 0, u)
                    for j in range(KD):
                        turn(1, 1, j)
                    pe.wait_ge(o_in, 16)
                    with pe.Fori(0, NT - 1) as t:
                        batch(2 * t, 0, True, True)
                        batch(2 * t + 1, 1, True, True)
                        finish(t)
                    batch(B - 2, 0, True, False)
                    batch(B - 1, 1, False, False)
                    finish(NT - 1)

                @block.scalar
                def _(act):
                    act.sem_inc(q_ok, 2)
                    act.sem_inc(j_cp, 2)
                    act.sem_inc(s_exp, 2)
                    act.wait_ge(b_in, 64)
                    act.activation(bqs[:, :], bias["bq"][:, :], ACT.Copy, scale=SCALE).then_inc(bqs_ok, 1)
                    act.wait_ge(bqs_ok, 1)
                    for n in range(2 * KD):
                        m, h = n % KD, n // KD
                        act.wait_ge(q_mm, n + 1)
                        act.activation(QT[:, m, h * CK:(h + 1) * CK], bankJ[n % 2][:, :], ACT.Identity,
                                       bias=bqs[:, m:m + 1], scale=SCALE).then_inc(q_ok, 1)

                    def copy_kv(g, b, u):
                        act.wait_ge(j_mm, NP * g + u + 1)
                        if u < KD:
                            act.activation(KT[:, b, u, :], bankJ[u % 2][:, :], ACT.Identity,
                                           bias=bias["bk"][:, u:u + 1]).then_inc(j_cp, 1)
                        else:
                            act.activation(V[:, b, u - KD, :], bankJ[u % 2][:, :], ACT.Copy).then_inc(j_cp, 1)

                    def batch(g, b, nxt):
                        for u in range(NP):
                            n = NP * g + u
                            act.wait_ge(s_max, n + 1)
                            act.wait_ge(p_mm, n + 1)
                            act.activation(prob[:, u % 2, :], bankS[u % 2][:, :], ACT.Exp,
                                           bias=nmax[:, b, u:u + 1],
                                           accum_out=rsum[:, b, u:u + 1]).then_inc(s_exp, 1)
                            if nxt:
                                if u == KD:
                                    act.wait_ge(o_mm, NP * g + 2)
                                copy_kv(g + 1, 1 - b, u)

                    def finish(t):
                        act.wait_ge(ct_mm, t + 1)
                        for k in range(KD):
                            act.activation(cnT[:, k, :], bankX[:, k * P:(k + 1) * P], ACT.Identity,
                                           bias=bias["bv"][:, k:k + 1]).then_inc(ct_cp, 1)

                    for u in range(NP):
                        copy_kv(0, 0, u)
                    with act.Fori(0, NT - 1) as t:
                        batch(2 * t, 0, True)
                        batch(2 * t + 1, 1, True)
                        finish(t)
                    batch(B - 2, 0, True)
                    batch(B - 1, 1, False)
                    finish(NT - 1)

                @block.vector
                def _(dve):
                    dve.sem_inc(t_cp, 1)
                    dve.sem_inc(p_cp, 1)
                    dve.sem_inc(c_cp, 2)
                    dve.sem_inc(y_add, 1)
                    c = Chain(dve, chain)
                    for e in range(2):
                        dve.memset(head_of[:, e:e + 1], 0.0).then_inc(mask_ok, 1)
                    dve.wait_ge(mask_ok, 2)
                    for hh in range(P // DH):
                        dve.memset(head_of[DH * hh:DH * hh + DH, hh % 2:hh % 2 + 1], 1.0).then_inc(mask_ok, 1)

                    def copy_ctx(g, b, j):
                        if j == 0 and not isinstance(g, int):
                            dve.wait_ge(j_mm, NP * (g - 1))
                        dve.wait_ge(t_mm, KD * g + j + 1)
                        dve.tensor_copy(ctxT[:, b, j, :], bankT[:, :, :].rearrange("p a b -> p (a b)")).then_inc(t_cp, 1)

                    def row_max(g, b, u):
                        dve.wait_ge(s_mm, NP * g + u + 1)
                        dve.tensor_reduce(nmax[:, b, u:u + 1], bankS[u % 2][:, :], AX.X, ALU.max,
                                          negate=True).then_inc(s_max, 1)

                    def copy_probs(g, u):
                        n = NP * g + u
                        dve.wait_ge(p_mm, 2 + n + 1)
                        dve.wait_ge(o_mm, n + 1)
                        dve.tensor_copy(probT[:, u % 2, :, :], bankP[:, :, :]).then_inc(p_cp, 1)

                    def batch(g, b, nxt2):
                        row_max(g, b, 0)
                        for u in range(NP):
                            if u + 1 < NP:
                                row_max(g, b, u + 1)
                            if nxt2 and u % 2 == 0:
                                copy_ctx(g + 2, b, u // 2)
                            copy_probs(g, u)
                        dve.wait_ge(s_exp, 2 + NP * (g + 1))
                        c.link(dve.reciprocal(rinv[:, b, :], rsum[:, b, :]))
                        dve.wait_ge(o_mm, 2 + NP * (g + 1))
                        for h in range(2):
                            r = slice(64 * h, 64 * h + 64)
                            dst = cn[64 * b:64 * b + 64, :].rearrange("p (u e d) -> p u e d", e=2, d=DH)[:, :, h, :]
                            dve.tensor_tensor(dst, bankO[r, :, DH * h:DH * h + DH],
                                              rinv[r, b, :].unsqueeze(2).to_broadcast([64, NP, DH]),
                                              ALU.mult).then_inc(c_cp, 1)

                    def finish(t):
                        dve.wait_ge(y_mm, t + 1)
                        dve.tensor_tensor(xres[:, ds(t, 1), :].rearrange("p a d -> p (a d)"),
                                          xres[:, ds(t, 1), :].rearrange("p a d -> p (a d)"),
                                          bankX[:, :], ALU.add).then_inc(y_add, 1)

                    for j in range(KD):
                        copy_ctx(0, 0, j)
                    for j in range(KD):
                        copy_ctx(1, 1, j)
                    dve.wait_ge(xbo, NT)
                    with dve.Fori(0, NT - 1) as t:
                        c.enter(t, 2)
                        batch(2 * t, 0, True)
                        batch(2 * t + 1, 1, True)
                        finish(t)
                        c.leave(NT - 1)
                    batch(B - 2, 0, False)
                    batch(B - 1, 1, False)
                    finish(NT - 1)

        def store_x():
            done = sem0("x_stored")
            with nc.Block() as block:
                @block.sync
                def _(sp):
                    sp.dma_start(out_d.rearrange("(t p) d -> p t d", p=P), xres[:, :, :]).then_inc(done, 16)
                    sp.wait_ge(done, 16)

        if debug == "attention":
            return store_x()
        norm_phase("n2_")
        with ExitStack() as st:
            sb, ps, sem = pool(st)
            Win = sb("Win", [P, 2, 2, KD, P])
            Wx = sb("Wx", [P, JD, R + 2 * N])
            Wdt = sb("Wdt", [R, 2, P])
            Wout = sb("Wout", [P, JD, D])
            chan = sb("channel_params", [P, JD, N + 7])
            cj = sb("channel_params_j", [P, 2, N + 7])
            BC = sb("BC_rows", [P, 2, N, HT])
            xc = sb("xc", [P, JD, HT])
            yz = sb("yz", [P, JD, HT])
            delta = sb("delta", [P, JD, HT])
            xdbl = sb("x_dbl", [R + 2 * N, HT])
            xpad = sb("x_padded", [P, 2, HB, S + 3])
            acc = sb("conv_sum", [P, 2, HT])
            dx = sb("delta_x", [P, 2, HT])
            ring = sb("ring", [P, 9, HT])
            DA, BX, HS, HC = 0, 2, 5, 7
            bc_d = nc.dram_tensor("bc_scratch", (2, 2 * N, HT), F32).ap()
            bankX = [ps(f"bankX{i}", [P, HT]) for i in range(2)]
            bankZ = [ps(f"bankZ{i}", [P, HT]) for i in range(2)]
            bankD = [ps(f"bankD{i}", [P, HT]) for i in range(2)]
            bankY = [ps(f"bankY{i}", [P, HT]) for i in range(2)]

            p_in, wx_in, wo_in = sem("params_in"), sem("wx_in"), sem("wout_in")
            win_in = [sem(f"win_in{i}") for i in range(2)]
            wdt_in = [sem(f"wdt_in{i}") for i in range(2)]
            bc_out = sem("bc_stored")
            bc_in = [sem(f"bc_in{i}") for i in range(N // 4)]
            neg_ok, pad_ok, start_ok = sem("A_ready"), sem("padding_zeroed"), sem("batch_starts_zeroed")
            x_mm, x_cp = sem("x_done"), sem("x_copied")
            z_mm, z_si = sem("z_done"), sem("z_gated")
            cv, xs = sem("conv_done"), sem("xc_done")
            bc_mm, bc_cp = sem("x_dbl_done"), sem("x_dbl_copied")
            d_mm, d_rd = sem("dt_done"), sem("dt_read")
            abs_ok = sem("minus_abs_ready")
            u_ok, l_ok, del_ok = sem("exp_done"), sem("log_done"), sem("delta_ready")
            aj = sem("channel_A_ready")
            da_ok, sc = sem("dA_ready"), sem("state_ready")
            hc_ok = sem("state_C_ready")
            y_mm = sem("y_summed")
            yo = sem("y_gated")
            o_mm, o_ad = sem("out_done"), sem("out_added")
            chain = sem("m_dve_chain")

            with nc.Block() as block:
                @block.sync
                def _(sp):
                    sp.dma_start(Wx[:, :, :], a["L0_attn_W_x"].rearrange("(j p) n -> p j n", p=P)).then_inc(wx_in, 16)
                    with sp.Fori(0, 2) as hf:
                        with sp.Fori(0, JD // 2) as jj:
                            for b in range(2):
                                J = hf * JD + 2 * jj + b
                                sp.wait_ge(z_mm, J + 1)
                                for z in range(2):
                                    sp.dma_start(Win[:, b, z, :, :], a["L0_attn_W_in"][
                                        :, ds(z * DI + (2 * jj + b) * P, P)].rearrange("(k p) n -> p k n", p=P)
                                        ).then_inc(win_in[b], 16)
                        sp.wait_ge(bc_cp, 2 * hf + 2)
                        sp.dma_start(bc_d[ds(hf, 1)].rearrange("h r t -> (h r) t"), xdbl[R:R + 2 * N, :]).then_inc(bc_out, 16)
                        sp.wait_ge(bc_out, 16 * hf + 16)
                        for q in range(N // 4):
                            src = bc_d[ds(hf, 1)].rearrange("h (s n) t -> (h s) n t", s=2)[:, 4 * q:4 * q + 4, :]
                            sp.dma_start(BC[:, :, 4 * q:4 * q + 4, :], src.partition_broadcast(P)).then_inc(bc_in[q], 16)
                        with sp.Fori(0, JD // 2) as jj:
                            for b in range(2):
                                J = hf * JD + 2 * jj + b
                                sp.wait_ge(d_mm, J + 1)
                                sp.dma_start(Wdt[:, b, :], a["L0_attn_W_dt"][:, ds((2 * jj + b) * P, P)]
                                             ).then_inc(wdt_in[b], 16)

                @block.gpsimd
                def _(pl):
                    with nc.allow_non_contiguous_dma("channel parameters"):
                        for lo, src in ((0, a["L0_attn_A_log"].rearrange("(j p) n -> p j n", p=P)),
                                        (N, a["L0_attn_D"].rearrange("(j p o) -> p j o", p=P, o=1)),
                                        (N + 1, a["L0_attn_b_dt"].rearrange("(j p o) -> p j o", p=P, o=1)),
                                        (N + 2, a["L0_attn_conv_b"].rearrange("(j p o) -> p j o", p=P, o=1)),
                                        (N + 3, a["L0_attn_conv_w"].rearrange("(j p) o k -> p j (o k)", p=P))):
                            pl.dma_start(chan[:, :, lo:lo + src.shape[2]], src).then_inc(p_in, 16)
                    pl.dma_start(Wout[:, :, :], a["L0_attn_W_out"].rearrange("(j p) n -> p j n", p=P)).then_inc(wo_in, 16)
                    pl.sem_inc(hc_ok, 2)
                    with pl.Fori(0, 2) as hf:
                        for q in range(N // 4):
                            pl.wait_ge(bc_in[q], 16 * hf + 16)
                        plain(pl)
                        with pl.Fori(0, JD) as j:
                            for n in range(N):
                                i = (hf * JD + j) * N + n
                                pl.wait_ge(sc, 2 + i + 1)
                                pl.wait_ge(y_mm, i + 1)
                                pl.tensor_tensor(ring[:, HC + n % 2, :], ring[:, HS + n % 2, :],
                                                 BC[:, 1, n, :], ALU.mult).then_inc(hc_ok, 1)

                @block.tensor
                def _(pe):
                    for s, v in ((z_mm, 2), (d_mm, 2), (y_mm, 2), (o_mm, 1)):
                        pe.sem_inc(s, v)
                    with pe.Fori(0, 2) as hf:
                        pe.wait_ge(o_ad, 2 + 4 * hf)
                        plain(pe)
                        with pe.Fori(0, JD // 2) as jj:
                            for b in range(2):
                                J = hf * JD + 2 * jj + b
                                pe.wait_ge(win_in[b], 16 * (J - b) + 32)
                                for z, bank, free, done in ((0, bankX, x_cp, x_mm), (1, bankZ, z_si, z_mm)):
                                    pe.wait_ge(free, J + 1)
                                    for k in range(KD):
                                        mm = pe.matmul(bank[b][:, :], Win[:, b, z, k, :], xnT[:, k, ds(hf * HT, HT)],
                                                       start=(k == 0), stop=(k == KD - 1))
                                    mm.then_inc(done, 1)
                        pe.wait_ge(xs, 2 + JD * (hf + 1))
                        pe.wait_ge(wx_in, 16)
                        pe.wait_ge(d_rd, JD * hf + 2)
                        for j in range(JD):
                            mm = pe.matmul(bankD[0][0:R + 2 * N, :], Wx[:, j, :], xc[:, j, :],
                                           start=(j == 0), stop=(j == JD - 1))
                        mm.then_inc(bc_mm, 1)
                        pe.wait_ge(bc_cp, 2 * hf + 2)
                        plain(pe)
                        with pe.Fori(0, JD // 2) as jj:
                            for b in range(2):
                                J = hf * JD + 2 * jj + b
                                pe.wait_ge(wdt_in[b], 8 * (J - b) + 16)
                                pe.wait_ge(d_rd, J + 1)
                                pe.matmul(bankD[b][:, :], Wdt[:, b, :], xdbl[0:R, :],
                                          start=True, stop=True).then_inc(d_mm, 1)
                        with pe.Fori(0, JD // 2) as jj:
                            for b in range(2):
                                J = hf * JD + 2 * jj + b
                                pe.wait_ge(yo, J + 1)
                                for n in range(N):
                                    pe.wait_ge(hc_ok, 2 + J * N + n + 1)
                                    pe.matmul(bankY[b][:, :], ident[:, :], ring[:, HC + n % 2, :],
                                              start=(n == 0), stop=(n == N - 1)).then_inc(y_mm, 1)
                        pe.wait_ge(yo, 2 + JD * (hf + 1))
                        pe.wait_ge(wo_in, 16)
                        for t in range(HT // P):
                            pe.wait_ge(o_ad, 4 * hf + t + 1)
                            for j in range(JD):
                                mm = pe.matmul(bankX[t % 2][:, :], yz[:, j, t * P:(t + 1) * P], Wout[:, j, :],
                                               start=(j == 0), stop=(j == JD - 1))
                            mm.then_inc(o_mm, 1)

                @block.scalar
                def _(act):
                    for s, v in ((x_cp, 2), (z_si, 2), (xs, 2)):
                        act.sem_inc(s, v)
                    act.wait_ge(p_in, 16 * 5)
                    act.activation(chan[:, :, 0:N], chan[:, :, 0:N], ACT.Exp).then_inc(neg_ok, 1)
                    with act.Fori(0, 2) as hf:
                        act.wait_ge(o_mm, 4 * hf + 1)
                        with act.Fori(0, JD // 2) as jj:
                            for b in range(2):
                                j = 2 * jj + b
                                J = hf * JD + j
                                act.wait_ge(x_mm, J + 1)
                                act.wait_ge(cv, J + 1)
                                act.activation(xpad[:, b, :, 3:S + 3],
                                               bankX[b][:, :].rearrange("p (g s) -> p g s", s=S), ACT.Copy).then_inc(x_cp, 1)
                                act.wait_ge(z_mm, 2 + J + 1)
                                plain(act)
                                act.activation(yz[:, ds(j, 1), :].rearrange("p a t -> p (a t)"), bankZ[b][:, :],
                                               ACT.Silu).then_inc(z_si, 1)
                                act.wait_ge(cv, 2 + J + 1)
                                plain(act)
                                act.activation(xc[:, ds(j, 1), :].rearrange("p a t -> p (a t)"), acc[:, b, :],
                                               ACT.Silu).then_inc(xs, 1)
                        act.wait_ge(bc_mm, hf + 1)
                        for r in (slice(0, R), slice(R, R + 2 * N)):
                            act.activation(xdbl[r, :], bankD[0][r, :], ACT.Copy).then_inc(bc_cp, 1)
                        with act.Fori(0, JD // 2) as jj:
                            for b in range(2):
                                act.wait_ge(abs_ok, hf * JD + 2 * jj + b + 1)
                                act.activation(ring[:, HS + b, :], ring[:, DA + b, :], ACT.Exp).then_inc(u_ok, 1)
                            act.wait_ge(u_ok, hf * JD + 2 * jj + 2)
                            for b in range(2):
                                act.activation(ring[:, HC + b, :], ring[:, HS + b, :], ACT.Ln, bias=1.0).then_inc(l_ok, 1)
                        act.wait_ge(start_ok, 2 * hf + 2)
                        with act.Fori(0, JD // 2) as jj:
                            for b in range(2):
                                j = 2 * jj + b
                                J = hf * JD + j
                                act.wait_ge(aj, J + 1)
                                for n in range(N):
                                    act.wait_ge(sc, J * N + n + 1)
                                    plain(act)
                                    act.activation(
                                        ring[:, DA + n % 2, :].rearrange("p (g s) -> p g s", s=S)[:, :, 1:S],
                                        delta[:, ds(j, 1), :].rearrange("p a (g s) -> p (a g) s", s=S)[:, :, 1:S],
                                        ACT.Exp, scale=cj[:, b, n:n + 1]).then_inc(da_ok, 1)

                @block.vector
                def _(dve):
                    for s, v in ((cv, 2), (d_rd, 2), (sc, 2), (yo, 2), (o_ad, 2)):
                        dve.sem_inc(s, v)
                    c = Chain(dve, chain)
                    dve.memset(xpad[:, :, :, 0:3], 0.0).then_inc(pad_ok, 1)
                    dve.wait_ge(neg_ok, 1)
                    c.link(dve.tensor_scalar(chan[:, :, 0:N], chan[:, :, 0:N], -1.0, None, ALU.mult))
                    with dve.Fori(0, 2) as hf:
                        c.enter(hf, JD // 2 * (8 + 10 + 2 * (1 + N) + 2))
                        with dve.Fori(0, JD // 2) as jj:
                            c.enter(jj, 8)
                            for b in range(2):
                                j = 2 * jj + b
                                J = hf * JD + j
                                c.link(dve.tensor_copy(cj[:, b, :], chan[:, ds(j, 1), :].rearrange("p a n -> p (a n)")))
                                dve.wait_ge(x_cp, 2 + J + 1)
                                dve.wait_ge(xs, J + 1)
                                s3 = acc[:, b, :].rearrange("p (g s) -> p g s", s=S)
                                c.link(dve.tensor_scalar(s3, xpad[:, b, :, 0:S], cj[:, b, N + 3:N + 4],
                                                         cj[:, b, N + 2:N + 3], ALU.mult, ALU.add))
                                for k in range(1, 4):
                                    ins = dve.scalar_tensor_tensor(s3, xpad[:, b, :, k:k + S], cj[:, b, N + 3 + k:N + 4 + k],
                                                                   s3, ALU.mult, ALU.add)
                                    if k < 3:
                                        c.link(ins)
                                    else:
                                        ins.then_inc(cv, 1)
                            c.leave(JD // 2)
                        with dve.Fori(0, JD // 2) as jj:
                            c.enter(jj, 10)
                            for b in range(2):
                                j = 2 * jj + b
                                J = hf * JD + j
                                c.link(dve.tensor_copy(cj[:, b, :], chan[:, ds(j, 1), :].rearrange("p a n -> p (a n)")))
                                dve.wait_ge(d_mm, 2 + J + 1)
                                c.count(dve.tensor_scalar(ring[:, BX + b, :], bankD[b][:, :], cj[:, b, N + 1:N + 2],
                                                          0.0, ALU.add, ALU.max))
                                dve.tensor_scalar(ring[:, DA + b, :], bankD[b][:, :], cj[:, b, N + 1:N + 2], 0.0,
                                                  ALU.add, ALU.min).then_inc(d_rd, 1)
                                dve.wait_ge(d_rd, 2 + J + 1)
                                dve.tensor_tensor(ring[:, DA + b, :], ring[:, DA + b, :], ring[:, BX + b, :],
                                                  ALU.subtract).then_inc(abs_ok, 1)
                            for b in range(2):
                                j = 2 * jj + b
                                J = hf * JD + j
                                t, m, u, l = (ring[:, o + b, :] for o in (DA, BX, HS, HC))
                                dve.wait_ge(l_ok, J + 1)
                                c.link(dve.tensor_scalar(t, u, 1.0, -1.0, ALU.add, ALU.add))
                                c.link(dve.tensor_tensor(t, u, t, ALU.subtract))
                                c.link(dve.tensor_tensor(t, t, l, ALU.add))
                                dve.tensor_tensor(delta[:, ds(j, 1), :].rearrange("p a t -> p (a t)"), t, m,
                                                  ALU.add).then_inc(del_ok, 1)
                            c.leave(JD // 2)
                        dve.wait_ge(del_ok, JD * (hf + 1))
                        for b in range(2):
                            dve.memset(ring[:, DA + b, :].rearrange("p (g s) -> p g s", s=S)[:, :, 0:1], 0.0
                                       ).then_inc(start_ok, 1)

                        def gate(j, J, b):
                            dve.wait_ge(y_mm, 2 + N * (J + 1))
                            flat = xc[:, ds(j, 1), :].rearrange("p a t -> p (a t)")
                            c.link(dve.scalar_tensor_tensor(acc[:, b, :], flat, cj[:, b, N:N + 1], bankY[b][:, :],
                                                            ALU.mult, ALU.add))
                            g = yz[:, ds(j, 1), :].rearrange("p a t -> p (a t)")
                            dve.tensor_tensor(g, acc[:, b, :], g, ALU.mult).then_inc(yo, 1)

                        with dve.Fori(0, JD // 2) as jj:
                            c.enter(jj, 2 * (1 + N) + 2)
                            for b in range(2):
                                j = 2 * jj + b
                                J = hf * JD + j
                                dve.tensor_copy(cj[:, b, :], chan[:, ds(j, 1), :].rearrange("p a n -> p (a n)")).then_inc(aj, 1)
                                c.link(dve.tensor_tensor(dx[:, b, :], delta[:, ds(j, 1), :].rearrange("p a t -> p (a t)"),
                                                         xc[:, ds(j, 1), :].rearrange("p a t -> p (a t)"), ALU.mult))
                                for q in range(N // 4):
                                    dve.wait_ge(bc_in[q], 16 * hf + 16)

                                def drive(n):
                                    return c.count(dve.tensor_tensor(ring[:, BX + n % 3, :], dx[:, b, :],
                                                                     BC[:, 0, n, :], ALU.mult))
                                ahead = drive(0)
                                for n in range(N):
                                    need = ahead
                                    if n + 1 < N:
                                        if n >= 2:
                                            dve.wait_ge(sc, 2 + J * N + n - 1)
                                        ahead = drive(n + 1)
                                    if b == 1 and n == 3:
                                        gate(2 * jj, hf * JD + 2 * jj, 0)
                                    dve.wait_ge(chain, need)
                                    dve.wait_ge(da_ok, J * N + n + 1)
                                    dve.wait_ge(hc_ok, J * N + n + 1)
                                    dve.tensor_tensor_scan(ring[:, HS + n % 2, :], ring[:, DA + n % 2, :],
                                                           ring[:, BX + n % 3, :], 0.0, ALU.mult, ALU.add).then_inc(sc, 1)
                            gate(2 * jj + 1, hf * JD + 2 * jj + 1, 1)
                            c.leave(JD // 2)
                        for t in range(HT // P):
                            dve.wait_ge(o_mm, 1 + 4 * hf + t + 1)
                            xr = xres[:, ds(hf * (HT // P) + t, 1), :].rearrange("p a d -> p (a d)")
                            dve.tensor_tensor(xr, xr, bankX[t % 2][:, :], ALU.add).then_inc(o_ad, 1)
                        c.leave(2)
        if debug == "mamba":
            return store_x()
        pos = sb0("slot_of_choice", [P, 2, NT], I32)
        prob2 = sb0("choice_prob", [P, 2, NT])
        eid = sb0("expert_of_slot_tile", [P, NS], I32)
        with ExitStack() as st:
            sb, ps, sem = pool(st)
            xrow = sb("xn_rows", [P, NT, D])
            norm_phase("n3_", keep=xrow)
            rw = sb("router_wT", [P, KD, E])
            rb = sb("router_b", [P, E])
            ones, before = sb("ones", [P, P]), sb("rows_before", [P, P])
            iE, iJ, iS = sb("iota_e_minus_E", [P, E]), sb("iota_tile_rows", [P, NT]), sb("iota_slot_tile", [P, NS])
            names = ("logits", "masked", "eq", "cand", "one1", "one2", "sel", "where_", "q1", "q2")
            lg, lg2, eq, cand, one1, one2, sel, where, q1, q2 = (sb("r_" + n, [P, NT, E]) for n in names)
            csel = sb("sel_of_tiles_before", [P, NT + 1, E])
            m1, m2, i1, i2, dif, e2, den, p1f, p2f = (sb("r_m%d" % n, [P, NT]) for n in range(9))
            cnt, ntile = sb("expert_count", [P, E]), sb("expert_tiles", [P, E])
            ends = sb("expert_tile_starts", [P, E + 1])
            rows0 = sb("expert_first_row", [P, E])
            more = sb("tile_needed", [P, E, NT])
            past = sb("expert_is_past", [P, NS, E])
            pastn = sb("experts_past", [P, NS])
            bankL, bankR, bankC = (ps("bank" + n, [P, 512]) for n in "LRC")
            r_in, io_ok, bf_ok = sem("router_in"), sem("iota_ready"), sem("rows_before_ready")
            one_ok = sem("ones_ready")
            l_mm, sel_ok, r_mm = sem("logits_done"), sem("choices_ready"), sem("ranks_done")
            dif_ok, e2_ok = sem("logit_gap_ready"), sem("gap_exp_ready")
            pos_ok, sc_done, chain = sem("slots_ready"), sem("rows_scattered"), sem("r_dve_chain")

            def tE(v):
                return v.unsqueeze(2).to_broadcast([P, NT, E])

            def eT(v):
                return v.unsqueeze(1).to_broadcast([P, NT, E])

            with nc.Block() as block:
                @block.sync
                def _(sp):
                    with nc.allow_non_contiguous_dma("router weights by model dimension"):
                        for k in range(KD):
                            sp.dma_start(rw[:, k, :], a["L0_ffn_router_w"][:, k * P:(k + 1) * P].rearrange("e p -> p e"),
                                         allow_slow_non_contiguous=True).then_inc(r_in, 16)
                    sp.dma_start(rb[:, :], a["L0_ffn_router_b"].partition_broadcast(P)).then_inc(r_in, 16)
                    sp.wait_ge(r_in, 16 * (KD + 1))

                @block.gpsimd
                def _(pl):
                    for v, base, step in ((iE, -E, 1), (iJ, 0, P), (iS, 0, 1)):
                        pl.iota(v[:, :], pattern=[[step, v.shape[1]]], base=base, channel_multiplier=0,
                                allow_small_or_imprecise_dtypes=True).then_inc(io_ok, 1)
                    pl.memset(ones[:, :], 1.0).then_inc(one_ok, 1)
                    pl.wait_ge(one_ok, 1)
                    pl.affine_select(out=before[:, :], in_=ones[:, :], compare_op=ALU.is_gt, fill=0.0,
                                     base=0, pattern=[[1, P]], channel_multiplier=-1).then_inc(bf_ok, 1)
                    pl.wait_ge(xs_zero, 16)
                    pl.wait_ge(pos_ok, 2)
                    for k in range(2):
                        for t in range(NT):
                            pl.indirect_dma_start(xs_d, bass.IndirectOffsetOnAxis(ap=pos[:, k, t:t + 1], axis=0),
                                                  xrow[:, t, :], None).then_inc(sc_done, 16)
                    pl.wait_ge(sc_done, 16 * 2 * NT)

                @block.tensor
                def _(pe):
                    pe.wait_ge(r_in, 16 * (KD + 1))
                    for t in range(NT):
                        for k in range(KD):
                            mm = pe.matmul(bankL[:, t * E:(t + 1) * E], xnT[:, k, t * P:(t + 1) * P], rw[:, k, :],
                                           start=(k == 0), stop=(k == KD - 1))
                    mm.then_inc(l_mm, 1)
                    pe.wait_ge(bf_ok, 1)
                    pe.wait_ge(sel_ok, 1)
                    pe.matmul(bankR[:, 0:NT * E], before[:, :], sel[:, :, :].rearrange("p t e -> p (t e)"),
                              start=True, stop=False)
                    pe.matmul(bankR[:, 0:NT * E], ones[:, :], csel[:, 0:NT, :].rearrange("p t e -> p (t e)"),
                              start=False, stop=True).then_inc(r_mm, 1)
                    pe.matmul(bankC[:, 0:E], ones[:, :], csel[:, NT, :], start=True, stop=True).then_inc(r_mm, 1)

                @block.scalar
                def _(act):
                    act.wait_ge(dif_ok, 1)
                    act.activation(e2[:, :], dif[:, :], ACT.Exp).then_inc(e2_ok, 1)

                @block.vector
                def _(dve):
                    c = Chain(dve, chain)

                    def tt(o, x, y, op):
                        c.link(dve.tensor_tensor(o, x, y, op))

                    def first_max(src, m, i, one):
                        c.link(dve.tensor_reduce(m[:, :], src[:, :, :], AX.X, ALU.max))
                        tt(eq[:, :, :], src[:, :, :], tE(m[:, :]), ALU.is_equal)
                        tt(cand[:, :, :], eq[:, :, :], eT(iE[:, :]), ALU.mult)
                        c.link(dve.tensor_reduce(i[:, :], cand[:, :, :], AX.X, ALU.min))
                        tt(one[:, :, :], eT(iE[:, :]), tE(i[:, :]), ALU.is_equal)

                    dve.wait_ge(l_mm, 1)
                    dve.wait_ge(io_ok, 3)
                    tt(lg[:, :, :], bankL[:, 0:NT * E].rearrange("p (t e) -> p t e", e=E), eT(rb[:, :]), ALU.add)
                    first_max(lg, m1, i1, one1)
                    c.link(dve.scalar_tensor_tensor(lg2[:, :, :], one1[:, :, :], -3e38, lg[:, :, :], ALU.mult, ALU.add))
                    first_max(lg2, m2, i2, one2)
                    dve.tensor_tensor(dif[:, :], m2[:, :], m1[:, :], ALU.subtract).then_inc(dif_ok, 1)
                    tt(sel[:, :, :], one1[:, :, :], one2[:, :, :], ALU.add)
                    c.link(dve.memset(csel[:, 0, :], 0.0))
                    for t in range(NT):
                        ins = dve.tensor_tensor(csel[:, t + 1, :], csel[:, t, :], sel[:, t, :], ALU.add)
                        if t + 1 < NT:
                            c.link(ins)
                    ins.then_inc(sel_ok, 1)
                    dve.wait_ge(e2_ok, 1)
                    c.link(dve.tensor_scalar(den[:, :], e2[:, :], 1.0, None, ALU.add))
                    c.link(dve.reciprocal(prob2[:, 0, :], den[:, :]))
                    tt(prob2[:, 1, :], prob2[:, 0, :], e2[:, :], ALU.mult)
                    dve.wait_ge(r_mm, 2)
                    c.link(dve.tensor_copy(cnt[:, :], bankC[:, 0:E]))
                    tt(more[:, :, :], cnt[:, :].unsqueeze(2).to_broadcast([P, E, NT]),
                       iJ[:, :].unsqueeze(1).to_broadcast([P, E, NT]), ALU.is_gt)
                    c.link(dve.tensor_reduce(ntile[:, :], more[:, :, :], AX.X, ALU.add))
                    c.link(dve.memset(ends[:, 0:1], 0.0))
                    for e in range(E):
                        tt(ends[:, e + 1:e + 2], ends[:, e:e + 1], ntile[:, e:e + 1], ALU.add)
                    c.link(dve.tensor_scalar(rows0[:, :], ends[:, 0:E], float(P), None, ALU.mult))
                    tt(where[:, :, :], bankR[:, 0:NT * E].rearrange("p (t e) -> p t e", e=E), eT(rows0[:, :]), ALU.add)
                    for k, (one, q, f) in enumerate(((one1, q1, p1f), (one2, q2, p2f))):
                        tt(q[:, :, :], one[:, :, :], where[:, :, :], ALU.mult)
                        c.link(dve.tensor_reduce(f[:, :], q[:, :, :], AX.X, ALU.add))
                        dve.tensor_copy(pos[:, k, :], f[:, :]).then_inc(pos_ok, 1)
                    tt(past[:, :, :], ends[:, 1:E + 1].unsqueeze(1).to_broadcast([P, NS, E]),
                       iS[:, :].unsqueeze(2).to_broadcast([P, NS, E]), ALU.is_le)
                    c.link(dve.tensor_reduce(pastn[:, :], past[:, :, :], AX.X, ALU.add))
                    c.link(dve.tensor_scalar(pastn[:, :], pastn[:, :], float(E - 1), None, ALU.min))
                    c.link(dve.tensor_copy(eid[:, :], pastn[:, :]))

        with ExitStack() as st:
            sb, ps, sem = pool(st)
            W, Vw = sb("We", [P, 2, KD, FH]), sb("Ve", [P, 2, KD, FH])
            Wo = sb("Woe", [P, 2, JF, D])
            xs = sb("slot_rows", [P, 2, D])
            xT = sb("slot_rowsT", [P, 2, KD, P])
            gate_ = sb("silu_b", [P, 2, 512])
            y = sb("hidden", [P, JF, P])
            yT = sb("hiddenT", [P, 2, JF, P])
            osb = sb("slot_out", [P, 2, D])
            bankA = [ps(f"bankA{i}", [P, 512]) for i in range(2)]
            bankB = [ps(f"bankB{i}", [P, 512]) for i in range(2)]
            bankT = [ps(f"bankYT{i}", [P, KD, P]) for i in range(2)]
            bankX, bankO = ps("bankXT", [P, KD, P]), ps("bankOut", [P, D])
            v_in, w_in, o_in, x_in2 = ([sem(f"{n}_in{i}") for i in range(2)] for n in ("ve", "we", "woe", "slot"))
            b_mm, a_mm = sem("b_done"), sem("a_done")
            o_mm = sem("slot_out_done")
            x_tr, x_cp = sem("slot_rows_turned"), sem("slot_rowsT_copied")
            g_ok = sem("silu_ready")
            y_ok = sem("hidden_ready")
            y_tr, y_cp = sem("hidden_turned"), [sem(f"hiddenT_copied{i}") for i in range(2)]
            o_cp = sem("slot_out_copied")
            o_st = [sem(f"slot_out_stored{i}") for i in range(2)]
            last = NS - 1

            def tiles(eng, first, step):
                pairs = (last - 1 - first) // 2
                with eng.Fori(0, pairs) as i:
                    for h in range(2):
                        step(2 * i + first + h, (first + h) % 2)
                for s in range(first + 2 * pairs, last + 1):
                    step(s, s % 2)

            def use(s, b):
                return (s - b) * 8 + 16

            with nc.Block() as block:
                @block.sync
                def _(sp):
                    def step(s, b):
                        e = sp.value_load(eid[0:1, ds(s, 1)] if not isinstance(s, int) else eid[0:1, s:s + 1],
                                          min_val=0, max_val=E - 1)
                        sp.wait_ge(x_tr, s + 1)
                        sp.dma_start(xs[:, b, :], xs_d[ds(s * P, P), :]).then_inc(x_in2[b], 16)
                        for buf, name, free, got in ((Vw, "V", b_mm, v_in), (W, "W", a_mm, w_in), (Wo, "W_out", o_mm, o_in)):
                            sp.wait_ge(free, s + 1)
                            sp.dma_start(buf[:, b, :, :], a["L0_ffn_" + name][ds(e, 1)].rearrange(
                                "e (k p) f -> p (e k) f", p=P)).then_inc(got[b], 16)
                    tiles(sp, 0, step)

                @block.gpsimd
                def _(pl):
                    def step(s, b):
                        pl.wait_ge(o_cp, 1 + s + 1)
                        plain(pl)
                        pl.dma_start(ys_d[ds(s * P, P), :], osb[:, b, :]).then_inc(o_st[b], 16)
                    tiles(pl, 0, step)
                    pl.wait_ge(o_st[0], 16 * ((NS + 1) // 2))
                    pl.wait_ge(o_st[1], 16 * (NS // 2))

                @block.tensor
                def _(pe):
                    for s, v in ((b_mm, 2), (a_mm, 2), (o_mm, 2), (x_tr, 2)):
                        pe.sem_inc(s, v)

                    def turn_x(s, b):
                        pe.wait_ge(x_in2[b], use(s, b))
                        pe.wait_ge(x_cp, s + 1)
                        for k in range(KD):
                            mm = pe.transpose(bankX[:, k, :], xs[:, b, k * P:(k + 1) * P], ident[:, :])
                        mm.then_inc(x_tr, 1)

                    def up(s, b, w, got, bank, free, done):
                        pe.wait_ge(got[b], use(s, b))
                        pe.wait_ge(free, 2 * s + 2)
                        for k in range(KD):
                            for h in range(2):
                                mm = pe.matmul(bank[h][:, :], xT[:, b, k, :], w[:, b, k, 512 * h:512 * h + 512],
                                               start=(k == 0), stop=(k == KD - 1))
                        mm.then_inc(done, 1)

                    def turn_y(s, b):
                        for h in range(2):
                            pe.wait_ge(y_ok, 2 + 2 * s + h + 1)
                            pe.wait_ge(y_cp[h], s + 1)
                            for k in range(KD):
                                mm = pe.transpose(bankT[h][:, k, :], y[:, KD * h + k, :], ident[:, :])
                            mm.then_inc(y_tr, 1)

                    def down(s, b):
                        pe.wait_ge(o_in[b], use(s, b))
                        pe.wait_ge(o_cp, s + 1)
                        for h in range(2):
                            pe.wait_ge(y_cp[h], 1 + s + 1)
                            for k in range(KD):
                                j = KD * h + k
                                mm = pe.matmul(bankO[:, :], yT[:, b, j, :], Wo[:, b, j, :],
                                               start=(j == 0), stop=(j == JF - 1))
                        mm.then_inc(o_mm, 1)

                    def step(s, b, first=False):
                        pe.wait_ge(x_cp, 1 + s + 1)
                        up(s, b, Vw, v_in, bankB, g_ok, b_mm)
                        up(s, b, W, w_in, bankA, y_ok, a_mm)
                        if not first:
                            down(s - 1, 1 - b)
                        turn_y(s, b)
                        if not (isinstance(s, int) and s == last):
                            turn_x(s + 1, 1 - b)
                    turn_x(0, 0)
                    step(0, 0, first=True)
                    tiles(pe, 1, step)
                    down(last, last % 2)

                @block.scalar
                def _(act):
                    act.sem_inc(x_cp, 1)
                    act.sem_inc(g_ok, 2)
                    act.sem_inc(y_cp[0], 1)

                    def copy_x(s, b):
                        act.wait_ge(x_tr, 2 + s + 1)
                        act.activation(xT[:, b, :, :], bankX[:, :, :], ACT.Copy).then_inc(x_cp, 1)

                    def step(s, b):
                        act.wait_ge(b_mm, 2 + s + 1)
                        act.wait_ge(y_ok, 2 * s + 2)
                        for h in range(2):
                            act.activation(gate_[:, h, :], bankB[h][:, :], ACT.Silu).then_inc(g_ok, 1)
                        act.wait_ge(y_tr, 2 * s + 1)
                        act.activation(yT[:, b, 0:KD, :], bankT[0][:, :, :], ACT.Copy).then_inc(y_cp[0], 1)
                        if not (isinstance(s, int) and s == last):
                            copy_x(s + 1, 1 - b)
                    copy_x(0, 0)
                    tiles(act, 0, step)

                @block.vector
                def _(dve):
                    dve.sem_inc(y_ok, 2)
                    dve.sem_inc(y_cp[1], 1)
                    dve.sem_inc(o_cp, 1)

                    def copy_out(s, b, stored=True):
                        dve.wait_ge(o_mm, 2 + s + 1)
                        if stored:
                            dve.wait_ge(o_st[b], (s - b) * 8)
                        dve.tensor_copy(osb[:, b, :], bankO[:, :]).then_inc(o_cp, 1)

                    def step(s, b, first=False):
                        dve.wait_ge(a_mm, 2 + s + 1)
                        if not first:
                            dve.wait_ge(y_tr, 2 * s)
                        for h in range(2):
                            dve.wait_ge(g_ok, 2 + 2 * s + h + 1)
                            dve.tensor_tensor(y[:, KD * h:KD * h + KD, :].rearrange("p k q -> p (k q)"),
                                              bankA[h][:, :], gate_[:, h, :], ALU.mult).then_inc(y_ok, 1)
                        if not first:
                            copy_out(s - 1, 1 - b, stored=not (isinstance(s, int) and s < 3))
                        dve.wait_ge(y_tr, 2 * s + 2)
                        dve.tensor_copy(yT[:, b, KD:JF, :], bankT[1][:, :, :]).then_inc(y_cp[1], 1)
                    for s in range(3):
                        step(s, s % 2, first=(s == 0))
                    tiles(dve, 3, step)
                    copy_out(last, last % 2)

        with ExitStack() as st:
            sb, ps, sem = pool(st)
            got = sb("expert_rows", [P, 2, NT, D])
            g_in = [sem(f"expert_rows_in{i}") for i in range(NT)]
            chain, done = sem("c_dve_chain"), sem("out_stored")
            f_ok = sem("x_final")
            with nc.Block() as block:
                @block.gpsimd
                def _(pl):
                    for t in range(NT):
                        for k in range(2):
                            pl.indirect_dma_start(got[:, k, t, :], None, ys_d,
                                                  bass.IndirectOffsetOnAxis(ap=pos[:, k, t:t + 1], axis=0)
                                                  ).then_inc(g_in[t], 16)

                @block.vector
                def _(dve):
                    c = Chain(dve, chain)
                    for t in range(NT):
                        dve.wait_ge(g_in[t], 32)
                        for k in range(2):
                            ins = dve.scalar_tensor_tensor(xres[:, t, :], got[:, k, t, :], prob2[:, k, t:t + 1],
                                                           xres[:, t, :], ALU.mult, ALU.add)
                            if k == 0:
                                c.link(ins)
                        ins.then_inc(f_ok, 1)

                @block.sync
                def _(sp):
                    for t in range(NT):
                        sp.wait_ge(f_ok, t + 1)
                        sp.dma_start(out_d[t * P:(t + 1) * P, :], xres[:, t, :]).then_inc(done, 16)
                    sp.wait_ge(done, 16 * NT)


DEBUG = None


def kernel(**inputs):
    import numpy as _np
    import concourse.bacc as _bacc
    from concourse import mybir as _mybir
    from concourse.bass_utils import run_bass_kernel_spmd as _run

    nc = _bacc.Bacc("TRN2", target_bir_lowering=False, num_devices=1)
    arrays, args = {}, {}
    for name, v in inputs.items():
        v = _np.ascontiguousarray(v)
        arrays[f"in_{name}"] = v
        args[name] = nc.dram_tensor(f"in_{name}", v.shape, _mybir.dt.from_np(v.dtype), kind="ExternalInput").ap()
    shape = arrays["in_x"].shape
    out = nc.dram_tensor("out_0", shape, F32, kind="ExternalOutput").ap()
    build(nc, args, out, DEBUG)
    r = _run(nc, [arrays], core_ids=[0])
    return r.results[0]["out_0"]
```

```python
from contextlib import ExitStack

import concourse.bass as bass
from concourse import mybir

F32 = mybir.dt.float32
F32R = mybir.dt.float32r
I32 = mybir.dt.int32
U32 = mybir.dt.uint32
ALU = mybir.AluOpType
ACT = mybir.ActivationFunctionType
AX = mybir.AxisListType

P = 128
EPS = 1e-5
ds = bass.ds


class Chain:

    def __init__(self, eng, sem):
        self.eng, self.sem, self.base, self.k, self.outer = eng, sem, 0, 0, []

    def count(self, ins):
        ins.then_inc(self.sem, 1)
        self.k += 1
        return self.base + self.k

    def link(self, ins):
        self.eng.wait_ge(self.sem, self.count(ins))

    def enter(self, i, per):
        self.outer.append((self.base, self.k, per))
        self.base, self.k = self.base + self.k + i * per, 0

    def leave(self, times):
        base, k, per = self.outer.pop()
        assert self.k == per, (self.k, per)
        self.base, self.k = base, k + per * times


def build(nc, a, out, debug=None):
    x_d = a["x"].rearrange("b s d -> (b s) d")
    ctx_d = a["ctx_1024"]
    out_d = out.rearrange("b s d -> (b s) d")
    B, S, D = a["x"].shape
    CK = ctx_d.shape[1]
    KD = D // P
    KC = CK // P
    TOK = B * S
    NT = TOK // P
    H, DH = 16, 32
    NP = H // 2
    SCALE = float(DH) ** -0.5
    DI = a["L0_attn_D"].shape[0]
    JD = DI // P
    N = a["L0_attn_A_log"].shape[1]
    R = a["L0_attn_W_dt"].shape[0]
    HT = TOK // 2
    HB = B // 2
    E = a["L0_ffn_router_w"].shape[0]
    FH = a["L0_ffn_W"].shape[2]
    JF = FH // P
    NS = 2 * TOK // P + E - 1

    whole = ExitStack()

    def pool(stack):
        def sb(name, shape, dt=F32):
            return stack.enter_context(nc.sbuf_tensor(name, shape, dt))

        def ps(name, shape):
            return stack.enter_context(nc.psum_tensor(name, shape, F32))

        def sem(name):
            return stack.enter_context(nc.semaphore(name))
        return sb, ps, sem

    with whole:
        sb0, _, sem0 = pool(whole)
        xres = sb0("xres", [P, NT, D])
        xnT = sb0("xnT", [P, KD, TOK])
        ident = sb0("ident", [P, P])
        xs_d = nc.dram_tensor("slot_rows_scratch", (NS * P, D), F32).ap()
        ys_d = nc.dram_tensor("slot_out_scratch", (NS * P, D), F32).ap()
        z_ok, xs_zero = sem0("zeros_ready"), sem0("slot_rows_zeroed")
        x_in, ident0, ident_ok = sem0("x_in"), sem0("ident_zeroed"), sem0("ident_ready")

        carried = sem0("waits_carried")

        def plain(eng):
            eng.sem_inc(carried, 1)

        with nc.sbuf_tensor("zeros", [P, D], F32) as zeros, nc.Block() as block:
            @block.sync
            def _(sp):
                sp.dma_start(xres[:, :, :], x_d.rearrange("(t p) d -> p t d", p=P)).then_inc(x_in, 16)
                sp.wait_ge(z_ok, 1)
                sp.dma_start(xs_d.rearrange("(s p) d -> p s d", p=P),
                             zeros[:, :].unsqueeze(1).to_broadcast([P, NS, D])).then_inc(xs_zero, 16)
                sp.wait_ge(x_in, 16)
                sp.wait_ge(xs_zero, 16)

            @block.gpsimd
            def _(pl):
                pl.memset(zeros[:, :], 0.0).then_inc(z_ok, 1)
                pl.memset(ident[:, :], 0.0).then_inc(ident0, 1)
                pl.wait_ge(ident0, 1)
                pl.affine_select(out=ident[:, :], in_=ident[:, :], compare_op=ALU.not_equal, fill=1.0,
                                 base=0, pattern=[[-1, P]], channel_multiplier=1).then_inc(ident_ok, 1)
                pl.wait_ge(ident_ok, 1)

        def norm_phase(tag, keep=None):
            with ExitStack() as st:
                sb, ps, sem = pool(st)
                stats = sb(tag + "stats", [P, NT, nc.vector.BN_STATS_DIM])
                mv = sb(tag + "mv", [P, NT, nc.vector.BN_AGGR_DIM])
                veps, std, rstd = (sb(tag + n, [P, NT]) for n in ("var_eps", "std", "rstd"))
                var_ready, std_ready = sem(tag + "var_ready"), sem(tag + "std_ready")
                xn = sb(tag + "xn", [P, 2, D])
                bank = [ps(tag + f"bank{i}", [P, KD, P]) for i in range(2)]
                chain = sem(tag + "dve_chain")
                xn_ready = sem(tag + "xn_ready")
                turned = sem(tag + "xn_turned")
                copied = sem(tag + "xnT_copied")
                kept = sem(tag + "xn_kept")
                with nc.Block() as block:
                    @block.vector
                    def _(dve):
                        for t in range(NT):
                            dve.bn_stats(stats[:, t, :], xres[:, t, :]).then_inc(chain, 1)
                        dve.wait_ge(chain, NT)
                        for t in range(NT):
                            dve.bn_aggr(mv[:, t, :], stats[:, t, :]).then_inc(chain, 1)
                        dve.wait_ge(chain, 2 * NT)
                        dve.tensor_scalar(veps[:, :], mv[:, :, 1:2].rearrange("p t o -> p (t o)"), EPS, None,
                                          ALU.add).then_inc(var_ready, 1)
                        dve.wait_ge(std_ready, 1)
                        dve.reciprocal(rstd[:, :], std[:, :]).then_inc(chain, 1)
                        dve.wait_ge(chain, 2 * NT + 1)
                        for t in range(NT):
                            dve.wait_ge(turned, t + 1)
                            if keep is not None:
                                dve.wait_ge(kept, t + 1)
                            dve.tensor_scalar(xn[:, t % 2, :], xres[:, t, :], mv[:, t, 0:1], rstd[:, t:t + 1],
                                              ALU.subtract, ALU.mult).then_inc(xn_ready, 1)

                    @block.tensor
                    def _(pe):
                        pe.sem_inc(turned, 2)
                        with pe.Fori(0, NT // 2) as i:
                            for b in range(2):
                                t = 2 * i + b
                                pe.wait_ge(xn_ready, t + 1)
                                pe.wait_ge(copied, t + 1)
                                for k in range(KD):
                                    mm = pe.transpose(bank[b][:, k, :], xn[:, b, k * P:(k + 1) * P], ident[:, :])
                                mm.then_inc(turned, 1)

                    @block.scalar
                    def _(act):
                        act.sem_inc(copied, 2)
                        act.wait_ge(var_ready, 1)
                        act.activation(std[:, :], veps[:, :], ACT.Sqrt).then_inc(std_ready, 1)
                        with act.Fori(0, NT // 2) as i:
                            for b in range(2):
                                t = 2 * i + b
                                act.wait_ge(turned, 2 + t + 1)
                                act.activation(xnT[:, :, ds(t * P, P)], bank[b][:, :, :], ACT.Copy).then_inc(copied, 1)

                    if keep is not None:
                        @block.gpsimd
                        def _(pl):
                            pl.sem_inc(kept, 2)
                            with pl.Fori(0, NT // 2) as i:
                                for b in range(2):
                                    t = 2 * i + b
                                    pl.wait_ge(xn_ready, t + 1)
                                    pl.tensor_copy(keep[:, t, :], xn[:, b, :]).then_inc(kept, 1)

        norm_phase("n1_")

        with ExitStack() as st:
            sb, ps, sem = pool(st)
            Wk, Wv = (sb(n, [P, 2, KD, D], F32R) for n in ("Wk_HL", "Wv_HL"))
            Wo = sb("Wo", [P, KD, D])
            ctxs = sb("ctx_rows", [P, 2, KC, D])
            Wq = sb("Wq", [P, KD, D])
            ctxT = sb("ctxT_HL", [P, 2, 2, KD, CK], F32R)
            KT = sb("KT", [P, 2, KD, CK])
            V = sb("V", [P, 2, KC, D])
            QT = sb("QT", [P, KD, TOK])
            qbd = [sb(f"q_blocks{i}", [P, KD, P]) for i in range(2)]
            head_of = sb("head_parity", [P, 2])
            prob = sb("prob", [P, 2, CK])
            probT = sb("probT", [P, 2, KC, P])
            nmax = sb("neg_max", [P, 2, NP])
            rsum = sb("row_sum", [P, 2, NP])
            rinv = sb("row_inv", [P, 2, NP])
            cn = sb("context", [P, D])
            cnT = sb("contextT", [P, KD, P])
            bias = {n: sb(n, [P, KD]) for n in ("bq", "bk", "bv")}
            bqs = sb("bq_scaled", [P, KD])
            bo = sb("bo_rows", [P, D])
            bankT = ps("bankT", [P, KC, P])
            bankJ = [ps(f"bankJ{i}", [P, CK]) for i in range(2)]
            bankS = [ps(f"bankS{i}", [P, CK]) for i in range(2)]
            bankP = ps("bankP", [P, KC, P])
            bankO = ps("bankO", [P, NP, 2 * DH])
            bankX = ps("bankX", [P, D])

            w_ok, c_hi = sem("wkv_split"), sem("ctxT_H_ready")
            wq_in, w_in, o_in, b_in = sem("wq_in"), sem("wkv_in"), sem("wo_in"), sem("b_in")
            ctx_in = [sem(f"ctx_in{i}") for i in range(2)]
            chain = sem("a_dve_chain")
            bqs_ok = sem("bqs_ready")
            q_mm, q_ok = sem("q_projected"), sem("qT_ready")
            mask_ok, qb = sem("head_mask_ready"), sem("q_blocks_ready")
            t_mm, t_cp = sem("ctx_turned"), sem("ctxT_copied")
            j_mm, j_cp = sem("kv_projected"), sem("kv_copied")
            s_mm, s_max = sem("scores_ready"), sem("max_ready")
            s_exp = sem("probs_ready")
            p_mm, p_cp = sem("probs_turned"), sem("probT_copied")
            o_mm = sem("pv_done")
            c_cp = sem("context_copied")
            ct_mm, ct_cp = sem("context_turned"), sem("contextT_copied")
            y_mm, y_add = sem("wo_done"), sem("x_added")
            xbo = sem("bo_added")

            with nc.Block() as block:
                @block.sync
                def _(sp):
                    sp.dma_start(Wq[:, :, :], a["L0_xattn_Wq"].rearrange("(k p) n -> p k n", p=P)).then_inc(wq_in, 16)
                    for g in range(2):
                        sp.dma_start(ctxs[:, g, :, :], ctx_d[g].rearrange("(k p) d -> p k d", p=P)).then_inc(ctx_in[g], 16)
                    for n, w in (("L0_xattn_Wk", KT), ("L0_xattn_Wv", V)):
                        sp.dma_start(w[:, 1, :, :], a[n].rearrange("(k p) n -> p k n", p=P)).then_inc(w_in, 16)
                    sp.dma_start(Wo[:, :, :], a["L0_xattn_Wo"].rearrange("(k p) n -> p k n", p=P)).then_inc(o_in, 16)
                    with sp.Fori(0, NT - 1) as t:
                        for b in range(2):
                            sp.wait_ge(t_mm, KD * (2 * t + b + 1))
                            sp.dma_start(ctxs[:, b, :, :], ctx_d[ds(2 * t + b + 2, 1)].rearrange(
                                "g (k p) d -> p (g k) d", p=P)).then_inc(ctx_in[b], 16)

                @block.gpsimd
                def _(pl):
                    for n in ("bq", "bk", "bv"):
                        with nc.allow_non_contiguous_dma("bias by channel"):
                            pl.dma_start(bias[n][:, :], a["L0_xattn_" + n].rearrange("(k p) -> p k", p=P)).then_inc(b_in, 16)
                    pl.dma_start(bo[:, :], a["L0_xattn_bo"].partition_broadcast(P)).then_inc(b_in, 16)

                    def place(g, b):
                        for e in range(2):
                            pl.tensor_tensor(qbd[b][:, :, e * S:e * S + S], QT[:, :, ds(g * S, S)],
                                             head_of[:, e:e + 1].unsqueeze(2).to_broadcast([P, KD, S]),
                                             ALU.mult).then_inc(qb, 1)
                    pl.wait_ge(mask_ok, 6)
                    pl.wait_ge(q_ok, 2 + KD * 2)
                    for b in range(2):
                        place(b, b)
                    pl.wait_ge(b_in, 64)
                    for t in range(NT):
                        pl.tensor_tensor(xres[:, t, :], xres[:, t, :], bo[:, :], ALU.add).then_inc(xbo, 1)
                    with pl.Fori(0, NT - 1) as t:
                        for b in range(2):
                            pl.wait_ge(s_mm, NP * (2 * t + b + 1))
                            place(2 * t + b + 2, b)

                @block.tensor
                def _(pe):
                    pe.sem_inc(p_mm, 2)
                    pe.sem_inc(o_mm, 2)
                    pe.wait_ge(wq_in, 16)
                    for n in range(2 * KD):
                        m, h = n % KD, n // KD
                        pe.wait_ge(q_ok, n + 1)
                        for k in range(KD):
                            mm = pe.matmul(bankJ[n % 2][:, :], Wq[:, k, m * P:(m + 1) * P],
                                           xnT[:, k, h * CK:(h + 1) * CK], start=(k == 0), stop=(k == KD - 1))
                        mm.then_inc(q_mm, 1)

                    def turn(g, b, j):
                        if j == 0:
                            pe.wait_ge(ctx_in[b], 16 * (g // 2 + 1) if isinstance(g, int) else g * 8 + (16 - 8 * b))
                        pe.wait_ge(t_cp, KD * g + j + 1)
                        for k in range(KC):
                            mm = pe.transpose(bankT[:, k, :], ctxs[:, b, k, j * P:(j + 1) * P], ident[:, :])
                        mm.then_inc(t_mm, 1)

                    def project(g, b, u):
                        if u == 0:
                            pe.wait_ge(t_cp, 1 + KD * (g + 1))
                        pe.wait_ge(j_cp, NP * g + u + 1)
                        for k in range(KD):
                            for l, r in ((0, 0), (0, 1), (1, 0)):
                                if u < KD:
                                    lhs, rhs = Wk[:, l, k, u * P:(u + 1) * P], ctxT[:, b, r, k, :]
                                else:
                                    lhs, rhs = ctxT[:, b, l, k, (u - KD) * P:(u - KD + 1) * P], Wv[:, r, k, :]
                                mm = pe.matmul(bankJ[u % 2][:, :], lhs, rhs, start=(k == l == r == 0),
                                               stop=(k == KD - 1 and l == 1))
                        mm.then_inc(j_mm, 1)

                    def scores(g, b, u):
                        if u == 0:
                            pe.wait_ge(qb, 2 * (g + 1))
                        pe.wait_ge(j_cp, 2 + NP * g + u // 2 + 1)
                        pe.wait_ge(s_exp, NP * g + u + 1)
                        r = slice(64 * (u % 2), 64 * (u % 2) + 64)
                        pe.matmul(bankS[u % 2][:, :], qbd[b][r, u // 2, :], KT[r, b, u // 2, :],
                                  start=True, stop=True).then_inc(s_mm, 1)

                    def turn_probs(g, u):
                        n = NP * g + u
                        pe.wait_ge(s_exp, 2 + n + 1)
                        pe.wait_ge(p_cp, n + 1)
                        for k in range(KC):
                            mm = pe.transpose(bankP[:, k, :], prob[:, u % 2, k * P:(k + 1) * P], ident[:, :])
                        mm.then_inc(p_mm, 1)

                    def values(g, b, u):
                        if u == 0:
                            pe.wait_ge(c_cp, 2 * g + 2)
                            pe.wait_ge(j_cp, 2 + NP * (g + 1))
                        pe.wait_ge(p_cp, 1 + NP * g + u + 1)
                        for k in range(KC):
                            mm = pe.matmul(bankO[:, u, :], probT[:, u % 2, k, :], V[:, b, k, 64 * u:64 * u + 64],
                                           start=(k == 0), stop=(k == KC - 1))
                        mm.then_inc(o_mm, 1)

                    def batch(g, b, nxt, nxt2):
                        scores(g, b, 0)
                        for u in range(NP):
                            if nxt:
                                project(g + 1, 1 - b, u)
                            if u + 1 < NP:
                                scores(g, b, u + 1)
                            if nxt2 and u % 2 == 0:
                                turn(g + 2, b, u // 2)
                            turn_probs(g, u)
                            if u:
                                values(g, b, u - 1)
                        values(g, b, NP - 1)

                    def finish(t):
                        pe.wait_ge(c_cp, 2 + 4 * (t + 1))
                        pe.wait_ge(y_add, t + 1)
                        for k in range(KD):
                            mm = pe.transpose(bankX[:, k * P:(k + 1) * P], cn[:, k * P:(k + 1) * P], ident[:, :])
                        mm.then_inc(ct_mm, 1)
                        pe.wait_ge(ct_cp, KD * (t + 1))
                        for k in range(KD):
                            mm = pe.matmul(bankX[:, :], cnT[:, k, :], Wo[:, k, :], start=(k == 0), stop=(k == KD - 1))
                        mm.then_inc(y_mm, 1)

                    for j in range(KD):
                        turn(0, 0, j)
                    pe.wait_ge(w_ok, 4)
                    pe.wait_ge(q_ok, 2 + 2 * KD)
                    for u in range(NP):
                        project(0, 0, u)
                    for j in range(KD):
                        turn(1, 1, j)
                    pe.wait_ge(o_in, 16)
                    with pe.Fori(0, NT - 1) as t:
                        batch(2 * t, 0, True, True)
                        batch(2 * t + 1, 1, True, True)
                        finish(t)
                    batch(B - 2, 0, True, False)
                    batch(B - 1, 1, False, False)
                    finish(NT - 1)

                @block.scalar
                def _(act):
                    act.sem_inc(q_ok, 2)
                    act.sem_inc(j_cp, 2)
                    act.sem_inc(s_exp, 2)
                    act.wait_ge(b_in, 64)
                    act.activation(bqs[:, :], bias["bq"][:, :], ACT.Copy, scale=SCALE).then_inc(bqs_ok, 1)
                    act.wait_ge(bqs_ok, 1)
                    for n in range(2 * KD):
                        m, h = n % KD, n // KD
                        act.wait_ge(q_mm, n + 1)
                        act.activation(QT[:, m, h * CK:(h + 1) * CK], bankJ[n % 2][:, :], ACT.Identity,
                                       bias=bqs[:, m:m + 1], scale=SCALE).then_inc(q_ok, 1)

                    def copy_kv(g, b, u):
                        act.wait_ge(j_mm, NP * g + u + 1)
                        if u < KD:
                            act.activation(KT[:, b, u, :], bankJ[u % 2][:, :], ACT.Identity,
                                           bias=bias["bk"][:, u:u + 1]).then_inc(j_cp, 1)
                        else:
                            act.activation(V[:, b, u - KD, :], bankJ[u % 2][:, :], ACT.Copy).then_inc(j_cp, 1)

                    def batch(g, b, nxt):
                        for u in range(NP):
                            n = NP * g + u
                            act.wait_ge(s_max, n + 1)
                            act.wait_ge(p_mm, n + 1)
                            act.activation(prob[:, u % 2, :], bankS[u % 2][:, :], ACT.Exp,
                                           bias=nmax[:, b, u:u + 1],
                                           accum_out=rsum[:, b, u:u + 1]).then_inc(s_exp, 1)
                            if nxt:
                                if u == KD:
                                    act.wait_ge(o_mm, NP * g + 2)
                                copy_kv(g + 1, 1 - b, u)

                    def finish(t):
                        act.wait_ge(ct_mm, t + 1)
                        for k in range(KD):
                            act.activation(cnT[:, k, :], bankX[:, k * P:(k + 1) * P], ACT.Identity,
                                           bias=bias["bv"][:, k:k + 1]).then_inc(ct_cp, 1)

                    for u in range(NP):
                        copy_kv(0, 0, u)
                    with act.Fori(0, NT - 1) as t:
                        batch(2 * t, 0, True)
                        batch(2 * t + 1, 1, True)
                        finish(t)
                    batch(B - 2, 0, True)
                    batch(B - 1, 1, False)
                    finish(NT - 1)

                @block.vector
                def _(dve):
                    dve.sem_inc(t_cp, 1)
                    dve.sem_inc(p_cp, 1)
                    dve.sem_inc(c_cp, 2)
                    dve.sem_inc(y_add, 1)
                    c = Chain(dve, chain)
                    for e in range(2):
                        dve.memset(head_of[:, e:e + 1], 0.0).then_inc(mask_ok, 1)
                    dve.wait_ge(mask_ok, 2)
                    for hh in range(P // DH):
                        dve.memset(head_of[DH * hh:DH * hh + DH, hh % 2:hh % 2 + 1], 1.0).then_inc(mask_ok, 1)

                    def copy_ctx(g, b, j):
                        if j == 0 and not isinstance(g, int):
                            dve.wait_ge(j_mm, NP * (g - 1))
                        dve.wait_ge(t_mm, KD * g + j + 1)
                        rows = bankT[:, :, :].rearrange("p a b -> p (a b)")
                        dve.tensor_copy(ctxT[:, b, 0, j, :], rows).then_inc(c_hi, 1)
                        dve.wait_ge(c_hi, KD * g + j + 1)
                        dve.tensor_tensor(ctxT[:, b, 1, j, :], rows, ctxT[:, b, 0, j, :], ALU.subtract).then_inc(t_cp, 1)

                    def row_max(g, b, u):
                        dve.wait_ge(s_mm, NP * g + u + 1)
                        dve.tensor_reduce(nmax[:, b, u:u + 1], bankS[u % 2][:, :], AX.X, ALU.max,
                                          negate=True).then_inc(s_max, 1)

                    def copy_probs(g, u):
                        n = NP * g + u
                        dve.wait_ge(p_mm, 2 + n + 1)
                        dve.wait_ge(o_mm, n + 1)
                        dve.tensor_copy(probT[:, u % 2, :, :], bankP[:, :, :]).then_inc(p_cp, 1)

                    def batch(g, b, nxt2):
                        row_max(g, b, 0)
                        for u in range(NP):
                            if u + 1 < NP:
                                row_max(g, b, u + 1)
                            if nxt2 and u % 2 == 0:
                                copy_ctx(g + 2, b, u // 2)
                            copy_probs(g, u)
                        dve.wait_ge(s_exp, 2 + NP * (g + 1))
                        c.link(dve.reciprocal(rinv[:, b, :], rsum[:, b, :]))
                        dve.wait_ge(o_mm, 2 + NP * (g + 1))
                        for h in range(2):
                            r = slice(64 * h, 64 * h + 64)
                            dst = cn[64 * b:64 * b + 64, :].rearrange("p (u e d) -> p u e d", e=2, d=DH)[:, :, h, :]
                            dve.tensor_tensor(dst, bankO[r, :, DH * h:DH * h + DH],
                                              rinv[r, b, :].unsqueeze(2).to_broadcast([64, NP, DH]),
                                              ALU.mult).then_inc(c_cp, 1)

                    def finish(t):
                        dve.wait_ge(y_mm, t + 1)
                        dve.tensor_tensor(xres[:, ds(t, 1), :].rearrange("p a d -> p (a d)"),
                                          xres[:, ds(t, 1), :].rearrange("p a d -> p (a d)"),
                                          bankX[:, :], ALU.add).then_inc(y_add, 1)

                    for j in range(KD):
                        copy_ctx(0, 0, j)
                    dve.wait_ge(w_in, 32)
                    for i, (whole_w, split_w) in enumerate(((KT, Wk), (V, Wv))):
                        dve.tensor_copy(split_w[:, 0, :, :], whole_w[:, 1, :, :]).then_inc(w_ok, 1)
                        dve.wait_ge(w_ok, 2 * i + 1)
                        dve.tensor_tensor(split_w[:, 1, :, :], whole_w[:, 1, :, :], split_w[:, 0, :, :],
                                          ALU.subtract).then_inc(w_ok, 1)
                    for j in range(KD):
                        copy_ctx(1, 1, j)
                    dve.wait_ge(xbo, NT)
                    with dve.Fori(0, NT - 1) as t:
                        c.enter(t, 2)
                        batch(2 * t, 0, True)
                        batch(2 * t + 1, 1, True)
                        finish(t)
                        c.leave(NT - 1)
                    batch(B - 2, 0, False)
                    batch(B - 1, 1, False)
                    finish(NT - 1)

        def store_x():
            done = sem0("x_stored")
            with nc.Block() as block:
                @block.sync
                def _(sp):
                    sp.dma_start(out_d.rearrange("(t p) d -> p t d", p=P), xres[:, :, :]).then_inc(done, 16)
                    sp.wait_ge(done, 16)

        if debug == "attention":
            return store_x()
        norm_phase("n2_")
        with ExitStack() as st:
            sb, ps, sem = pool(st)
            NQ = 4
            QT = TOK // NQ
            QB = B // NQ
            TQ = QT // P
            NY = 3
            Win = sb("Win", [P, 2, 2, KD, P])
            Wx = sb("Wx", [P, JD, R + 2 * N])
            Wdt = sb("Wdt", [R, JD, P])
            Wout = sb("Wout", [P, JD, D])
            CD, CT, CB, CW = N, N + 1, N + 2, N + 3
            chan = sb("channel_params", [P, JD, N + 7])
            BC = sb("BC_rows", [P, 2, 2, N, QT])
            xc = sb("xc", [P, 2, JD, QT])
            yz = sb("yz", [P, NY, JD, QT])
            delta = sb("delta", [P, 2, JD, QT])
            xdbl = sb("x_dbl", [R + 2 * N, 2, QT])
            xpad = sb("x_padded", [P, 2, QB, S + 3])
            acc = sb("conv_sum", [P, 2, QT])
            th = sb("tanh", [P, 2, 2, QT])
            gsum = sb("y_sum", [P, QT])
            spc = sb("log_rest", [P, QT])
            NA = 3
            dA = sb("dA", [P, NA, QT])
            hs = sb("state", [P, 4, QT])
            hc = sb("state_C", [P, 4, QT])
            bc_d = nc.dram_tensor("bc_scratch", (NQ, 2 * N, QT), F32).ap()
            bank_x, bank_d = (ps("bank_" + n, [P, D]) for n in ("x", "dt"))
            bank_z = [ps(f"bank_z{i}", [P, D]) for i in range(2)]
            bankY = [ps(f"bankY{i}", [P, D]) for i in range(2)]
            NX = 3
            bank_dx = [ps(f"bank_dx{i}", [P, 2, QT]) for i in range(2)]
            dx, bx = bank_dx[0][:, 0, :], [bank_dx[(i + 1) // 2][:, (i + 1) % 2, :] for i in range(NX)]

            p_in, wx_in, wdt_in, wo_in = sem("params_in"), sem("wx_in"), sem("wdt_in"), sem("wout_in")
            win_in = [sem(f"win_in{i}") for i in range(2)]
            bc_out = sem("bc_stored")
            bc_in = [sem(f"bc_in{i}") for i in range(N // 4)]
            neg_ok = sem("A_exp_ready")
            x_mm = sem("x_done")
            x_cp = sem("x_copied")
            z_mm = sem("z_done")
            cv = sem("conv_done")
            z_th, x_th = sem("tanh_z_done"), sem("tanh_x_done")
            xs = sem("xc_and_gate_done")
            bc_mm, bc_cp = sem("x_dbl_done"), sem("x_dbl_copied")
            d_mm = sem("dt_done")
            abs_ok = sem("abs_ready")
            d_rd = sem("dt_read")
            u_ok = sem("exp_done")
            part_ok, ln_ok = sem("delta_part_ready"), sem("log_done")
            dl_ok = sem("delta_ready")
            da_ok, sc = sem("dA_ready"), sem("state_ready")
            hc_ok = sem("state_C_ready")
            y_mm = sem("y_summed")
            yo = sem("y_gated")
            o_mm, o_ad = sem("out_done"), sem("out_added")
            chain = sem("m_dve_chain")

            def cols(bank, m=P):
                return bank[0:m, 0:QT]

            def uq(q):
                return yz[:, (q + 1) % NY]

            def batches(v):
                return v.rearrange("p (g s) -> p g s", s=S)

            def quarters(slot, step):
                for q in range(NQ + 1):
                    for j in range(JD):
                        for n in range(N):
                            if q < NQ:
                                slot(q, N * j + n)
                            if q > 0:
                                step(q - 1, j, n)

            UNIT, XDBL, XCP, D0, DUNIT, LOG, SUM = 7, 66, 71, 73, 4, 113, 119

            def units(T, first, every):
                u = (T - first) // every
                return [u] if T == first + every * u and 0 <= u < JD else []

            with nc.Block() as block:
                @block.sync
                def _(sp):
                    for q in range(NQ):
                        with sp.Fori(0, JD // 2) as jj:
                            for b in range(2):
                                sp.wait_ge(z_mm, JD * q + 2 * jj + b + 1)
                                for z in range(2):
                                    sp.dma_start(Win[:, b, z, :, :], a["L0_attn_W_in"][
                                        :, ds(z * DI + (2 * jj + b) * P, P)].rearrange("(k p) n -> p k n", p=P)
                                        ).then_inc(win_in[b], 16)
                        sp.wait_ge(bc_cp, 2 * q + 2)
                        sp.dma_start(bc_d[q], xdbl[R:R + 2 * N, q % 2, :]).then_inc(bc_out, 16)
                        sp.wait_ge(bc_out, 16 * q + 16)
                        if q >= 2:
                            sp.wait_ge(yo, 2 + JD * (q - 1))
                        for c4 in range(N // 4):
                            src = bc_d[q].rearrange("(s n) t -> s n t", s=2)[:, 4 * c4:4 * c4 + 4, :]
                            sp.dma_start(BC[:, q % 2, :, 4 * c4:4 * c4 + 4, :],
                                         src.partition_broadcast(P)).then_inc(bc_in[c4], 16)

                @block.gpsimd
                def _(pl):
                    with nc.allow_non_contiguous_dma("channel parameters"):
                        for lo, src in ((0, a["L0_attn_A_log"].rearrange("(j p) n -> p j n", p=P)),
                                        (CD, a["L0_attn_D"].rearrange("(j p o) -> p j o", p=P, o=1)),
                                        (CT, a["L0_attn_b_dt"].rearrange("(j p o) -> p j o", p=P, o=1)),
                                        (CB, a["L0_attn_conv_b"].rearrange("(j p o) -> p j o", p=P, o=1)),
                                        (CW, a["L0_attn_conv_w"].rearrange("(j p) o k -> p j (o k)", p=P))):
                            pl.dma_start(chan[:, :, lo:lo + src.shape[2]], src).then_inc(p_in, 16)
                    pl.dma_start(Wx[:, :, :], a["L0_attn_W_x"].rearrange("(j p) n -> p j n", p=P)).then_inc(wx_in, 16)
                    pl.dma_start(Wdt[:, :, :], a["L0_attn_W_dt"].rearrange("r (j p) -> r j p", p=P)).then_inc(wdt_in, 16)
                    pl.dma_start(Wout[:, :, :], a["L0_attn_W_out"].rearrange("(j p) n -> p j n", p=P)).then_inc(wo_in, 16)
                    pl.sem_inc(hc_ok, 4)
                    for q in range(NQ):
                        for c4 in range(N // 4):
                            pl.wait_ge(bc_in[c4], 16 * q + 16)
                        with pl.Fori(0, JD) as j:
                            for n in range(N):
                                i = (q * JD + j) * N + n
                                pl.wait_ge(sc, NA + i + 1)
                                pl.wait_ge(y_mm, i + 1)
                                pl.tensor_tensor(hc[:, n % 4, :], hs[:, n % 4, :],
                                                 BC[:, q % 2, 1, n, :], ALU.mult).then_inc(hc_ok, 1)

                @block.tensor
                def _(pe):
                    for s, v in ((z_mm, 2), (y_mm, 4)):
                        pe.sem_inc(s, v)

                    def project(q, u, z):
                        U, w = JD * q + u, u % 2
                        if z == 0:
                            pe.wait_ge(win_in[w], 16 * (U - w) + 32)
                            pe.wait_ge(x_cp, U + 1)
                        else:
                            pe.wait_ge(xs, U + 1)
                        for k in range(KD):
                            mm = pe.matmul(cols((bank_x, bank_z[w])[z]), Win[:, w, z, k, :],
                                           xnT[:, k, q * QT:(q + 1) * QT], start=(k == 0), stop=(k == KD - 1))
                        mm.then_inc((x_mm, z_mm)[z], 1)

                    def x_dbl(q):
                        pe.wait_ge(xs, 2 + JD * (q + 1))
                        pe.wait_ge(x_cp, 1 + JD * (q + 1))
                        pe.wait_ge(wx_in, 16)
                        for j in range(JD):
                            mm = pe.matmul(cols(bank_x, R + 2 * N), Wx[:, j, :], xc[:, q % 2, j, :],
                                           start=(j == 0), stop=(j == JD - 1))
                        mm.then_inc(bc_mm, 1)

                    def slot(q, T):
                        for z in range(2):
                            for u in units(T, 2 * z, UNIT):
                                project(q, u, z)
                        if T == XDBL:
                            x_dbl(q)
                        for u in units(T, D0, DUNIT):
                            if u == 0:
                                pe.wait_ge(bc_cp, 2 * q + 2)
                                pe.wait_ge(wdt_in, 16)
                                if q > 1:
                                    pe.wait_ge(o_ad, TQ * (q - 1))
                            pe.wait_ge(d_rd, JD * q + u + 1)
                            pe.matmul(cols(bank_d), Wdt[:, u, :], xdbl[0:R, q % 2, :],
                                      start=True, stop=True).then_inc(d_mm, 1)

                    def out_part(q, t, js):
                        if js[0] == 0:
                            pe.wait_ge(yo, 2 + JD * (q + 1))
                            pe.wait_ge(wo_in, 16)
                            if TQ * q + t:
                                pe.wait_ge(o_ad, TQ * q + t)
                            if q + 1 < NQ:
                                pe.wait_ge(d_rd, 1 + JD * (q + 2))
                        for j in js:
                            mm = pe.matmul(bank_d[:, :], yz[:, q % NY, j, t * P:(t + 1) * P], Wout[:, j, :],
                                           start=(j == 0), stop=(j == JD - 1))
                        if js[-1] == JD - 1:
                            mm.then_inc(o_mm, 1)

                    def step(q, j, n):
                        J = JD * q + j
                        if n == 0:
                            pe.wait_ge(yo, J + 1)
                        pe.wait_ge(hc_ok, 4 + J * N + n + 1)
                        pe.matmul(bankY[j % 2][:, 0:QT], ident[:, :], hc[:, n % 4, :],
                                  start=(n == 0), stop=(n == N - 1)).then_inc(y_mm, 1)
                        if q > 0 and j < JD // 2 and n in (9, 12):
                            lo = 4 * (j % 2) + 2 * (n == 12)
                            out_part(q - 1, j // 2, (lo, lo + 1))

                    quarters(slot, step)
                    for t in range(TQ):
                        out_part(NQ - 1, t, tuple(range(JD)))

                @block.scalar
                def _(act):
                    act.sem_inc(x_cp, 1)
                    act.sem_inc(d_rd, 1)
                    act.wait_ge(p_in, 16 * 5)
                    act.activation(chan[:, :, 0:N], chan[:, :, 0:N], ACT.Exp).then_inc(neg_ok, 1)

                    def pad_x(q, u):
                        U, w = JD * q + u, u % 2
                        act.wait_ge(x_mm, U + 1)
                        act.wait_ge(cv, U + 1)
                        act.activation(xpad[:, w, :, 3:S + 3], batches(cols(bank_x)), ACT.Copy).then_inc(x_cp, 1)

                    def tanh_z(q, u):
                        U, w = JD * q + u, u % 2
                        act.wait_ge(z_mm, 2 + U + 1)
                        act.wait_ge(xs, U + 1)
                        act.activation(th[:, w, 1, :], cols(bank_z[w]), ACT.Tanh, scale=0.5).then_inc(z_th, 1)

                    def tanh_x(q, u):
                        U, w = JD * q + u, u % 2
                        act.wait_ge(cv, 2 + U + 1)
                        act.activation(th[:, w, 0, :], acc[:, w, :], ACT.Tanh).then_inc(x_th, 1)

                    def rectify(q, u):
                        act.wait_ge(d_mm, JD * q + u + 1)
                        if q > 1 and u == 0:
                            act.wait_ge(o_mm, TQ * (q - 1))
                        v, b = cols(bank_d), chan[:, u, CT:CT + 1]
                        act.activation(uq(q)[:, u, :], v, ACT.Abs, bias=b).then_inc(abs_ok, 1)
                        act.activation(delta[:, q % 2, u, :], v, ACT.Relu, bias=b).then_inc(d_rd, 1)

                    def exp_abs(q, u):
                        act.wait_ge(abs_ok, JD * q + u + 1)
                        act.activation(uq(q)[:, u, :], uq(q)[:, u, :], ACT.Exp, scale=-1.0).then_inc(u_ok, 1)

                    def slot(q, T):
                        for what, first, every in ((pad_x, 5, UNIT), (tanh_z, 7, UNIT), (tanh_x, 13, UNIT),
                                                   (rectify, D0 + 3, DUNIT), (exp_abs, D0 + 4, DUNIT)):
                            for u in units(T, first, every):
                                what(q, u)
                        if T == XCP:
                            act.wait_ge(bc_mm, q + 1)
                            for r in (slice(0, R), slice(R, R + 2 * N)):
                                act.activation(xdbl[r, q % 2, :], bank_x[r, 0:QT], ACT.Copy).then_inc(bc_cp, 1)
                        if T == LOG:
                            act.wait_ge(part_ok, 1 + JD * (q + 1))
                            act.activation(uq(q), uq(q), ACT.Ln, bias=1.0).then_inc(ln_ok, 1)

                    def step(q, j, n):
                        i = (JD * q + j) * N + n
                        if j in (0, JD // 2) and n == 0:
                            act.wait_ge(dl_ok, 2 * q + 1 + (j > 0))
                            act.wait_ge(neg_ok, 2)
                        act.wait_ge(sc, i + 1)
                        act.activation(batches(dA[:, i % NA, :])[:, :, 1:S], batches(delta[:, q % 2, j, :])[:, :, 1:S],
                                       ACT.Exp, scale=chan[:, j, n:n + 1]).then_inc(da_ok, 1)

                    quarters(slot, step)

                @block.vector
                def _(dve):
                    for s, v in ((cv, 2), (xs, 2), (part_ok, 1), (sc, NA), (yo, 2)):
                        dve.sem_inc(s, v)
                    c = Chain(dve, chain)
                    c.count(dve.memset(xpad[:, :, :, 0:3], 0.0))
                    for n in range(NA):
                        c.count(dve.memset(batches(dA[:, n, :])[:, :, 0:1], 0.0))
                    dve.wait_ge(neg_ok, 1)
                    dve.tensor_scalar(chan[:, :, 0:N], chan[:, :, 0:N], -1.0, None, ALU.mult).then_inc(neg_ok, 1)
                    c.link(dve.tensor_scalar(chan[:, :, CB:], chan[:, :, CB:], 0.5, None, ALU.mult))
                    last = {"bx": {}}

                    def conv(q, u, k):
                        U, w = JD * q + u, u % 2
                        s3, tap = batches(acc[:, w, :]), chan[:, u, CW + k:CW + k + 1]
                        if k == 0:
                            dve.wait_ge(x_cp, 1 + U + 1)
                            dve.wait_ge(xs, U + 1)
                            last["conv", w] = c.count(dve.tensor_scalar(
                                s3, xpad[:, w, :, 0:S], tap, chan[:, u, CB:CB + 1], ALU.mult, ALU.add))
                            return
                        dve.wait_ge(chain, last["conv", w])
                        ins = dve.scalar_tensor_tensor(s3, xpad[:, w, :, k:k + S], tap, s3, ALU.mult, ALU.add)
                        if k < 3:
                            last["conv", w] = c.count(ins)
                        else:
                            ins.then_inc(cv, 1)

                    def gates(q, u, part):
                        U, w = JD * q + u, u % 2
                        if part == 0:
                            dve.wait_ge(x_th, U + 1)
                            dve.scalar_tensor_tensor(xc[:, q % 2, u, :], th[:, w, 0, :], 1.0, acc[:, w, :],
                                                     ALU.add, ALU.mult)
                        else:
                            dve.wait_ge(z_th, U + 1)
                            dve.scalar_tensor_tensor(yz[:, q % NY, u, :], th[:, w, 1, :], 1.0, cols(bank_z[w]),
                                                     ALU.add, ALU.mult).then_inc(xs, 1)

                    def log_rest(q, u, part):
                        U, uu, dl = JD * q + u, uq(q)[:, u, :], delta[:, q % 2, u, :]
                        if part == 0:
                            dve.wait_ge(u_ok, U + 1)
                            dve.wait_ge(part_ok, U + 1)
                            last["rest"] = c.count(dve.tensor_scalar(spc[:, :], uu, 1.0, -1.0, ALU.add, ALU.add))
                        elif part == 1:
                            dve.wait_ge(chain, last["rest"])
                            last["rest"] = c.count(dve.tensor_tensor(spc[:, :], uu, spc[:, :], ALU.subtract))
                        else:
                            dve.wait_ge(chain, last["rest"])
                            dve.tensor_tensor(dl, dl, spc[:, :], ALU.add).then_inc(part_ok, 1)

                    def slot(q, T):
                        for what, first, every, parts in ((conv, 7, UNIT, 4), (gates, 15, UNIT, 2),
                                                          (log_rest, D0 + 7, DUNIT, 3)):
                            for part in range(parts):
                                for u in units(T, first + part, every):
                                    what(q, u, part)
                        if T in (SUM, SUM + 1):
                            dve.wait_ge(ln_ok, q + 1)
                            h = slice(0, JD // 2) if T == SUM else slice(JD // 2, JD)
                            dl = delta[:, q % 2, h, :]
                            dve.tensor_tensor(dl, dl, uq(q)[:, h, :], ALU.add).then_inc(dl_ok, 1)

                    def prepare(q, j):
                        if JD * q + j:
                            dve.wait_ge(chain, last["bx"][N - 1])
                        if j == 0:
                            dve.wait_ge(dl_ok, 2 * q + 2)
                            for c4 in range(N // 4):
                                dve.wait_ge(bc_in[c4], 16 * q + 16)
                        last["dx"] = c.count(dve.tensor_tensor(dx, delta[:, q % 2, j, :],
                                                               xc[:, q % 2, j, :], ALU.mult))

                    def drive(q, j, n):
                        i = (JD * q + j) * N + n
                        if n == 0:
                            dve.wait_ge(chain, last["dx"])
                        if i >= NX:
                            dve.wait_ge(sc, NA + i - NX + 1)
                        last["bx"][n] = c.count(dve.tensor_tensor(bx[i % NX], dx,
                                                                  BC[:, q % 2, 0, n, :], ALU.mult))

                    def gate_y(q, j, part):
                        if part == 0:
                            dve.wait_ge(y_mm, 4 + N * (JD * q + j + 1))
                            dve.wait_ge(yo, 2 + JD * q + j)
                            last["gate"] = c.count(dve.scalar_tensor_tensor(
                                gsum[:, :], xc[:, q % 2, j, :], chan[:, j, CD:CD + 1], bankY[j % 2][:, 0:QT],
                                ALU.mult, ALU.add))
                        else:
                            dve.wait_ge(chain, last["gate"])
                            g = yz[:, q % NY, j, :]
                            dve.scalar_tensor_tensor(g, gsum[:, :], 0.5, g, ALU.mult, ALU.mult).then_inc(yo, 1)

                    def add_out(q, t):
                        dve.wait_ge(o_mm, TQ * q + t + 1)
                        xr = xres[:, TQ * q + t, :]
                        dve.tensor_tensor(xr, xr, bank_d[:, :], ALU.add).then_inc(o_ad, 1)

                    def step(q, j, n):
                        i = (JD * q + j) * N + n
                        if i == 0:
                            prepare(0, 0)
                            drive(0, 0, 0)
                        need = last["bx"][n]
                        before, after = divmod(JD * q + j - 1, JD), divmod(JD * q + j + 1, JD)
                        if i >= N and n in (5, 6):
                            gate_y(*before, n - 5)
                        if q > 0 and (j, n) in ((2, 2), (4, 2)):
                            add_out(q - 1, j // 2 - 1)
                        if n < N - 1:
                            drive(q, j, n + 1)
                        elif after[0] < NQ:
                            prepare(*after)
                            drive(*after, 0)
                        dve.wait_ge(chain, need)
                        dve.wait_ge(da_ok, i + 1)
                        dve.wait_ge(hc_ok, i + 1)
                        dve.tensor_tensor_scan(hs[:, n % 4, :], dA[:, i % NA, :], bx[i % NX],
                                               0.0, ALU.mult, ALU.add).then_inc(sc, 1)

                    quarters(slot, step)
                    for part in range(2):
                        gate_y(NQ - 1, JD - 1, part)
                    for t in range(TQ):
                        add_out(NQ - 1, t)
        if debug == "mamba":
            return store_x()

        pos = sb0("slot_of_choice", [P, 2, NT], I32)
        prob2 = sb0("choice_prob", [P, 2, NT])
        eid = sb0("expert_of_slot_tile", [P, NS], I32)
        with ExitStack() as st:
            sb, ps, sem = pool(st)
            xrow = sb("xn_rows", [P, NT, D])
            norm_phase("n3_", keep=xrow)
            rw = sb("router_wT", [P, KD, E])
            rb = sb("router_b", [P, E])
            ones, before = sb("ones", [P, P]), sb("rows_before", [P, P])
            iE, iJ, iS = sb("iota_e_minus_E", [P, E]), sb("iota_tile_rows", [P, NT]), sb("iota_slot_tile", [P, NS])
            names = ("logits", "masked", "eq", "cand", "one1", "one2", "sel", "where_", "q1", "q2")
            lg, lg2, eq, cand, one1, one2, sel, where, q1, q2 = (sb("r_" + n, [P, NT, E]) for n in names)
            csel = sb("sel_of_tiles_before", [P, NT + 1, E])
            m1, m2, i1, i2, dif, e2, den, p1f, p2f = (sb("r_m%d" % n, [P, NT]) for n in range(9))
            cnt, ntile = sb("expert_count", [P, E]), sb("expert_tiles", [P, E])
            ends = sb("expert_tile_starts", [P, E + 1])
            rows0 = sb("expert_first_row", [P, E])
            more = sb("tile_needed", [P, E, NT])
            past = sb("expert_is_past", [P, NS, E])
            pastn = sb("experts_past", [P, NS])
            bankL, bankR, bankC = (ps("bank" + n, [P, 512]) for n in "LRC")
            r_in, io_ok, bf_ok = sem("router_in"), sem("iota_ready"), sem("rows_before_ready")
            one_ok = sem("ones_ready")
            l_mm, sel_ok, r_mm = sem("logits_done"), sem("choices_ready"), sem("ranks_done")
            dif_ok, e2_ok = sem("logit_gap_ready"), sem("gap_exp_ready")
            pos_ok, sc_done, chain = sem("slots_ready"), sem("rows_scattered"), sem("r_dve_chain")

            def tE(v):
                return v.unsqueeze(2).to_broadcast([P, NT, E])

            def eT(v):
                return v.unsqueeze(1).to_broadcast([P, NT, E])

            with nc.Block() as block:
                @block.sync
                def _(sp):
                    with nc.allow_non_contiguous_dma("router weights by model dimension"):
                        for k in range(KD):
                            sp.dma_start(rw[:, k, :], a["L0_ffn_router_w"][:, k * P:(k + 1) * P].rearrange("e p -> p e"),
                                         allow_slow_non_contiguous=True).then_inc(r_in, 16)
                    sp.dma_start(rb[:, :], a["L0_ffn_router_b"].partition_broadcast(P)).then_inc(r_in, 16)
                    sp.wait_ge(r_in, 16 * (KD + 1))

                @block.gpsimd
                def _(pl):
                    for v, base, step in ((iE, -E, 1), (iJ, 0, P), (iS, 0, 1)):
                        pl.iota(v[:, :], pattern=[[step, v.shape[1]]], base=base, channel_multiplier=0,
                                allow_small_or_imprecise_dtypes=True).then_inc(io_ok, 1)
                    pl.memset(ones[:, :], 1.0).then_inc(one_ok, 1)
                    pl.wait_ge(one_ok, 1)
                    pl.affine_select(out=before[:, :], in_=ones[:, :], compare_op=ALU.is_gt, fill=0.0,
                                     base=0, pattern=[[1, P]], channel_multiplier=-1).then_inc(bf_ok, 1)
                    pl.wait_ge(xs_zero, 16)
                    pl.wait_ge(pos_ok, 2)
                    for k in range(2):
                        for t in range(NT):
                            pl.indirect_dma_start(xs_d, bass.IndirectOffsetOnAxis(ap=pos[:, k, t:t + 1], axis=0),
                                                  xrow[:, t, :], None).then_inc(sc_done, 16)
                    pl.wait_ge(sc_done, 16 * 2 * NT)

                @block.tensor
                def _(pe):
                    pe.wait_ge(r_in, 16 * (KD + 1))
                    for t in range(NT):
                        for k in range(KD):
                            mm = pe.matmul(bankL[:, t * E:(t + 1) * E], xnT[:, k, t * P:(t + 1) * P], rw[:, k, :],
                                           start=(k == 0), stop=(k == KD - 1))
                    mm.then_inc(l_mm, 1)
                    pe.wait_ge(bf_ok, 1)
                    pe.wait_ge(sel_ok, 1)
                    pe.matmul(bankR[:, 0:NT * E], before[:, :], sel[:, :, :].rearrange("p t e -> p (t e)"),
                              start=True, stop=False)
                    pe.matmul(bankR[:, 0:NT * E], ones[:, :], csel[:, 0:NT, :].rearrange("p t e -> p (t e)"),
                              start=False, stop=True).then_inc(r_mm, 1)
                    pe.matmul(bankC[:, 0:E], ones[:, :], csel[:, NT, :], start=True, stop=True).then_inc(r_mm, 1)

                @block.scalar
                def _(act):
                    act.wait_ge(dif_ok, 1)
                    act.activation(e2[:, :], dif[:, :], ACT.Exp).then_inc(e2_ok, 1)

                @block.vector
                def _(dve):
                    c = Chain(dve, chain)

                    def tt(o, x, y, op):
                        c.link(dve.tensor_tensor(o, x, y, op))

                    def first_max(src, m, i, one):
                        c.link(dve.tensor_reduce(m[:, :], src[:, :, :], AX.X, ALU.max))
                        tt(eq[:, :, :], src[:, :, :], tE(m[:, :]), ALU.is_equal)
                        tt(cand[:, :, :], eq[:, :, :], eT(iE[:, :]), ALU.mult)
                        c.link(dve.tensor_reduce(i[:, :], cand[:, :, :], AX.X, ALU.min))
                        tt(one[:, :, :], eT(iE[:, :]), tE(i[:, :]), ALU.is_equal)

                    dve.wait_ge(l_mm, 1)
                    dve.wait_ge(io_ok, 3)
                    tt(lg[:, :, :], bankL[:, 0:NT * E].rearrange("p (t e) -> p t e", e=E), eT(rb[:, :]), ALU.add)
                    first_max(lg, m1, i1, one1)
                    c.link(dve.scalar_tensor_tensor(lg2[:, :, :], one1[:, :, :], -3e38, lg[:, :, :], ALU.mult, ALU.add))
                    first_max(lg2, m2, i2, one2)
                    dve.tensor_tensor(dif[:, :], m2[:, :], m1[:, :], ALU.subtract).then_inc(dif_ok, 1)
                    tt(sel[:, :, :], one1[:, :, :], one2[:, :, :], ALU.add)
                    c.link(dve.memset(csel[:, 0, :], 0.0))
                    for t in range(NT):
                        ins = dve.tensor_tensor(csel[:, t + 1, :], csel[:, t, :], sel[:, t, :], ALU.add)
                        if t + 1 < NT:
                            c.link(ins)
                    ins.then_inc(sel_ok, 1)
                    dve.wait_ge(e2_ok, 1)
                    c.link(dve.tensor_scalar(den[:, :], e2[:, :], 1.0, None, ALU.add))
                    c.link(dve.reciprocal(prob2[:, 0, :], den[:, :]))
                    tt(prob2[:, 1, :], prob2[:, 0, :], e2[:, :], ALU.mult)
                    dve.wait_ge(r_mm, 2)
                    c.link(dve.tensor_copy(cnt[:, :], bankC[:, 0:E]))
                    tt(more[:, :, :], cnt[:, :].unsqueeze(2).to_broadcast([P, E, NT]),
                       iJ[:, :].unsqueeze(1).to_broadcast([P, E, NT]), ALU.is_gt)
                    c.link(dve.tensor_reduce(ntile[:, :], more[:, :, :], AX.X, ALU.add))
                    c.link(dve.memset(ends[:, 0:1], 0.0))
                    for e in range(E):
                        tt(ends[:, e + 1:e + 2], ends[:, e:e + 1], ntile[:, e:e + 1], ALU.add)
                    c.link(dve.tensor_scalar(rows0[:, :], ends[:, 0:E], float(P), None, ALU.mult))
                    tt(where[:, :, :], bankR[:, 0:NT * E].rearrange("p (t e) -> p t e", e=E), eT(rows0[:, :]), ALU.add)
                    for k, (one, q, f) in enumerate(((one1, q1, p1f), (one2, q2, p2f))):
                        tt(q[:, :, :], one[:, :, :], where[:, :, :], ALU.mult)
                        c.link(dve.tensor_reduce(f[:, :], q[:, :, :], AX.X, ALU.add))
                        dve.tensor_copy(pos[:, k, :], f[:, :]).then_inc(pos_ok, 1)
                    tt(past[:, :, :], ends[:, 1:E + 1].unsqueeze(1).to_broadcast([P, NS, E]),
                       iS[:, :].unsqueeze(2).to_broadcast([P, NS, E]), ALU.is_le)
                    c.link(dve.tensor_reduce(pastn[:, :], past[:, :, :], AX.X, ALU.add))
                    c.link(dve.tensor_scalar(pastn[:, :], pastn[:, :], float(E - 1), None, ALU.min))
                    c.link(dve.tensor_copy(eid[:, :], pastn[:, :]))

        with ExitStack() as st:
            sb, ps, sem = pool(st)
            V_, W_, O_ = range(3)
            PCS = 4
            PER = 3 * PCS
            COLS = KD * FH // PCS
            w_all = [sb(n, [P, 2, PCS, COLS]) for n in ("Ve", "We", "Woe")]
            ring = sb("weight_pieces_HL", [P, PCS, 2, COLS], F32R)
            xs = sb("slot_rows", [P, 2, D])
            xT = sb("slot_rowsT_HL", [P, 2, 2, KD, P], F32R)
            gate_ = sb("silu_b", [P, 2, 512])
            y = sb("hidden", [P, JF, P])
            yT = sb("hiddenT_HL", [P, 2, JF, P], F32R)
            osb = sb("slot_out", [P, 2, D])
            bankA = [ps(f"bankA{i}", [P, 512]) for i in range(2)]
            bankB = [ps(f"bankB{i}", [P, 512]) for i in range(2)]
            bankT = [ps(f"bankYT{i}", [P, KD, P]) for i in range(2)]
            bankX, bankO = ps("bankXT", [P, KD, P]), ps("bankOut", [P, D])
            in_ = [[sem(f"{n}_in{i}") for i in range(2)] for n in ("ve", "we", "woe")]
            x_in2 = [sem(f"slot_in{i}") for i in range(2)]
            hi, lo = sem("piece_H_ready"), sem("piece_L_ready")
            HEAD = 2 * PER
            used = sem("piece_used")
            x_tr = sem("slot_rows_turned")
            x_hi, x_cp = sem("slot_rowsT_H_ready"), sem("slot_rowsT_ready")
            g_ok = sem("silu_ready")
            y_ok = sem("hidden_ready")
            y_tr, y_hi = sem("hidden_turned"), sem("hiddenT_H_ready")
            y_cp = sem("hiddenT_ready")
            o_cp = sem("slot_out_copied")
            o_st = [sem(f"slot_out_stored{i}") for i in range(2)]
            last = NS - 1

            def tiles(eng, first, step):
                pairs = (last - 1 - first) // 2
                with eng.Fori(0, pairs) as i:
                    for h in range(2):
                        step(2 * i + first + h, (first + h) % 2)
                for s in range(first + 2 * pairs, last + 1):
                    step(s, s % 2)

            def use(s, b):
                return (s - b) * 8 + 16

            def piece(s, m, k):
                if isinstance(s, int) and s in (0, last + 1):
                    return PER * s - (PCS if s else 0) + PCS * (m if s == 0 else 0) + k
                return PER * s + (PCS * (m - 1) + k)

            def out_piece(s):
                return piece(s + 1, O_, PCS - 1)

            with nc.Block() as block:
                @block.sync
                def _(sp):
                    def step(s, b):
                        e = sp.value_load(eid[0:1, ds(s, 1)], min_val=0, max_val=E - 1)
                        new = 1
                        if not (isinstance(s, int) and s < 2):
                            new = e != sp.value_load(eid[0:1, ds(s - 2, 1)], min_val=0, max_val=E - 1)
                        sp.wait_ge(x_tr, s + 1)
                        plain(sp)
                        sp.dma_start(xs[:, b, :], xs_d[ds(s * P, P), :]).then_inc(x_in2[b], 16)
                        for m, name in ((V_, "V"), (W_, "W"), (O_, "W_out")):
                            sp.wait_ge(lo, PER * s + (PCS, 2 * PCS, HEAD - PCS)[m])
                            plain(sp)
                            sp.dma_start(w_all[m][:, b, :, :].rearrange("p c n -> p (c n)").rearrange(
                                "p (k f) -> p k f", f=(FH, FH, D)[m]), a["L0_ffn_" + name][ds(e, 1)].rearrange(
                                "e (k p) f -> p (e k) f", p=P), cond=new).then_inc(in_[m][b], 16)
                    step(0, 0)
                    step(1, 1)
                    tiles(sp, 2, step)

                @block.gpsimd
                def _(pl):
                    def step(s, b):
                        pl.wait_ge(o_cp, 1 + s + 1)
                        plain(pl)
                        pl.dma_start(ys_d[ds(s * P, P), :], osb[:, b, :]).then_inc(o_st[b], 16)
                    tiles(pl, 0, step)
                    pl.wait_ge(o_st[0], 16 * ((NS + 1) // 2))
                    pl.wait_ge(o_st[1], 16 * (NS // 2))

                @block.tensor
                def _(pe):
                    for s, v in ((used, PCS), (x_tr, 2)):
                        pe.sem_inc(s, v)

                    def turn_x(s, b):
                        pe.wait_ge(x_in2[b], use(s, b))
                        pe.wait_ge(x_cp, s + 1)
                        for k in range(KD):
                            mm = pe.transpose(bankX[:, k, :], xs[:, b, k * P:(k + 1) * P], ident[:, :])
                        mm.then_inc(x_tr, 1)

                    def up(s, b, m, bank, free):
                        pe.wait_ge(free, 2 * s + 2)
                        for k in range(KD):
                            pe.wait_ge(lo, HEAD + piece(s, m, k) + 1)
                            for l, r in ((0, 0), (0, 1), (1, 0)):
                                for h in range(2):
                                    mm = pe.matmul(bank[h][:, :], xT[:, b, l, k, :],
                                                   ring[:, k, r, 512 * h:512 * h + 512],
                                                   start=(k == l == r == 0), stop=(k == KD - 1 and l == 1))
                            mm.then_inc(used, 1)

                    def turn_y(s):
                        for h in range(2):
                            pe.wait_ge(y_ok, 2 + 2 * s + h + 1)
                            pe.wait_ge(y_cp, 2 * s + h + 1)
                            for k in range(KD):
                                mm = pe.transpose(bankT[h][:, k, :], y[:, KD * h + k, :], ident[:, :])
                            mm.then_inc(y_tr, 1)

                    def down(s, nxt):
                        pe.wait_ge(o_cp, s + 1)
                        pe.wait_ge(y_cp, 2 + 2 * s + 2)
                        for c in range(PCS):
                            pe.wait_ge(lo, HEAD + piece(nxt, O_, c) + 1)
                            for h in range(2):
                                j = 2 * c + h
                                for l, r in ((0, 0), (0, 1), (1, 0)):
                                    mm = pe.matmul(bankO[:, :], yT[:, l, j, :], ring[:, c, r, 512 * h:512 * h + 512],
                                                   start=(j == l == r == 0), stop=(j == JF - 1 and l == 1))
                            mm.then_inc(used, 1)

                    def step(s, b, first=False):
                        pe.wait_ge(x_cp, 1 + s + 1)
                        up(s, b, V_, bankB, g_ok)
                        up(s, b, W_, bankA, y_ok)
                        if not (isinstance(s, int) and s == last):
                            turn_x(s + 1, 1 - b)
                        if not first:
                            down(s - 1, s)
                        turn_y(s)
                    turn_x(0, 0)
                    step(0, 0, first=True)
                    tiles(pe, 1, step)
                    down(last, last + 1)

                @block.scalar
                def _(act):
                    act.sem_inc(g_ok, 2)

                    def split(s, b, m, k):
                        n = piece(s, m, k)
                        if k == 0:
                            act.wait_ge(in_[m][b], use(s if m != O_ else s - 1, b))
                        act.wait_ge(used, n + 1)
                        act.activation(ring[:, k, 0, :], w_all[m][:, b, k, :], ACT.Copy).then_inc(hi, 1)

                    def x_high(s, b):
                        act.wait_ge(x_tr, 2 + s + 1)
                        act.activation(xT[:, b, 0, :, :], bankX[:, :, :], ACT.Copy).then_inc(x_hi, 1)

                    def y_high(s):
                        for h in range(2):
                            act.wait_ge(y_tr, 2 * s + h + 1)
                            act.activation(yT[:, 0, KD * h:KD * h + KD, :], bankT[h][:, :, :], ACT.Copy).then_inc(y_hi, 1)

                    def step(s, b, first=False):
                        for k in range(PCS):
                            split(s, b, V_, k)
                        if not first:
                            y_high(s - 1)
                        for k in range(PCS):
                            split(s, b, W_, k)
                        act.wait_ge(used, PCS + piece(s, V_, PCS - 1) + 1)
                        act.wait_ge(y_ok, 2 * s + 2)
                        for h in range(2):
                            act.activation(gate_[:, h, :], bankB[h][:, :], ACT.Silu).then_inc(g_ok, 1)
                        if not first:
                            for k in range(PCS - 1):
                                split(s, 1 - b, O_, k)
                        if not (isinstance(s, int) and s == last):
                            x_high(s + 1, 1 - b)
                        if not first:
                            split(s, 1 - b, O_, PCS - 1)
                    x_high(0, 0)
                    step(0, 0, first=True)
                    tiles(act, 1, step)
                    y_high(last)
                    for k in range(PCS):
                        split(last + 1, last % 2, O_, k)

                @block.vector
                def _(dve):
                    dve.sem_inc(lo, HEAD)
                    dve.sem_inc(x_cp, 1)
                    dve.sem_inc(y_ok, 2)
                    dve.sem_inc(y_cp, 2)
                    dve.sem_inc(o_cp, 1)

                    def rest(s, b, m, k):
                        dve.wait_ge(hi, piece(s, m, k) + 1)
                        dve.tensor_tensor(ring[:, k, 1, :], w_all[m][:, b, k, :], ring[:, k, 0, :],
                                          ALU.subtract).then_inc(lo, 1)

                    def x_low(s, b):
                        dve.wait_ge(x_hi, s + 1)
                        dve.tensor_tensor(xT[:, b, 1, :, :], bankX[:, :, :], xT[:, b, 0, :, :],
                                          ALU.subtract).then_inc(x_cp, 1)

                    def y_low(s):
                        for h in range(2):
                            r = slice(KD * h, KD * h + KD)
                            dve.wait_ge(y_hi, 2 * s + h + 1)
                            dve.tensor_tensor(yT[:, 1, r, :], bankT[h][:, :, :], yT[:, 0, r, :],
                                              ALU.subtract).then_inc(y_cp, 1)

                    def copy_out(s, b, stored=True):
                        dve.wait_ge(used, PCS + out_piece(s) + 1)
                        if stored:
                            dve.wait_ge(o_st[b], (s - b) * 8)
                        dve.tensor_copy(osb[:, b, :], bankO[:, :]).then_inc(o_cp, 1)

                    def step(s, b, first=False):
                        for k in range(PCS):
                            rest(s, b, V_, k)
                        if not first:
                            y_low(s - 1)
                            if not (isinstance(s, int) and s < 2):
                                copy_out(s - 2, b, stored=not (isinstance(s, int) and s < 4))
                        for k in range(PCS):
                            rest(s, b, W_, k)
                        if not first:
                            for k in range(PCS - 1):
                                rest(s, 1 - b, O_, k)
                        dve.wait_ge(used, PCS + piece(s, W_, PCS - 1) + 1)
                        if not first:
                            dve.wait_ge(y_tr, 2 * s)
                        for h in range(2):
                            dve.wait_ge(g_ok, 2 + 2 * s + h + 1)
                            dve.tensor_tensor(y[:, KD * h:KD * h + KD, :].rearrange("p k q -> p (k q)"),
                                              bankA[h][:, :], gate_[:, h, :], ALU.mult).then_inc(y_ok, 1)
                        if not (isinstance(s, int) and s == last):
                            x_low(s + 1, 1 - b)
                        if not first:
                            rest(s, 1 - b, O_, PCS - 1)
                    x_low(0, 0)
                    for s in range(4):
                        step(s, s % 2, first=(s == 0))
                    tiles(dve, 4, step)
                    y_low(last)
                    copy_out(last - 1, (last - 1) % 2)
                    for k in range(PCS):
                        rest(last + 1, last % 2, O_, k)
                    copy_out(last, last % 2)

        with ExitStack() as st:
            sb, ps, sem = pool(st)
            got = sb("expert_rows", [P, 2, NT, D])
            g_in = [sem(f"expert_rows_in{i}") for i in range(NT)]
            chain, done = sem("c_dve_chain"), sem("out_stored")
            f_ok = sem("x_final")
            with nc.Block() as block:
                @block.gpsimd
                def _(pl):
                    for t in range(NT):
                        for k in range(2):
                            pl.indirect_dma_start(got[:, k, t, :], None, ys_d,
                                                  bass.IndirectOffsetOnAxis(ap=pos[:, k, t:t + 1], axis=0)
                                                  ).then_inc(g_in[t], 16)

                @block.vector
                def _(dve):
                    c = Chain(dve, chain)
                    for t in range(NT):
                        dve.wait_ge(g_in[t], 32)
                        for k in range(2):
                            ins = dve.scalar_tensor_tensor(xres[:, t, :], got[:, k, t, :], prob2[:, k, t:t + 1],
                                                           xres[:, t, :], ALU.mult, ALU.add)
                            if k == 0:
                                c.link(ins)
                        ins.then_inc(f_ok, 1)

                @block.sync
                def _(sp):
                    for t in range(NT):
                        sp.wait_ge(f_ok, t + 1)
                        sp.dma_start(out_d[t * P:(t + 1) * P, :], xres[:, t, :]).then_inc(done, 16)
                    sp.wait_ge(done, 16 * NT)


DEBUG = None


def kernel(**inputs):
    import numpy as _np
    import concourse.bacc as _bacc
    from concourse import mybir as _mybir
    from concourse.bass_utils import run_bass_kernel_spmd as _run

    nc = _bacc.Bacc("TRN2", target_bir_lowering=False, num_devices=1)
    arrays, args = {}, {}
    for name, v in inputs.items():
        v = _np.ascontiguousarray(v)
        arrays[f"in_{name}"] = v
        args[name] = nc.dram_tensor(f"in_{name}", v.shape, _mybir.dt.from_np(v.dtype), kind="ExternalInput").ap()
    shape = arrays["in_x"].shape
    out = nc.dram_tensor("out_0", shape, F32, kind="ExternalOutput").ap()
    build(nc, args, out, DEBUG)
    r = _run(nc, [arrays], core_ids=[0])
    return r.results[0]["out_0"]
```

```python
from contextlib import ExitStack

import concourse.bass as bass
from concourse import mybir

F32 = mybir.dt.float32
F32R = mybir.dt.float32r
I32 = mybir.dt.int32
U32 = mybir.dt.uint32
ALU = mybir.AluOpType
ACT = mybir.ActivationFunctionType
AX = mybir.AxisListType

P = 128
EPS = 1e-5
ds = bass.ds


class Chain:

    def __init__(self, eng, sem):
        self.eng, self.sem, self.base, self.k, self.outer = eng, sem, 0, 0, []

    def count(self, ins):
        ins.then_inc(self.sem, 1)
        self.k += 1
        return self.base + self.k

    def link(self, ins):
        self.eng.wait_ge(self.sem, self.count(ins))

    def enter(self, i, per):
        self.outer.append((self.base, self.k, per))
        self.base, self.k = self.base + self.k + i * per, 0

    def leave(self, times):
        base, k, per = self.outer.pop()
        assert self.k == per, (self.k, per)
        self.base, self.k = base, k + per * times


def build(nc, a, out, debug=None):
    x_d = a["x"].rearrange("b s d -> (b s) d")
    ctx_d = a["ctx_1024"]
    out_d = out.rearrange("b s d -> (b s) d")
    B, S, D = a["x"].shape
    CK = ctx_d.shape[1]
    KD = D // P
    KC = CK // P
    TOK = B * S
    NT = TOK // P
    H, DH = 16, 32
    NP = H // 2
    SCALE = float(DH) ** -0.5
    DI = a["L0_attn_D"].shape[0]
    JD = DI // P
    N = a["L0_attn_A_log"].shape[1]
    R = a["L0_attn_W_dt"].shape[0]
    E = a["L0_ffn_router_w"].shape[0]
    FH = a["L0_ffn_W"].shape[2]
    JF = FH // P
    NS = 2 * TOK // P + E - 1

    whole = ExitStack()

    def pool(stack):
        def sb(name, shape, dt=F32):
            return stack.enter_context(nc.sbuf_tensor(name, shape, dt))

        def ps(name, shape):
            return stack.enter_context(nc.psum_tensor(name, shape, F32))

        def sem(name):
            return stack.enter_context(nc.semaphore(name))
        return sb, ps, sem

    with whole:
        sb0, _, sem0 = pool(whole)
        xres = sb0("xres", [P, NT, D])
        xnT = sb0("xnT", [P, KD, TOK])
        ident = sb0("ident", [P, P])
        xs_d = nc.dram_tensor("slot_rows_scratch", (NS * P, D), F32).ap()
        ys_d = nc.dram_tensor("slot_out_scratch", (NS * P, D), F32).ap()
        z_ok, xs_zero = sem0("zeros_ready"), sem0("slot_rows_zeroed")
        x_in, ident0, ident_ok = sem0("x_in"), sem0("ident_zeroed"), sem0("ident_ready")

        carried = sem0("waits_carried")

        def plain(eng):
            eng.sem_inc(carried, 1)

        def norm_phase(tag, keep=None, load=None, use=None):
            with ExitStack() as st:
                sb, ps, sem = pool(st)
                stats = sb(tag + "stats", [P, NT, nc.vector.BN_STATS_DIM])
                mv = sb(tag + "mv", [P, NT, nc.vector.BN_AGGR_DIM])
                veps, std, rstd = (sb(tag + n, [P, NT]) for n in ("var_eps", "std", "rstd"))
                var_ready, std_ready = sem(tag + "var_ready"), sem(tag + "std_ready")
                xn = keep if keep is not None else sb(tag + "xn", [P, 2, D])
                bank = [ps(tag + f"bank{i}", [P, KD, P]) for i in range(2)]
                chain = sem(tag + "dve_chain")
                xn_ready = sem(tag + "xn_ready")
                turned = sem(tag + "xn_turned")
                copied = sem(tag + "xnT_copied")
                with nc.Block() as block:
                    @block.vector
                    def _(dve):
                        for t in range(NT):
                            dve.bn_stats(stats[:, t, :], xres[:, t, :]).then_inc(chain, 1)
                        dve.wait_ge(chain, NT)
                        for t in range(NT):
                            dve.bn_aggr(mv[:, t, :], stats[:, t, :]).then_inc(chain, 1)
                        dve.wait_ge(chain, 2 * NT)
                        dve.tensor_scalar(veps[:, :], mv[:, :, 1:2].rearrange("p t o -> p (t o)"), EPS, None,
                                          ALU.add).then_inc(var_ready, 1)
                        dve.wait_ge(std_ready, 1)
                        dve.reciprocal(rstd[:, :], std[:, :]).then_inc(chain, 1)
                        dve.wait_ge(chain, 2 * NT + 1)
                        for t in range(NT):
                            b = t if keep is not None else t % 2
                            if keep is None:
                                dve.wait_ge(turned, t + 1)
                            dve.tensor_scalar(xn[:, b, :], xres[:, t, :], mv[:, t, 0:1], rstd[:, t:t + 1],
                                              ALU.subtract, ALU.mult).then_inc(xn_ready, 1)

                    @block.tensor
                    def _(pe):
                        pe.sem_inc(turned, 2)

                        def turn(t, b, row):
                            pe.wait_ge(xn_ready, t + 1)
                            pe.wait_ge(copied, t + 1)
                            for k in range(KD):
                                mm = pe.transpose(bank[b][:, k, :], xn[:, row, k * P:(k + 1) * P], ident[:, :])
                            mm.then_inc(turned, 1)
                        if keep is None:
                            with pe.Fori(0, NT // 2) as i:
                                for b in range(2):
                                    turn(2 * i + b, b, b)
                        else:
                            for t in range(NT + 1):
                                if t < NT:
                                    turn(t, t % 2, t)
                                if t > 0:
                                    pe.wait_ge(copied, 2 + t)
                                    use(pe, t - 1)

                    @block.scalar
                    def _(act):
                        act.sem_inc(copied, 2)
                        act.wait_ge(var_ready, 1)
                        act.activation(std[:, :], veps[:, :], ACT.Sqrt).then_inc(std_ready, 1)
                        with act.Fori(0, NT // 2) as i:
                            for b in range(2):
                                t = 2 * i + b
                                act.wait_ge(turned, 2 + t + 1)
                                act.activation(xnT[:, :, ds(t * P, P)], bank[b][:, :, :], ACT.Copy).then_inc(copied, 1)

                    if load is not None:
                        @block.sync
                        def _(sp):
                            load(sp)

        with ExitStack() as st:
            sb, ps, sem = pool(st)
            Wk, Wv = (sb(n, [P, 2, KD, D], F32R) for n in ("Wk_HL", "Wv_HL"))
            Wo = sb("Wo", [P, KD, D])
            ctxs = sb("ctx_rows", [P, 2, KC, D])
            Wq = sb("Wq", [P, KD, D])
            ctxT = sb("ctxT_HL", [P, 2, 2, KD, CK], F32R)
            KT = sb("KT", [P, 2, KD, CK])
            V = sb("V", [P, 2, KC, D])
            QT = sb("QT", [P, KD, TOK])
            qbd = [sb(f"q_blocks{i}", [P, KD, P]) for i in range(2)]
            head_of = sb("head_parity", [P, 2])
            prob = sb("prob", [P, 2, CK])
            probT = sb("probT", [P, 2, KC, P])
            nmax = sb("neg_max", [P, 2, NP])
            rsum = sb("row_sum", [P, 2, NP])
            rinv = sb("row_inv", [P, 2, NP])
            cn = sb("context", [P, D])
            cnT = sb("contextT", [P, KD, P])
            bias = {n: sb(n, [P, KD]) for n in ("bq", "bk", "bv")}
            bqs = sb("bq_scaled", [P, KD])
            bo = sb("bo_rows", [P, D])
            zeros = sb("zeros", [P, D])
            wq_in, w_in, o_in, b_in = sem("wq_in"), sem("w_kv_in"), sem("wo_in"), sem("b_in")
            ctx_in = [sem(f"ctx_in{i}") for i in range(2)]

            with nc.Block() as block:
                @block.sync
                def _(sp):
                    sp.dma_start(xres[:, :, :], x_d.rearrange("(t p) d -> p t d", p=P)).then_inc(x_in, 16)
                    sp.dma_start(Wq[:, :, :], a["L0_xattn_Wq"].rearrange("(k p) n -> p k n", p=P)).then_inc(wq_in, 16)
                    for n in ("bq", "bk", "bv"):
                        with nc.allow_non_contiguous_dma("bias by channel"):
                            sp.dma_start(bias[n][:, :], a["L0_xattn_" + n].rearrange("(k p) -> p k", p=P)).then_inc(b_in, 16)
                    sp.dma_start(bo[:, :], a["L0_xattn_bo"].partition_broadcast(P)).then_inc(b_in, 16)
                    for n, w in (("L0_xattn_Wk", KT), ("L0_xattn_Wv", V)):
                        sp.dma_start(w[:, 1, :, :], a[n].rearrange("(k p) n -> p k n", p=P)).then_inc(w_in, 16)
                    for g in range(2):
                        sp.dma_start(ctxs[:, g, :, :], ctx_d[g].rearrange("(k p) d -> p k d", p=P)).then_inc(ctx_in[g], 16)
                    sp.dma_start(Wo[:, :, :], a["L0_xattn_Wo"].rearrange("(k p) n -> p k n", p=P)).then_inc(o_in, 16)
                    sp.wait_ge(x_in, 16)

                @block.gpsimd
                def _(pl):
                    pl.memset(ident[:, :], 0.0).then_inc(ident0, 1)
                    pl.wait_ge(ident0, 1)
                    pl.affine_select(out=ident[:, :], in_=ident[:, :], compare_op=ALU.not_equal, fill=1.0,
                                     base=0, pattern=[[-1, P]], channel_multiplier=1).then_inc(ident_ok, 1)
                    pl.memset(zeros[:, :], 0.0).then_inc(z_ok, 1)
                    pl.wait_ge(ident_ok, 1)

            norm_phase("n1_")

            bankT = ps("bankT", [P, KC, P])
            bankJ = [ps(f"bankJ{i}", [P, CK]) for i in range(2)]
            bankS = [ps(f"bankS{i}", [P, CK]) for i in range(2)]
            bankP = ps("bankP", [P, KC, P])
            bankO = ps("bankO", [P, NP, 2 * DH])
            bankX = ps("bankX", [P, D])

            w_ok, c_hi = sem("wkv_split"), sem("ctxT_H_ready")
            chain = sem("a_dve_chain")
            bqs_ok = sem("bqs_ready")
            q_mm, q_ok = sem("q_projected"), sem("qT_ready")
            mask_ok, qb = sem("head_mask_ready"), sem("q_blocks_ready")
            t_mm, t_cp = sem("ctx_turned"), sem("ctxT_copied")
            j_mm, j_cp = sem("kv_projected"), sem("kv_copied")
            s_mm, s_max = sem("scores_ready"), sem("max_ready")
            s_exp = sem("probs_ready")
            p_mm, p_cp = sem("probs_turned"), sem("probT_copied")
            o_mm = sem("pv_done")
            c_cp = sem("context_copied")
            ct_mm, ct_cp = sem("context_turned"), sem("contextT_copied")
            y_mm, y_add = sem("wo_done"), sem("x_added")
            xbo = sem("bo_added")

            with nc.Block() as block:
                @block.sync
                def _(sp):
                    sp.wait_ge(z_ok, 1)
                    sp.dma_start(xs_d.rearrange("(s p) d -> p s d", p=P),
                                 zeros[:, :].unsqueeze(1).to_broadcast([P, NS, D])).then_inc(xs_zero, 16)
                    with sp.Fori(0, NT - 1) as t:
                        for b in range(2):
                            sp.wait_ge(t_mm, KD * (2 * t + b + 1))
                            sp.dma_start(ctxs[:, b, :, :], ctx_d[ds(2 * t + b + 2, 1)].rearrange(
                                "g (k p) d -> p (g k) d", p=P)).then_inc(ctx_in[b], 16)
                    sp.wait_ge(xs_zero, 16)

                @block.gpsimd
                def _(pl):
                    def place(g, b):
                        for e in range(2):
                            pl.tensor_tensor(qbd[b][:, :, e * S:e * S + S], QT[:, :, ds(g * S, S)],
                                             head_of[:, e:e + 1].unsqueeze(2).to_broadcast([P, KD, S]),
                                             ALU.mult).then_inc(qb, 1)
                    pl.wait_ge(mask_ok, 6)
                    pl.wait_ge(q_ok, 2 + KD * 2)
                    for b in range(2):
                        place(b, b)
                    pl.wait_ge(b_in, 64)
                    for t in range(NT):
                        pl.tensor_tensor(xres[:, t, :], xres[:, t, :], bo[:, :], ALU.add).then_inc(xbo, 1)
                    with pl.Fori(0, NT - 1) as t:
                        for b in range(2):
                            pl.wait_ge(s_mm, NP * (2 * t + b + 1))
                            place(2 * t + b + 2, b)

                @block.tensor
                def _(pe):
                    pe.sem_inc(p_mm, 2)
                    pe.sem_inc(o_mm, 2)
                    def turn(g, b, j):
                        if j == 0:
                            pe.wait_ge(ctx_in[b], 16 * (g // 2 + 1) if isinstance(g, int) else g * 8 + (16 - 8 * b))
                        pe.wait_ge(t_cp, KD * g + j + 1)
                        for k in range(KC):
                            mm = pe.transpose(bankT[:, k, :], ctxs[:, b, k, j * P:(j + 1) * P], ident[:, :])
                        mm.then_inc(t_mm, 1)

                    def project(g, b, u):
                        if u == 0:
                            pe.wait_ge(t_cp, 1 + KD * (g + 1))
                        pe.wait_ge(j_cp, NP * g + u + 1)
                        for k in range(KD):
                            for l, r in ((0, 0), (0, 1), (1, 0)):
                                if u < KD:
                                    lhs, rhs = Wk[:, l, k, u * P:(u + 1) * P], ctxT[:, b, r, k, :]
                                else:
                                    lhs, rhs = ctxT[:, b, l, k, (u - KD) * P:(u - KD + 1) * P], Wv[:, r, k, :]
                                mm = pe.matmul(bankJ[u % 2][:, :], lhs, rhs, start=(k == l == r == 0),
                                               stop=(k == KD - 1 and l == 1))
                        mm.then_inc(j_mm, 1)

                    def scores(g, b, u):
                        if u == 0:
                            pe.wait_ge(qb, 2 * (g + 1))
                        pe.wait_ge(j_cp, 2 + NP * g + u // 2 + 1)
                        pe.wait_ge(s_exp, NP * g + u + 1)
                        r = slice(64 * (u % 2), 64 * (u % 2) + 64)
                        pe.matmul(bankS[u % 2][:, :], qbd[b][r, u // 2, :], KT[r, b, u // 2, :],
                                  start=True, stop=True).then_inc(s_mm, 1)

                    def turn_probs(g, u):
                        n = NP * g + u
                        pe.wait_ge(s_exp, 2 + n + 1)
                        pe.wait_ge(p_cp, n + 1)
                        for k in range(KC):
                            mm = pe.transpose(bankP[:, k, :], prob[:, u % 2, k * P:(k + 1) * P], ident[:, :])
                        mm.then_inc(p_mm, 1)

                    def values(g, b, u):
                        if u == 0:
                            pe.wait_ge(c_cp, 2 * g + 2)
                            pe.wait_ge(j_cp, 2 + NP * (g + 1))
                        pe.wait_ge(p_cp, 1 + NP * g + u + 1)
                        for k in range(KC):
                            mm = pe.matmul(bankO[:, u, :], probT[:, u % 2, k, :], V[:, b, k, 64 * u:64 * u + 64],
                                           start=(k == 0), stop=(k == KC - 1))
                        mm.then_inc(o_mm, 1)

                    def batch(g, b, nxt, nxt2, fin=None):
                        scores(g, b, 0)
                        for u in range(NP):
                            if nxt:
                                project(g + 1, 1 - b, u)
                            if fin is not None and u == 1:
                                turn_context(fin)
                            if fin is not None and u == 3:
                                output(fin)
                            if u + 1 < NP:
                                scores(g, b, u + 1)
                            if nxt2 and u % 2 == 0:
                                turn(g + 2, b, u // 2)
                            turn_probs(g, u)
                            if u:
                                values(g, b, u - 1)
                        values(g, b, NP - 1)

                    def turn_context(t):
                        pe.wait_ge(c_cp, 2 + 4 * (t + 1))
                        pe.wait_ge(y_add, t + 1)
                        for k in range(KD):
                            mm = pe.transpose(bankX[:, k * P:(k + 1) * P], cn[:, k * P:(k + 1) * P], ident[:, :])
                        mm.then_inc(ct_mm, 1)

                    def output(t):
                        pe.wait_ge(ct_cp, KD * (t + 1))
                        for k in range(KD):
                            mm = pe.matmul(bankX[:, :], cnT[:, k, :], Wo[:, k, :], start=(k == 0), stop=(k == KD - 1))
                        mm.then_inc(y_mm, 1)

                    pe.wait_ge(wq_in, 16)
                    for n in range(2 * KD):
                        m, h = n % KD, n // KD
                        pe.wait_ge(q_ok, n + 1)
                        for k in range(KD):
                            mm = pe.matmul(bankJ[n % 2][:, :], Wq[:, k, m * P:(m + 1) * P],
                                           xnT[:, k, h * CK:(h + 1) * CK], start=(k == 0), stop=(k == KD - 1))
                        mm.then_inc(q_mm, 1)
                        if n % 2:
                            turn(0, 0, n // 2)
                    pe.wait_ge(w_ok, 4)
                    pe.wait_ge(q_ok, 2 + 2 * KD)
                    for u in range(NP):
                        project(0, 0, u)
                        if u % 2:
                            turn(1, 1, u // 2)
                    pe.wait_ge(o_in, 16)
                    batch(0, 0, True, True)
                    batch(1, 1, True, True)
                    with pe.Fori(0, NT - 2) as i:
                        batch(2 * i + 2, 0, True, True, fin=i)
                        batch(2 * i + 3, 1, True, True)
                    batch(B - 2, 0, True, False, fin=NT - 2)
                    batch(B - 1, 1, False, False)
                    turn_context(NT - 1)
                    output(NT - 1)

                @block.scalar
                def _(act):
                    act.sem_inc(q_ok, 2)
                    act.sem_inc(j_cp, 2)
                    act.sem_inc(s_exp, 2)
                    act.wait_ge(b_in, 64)
                    act.activation(bqs[:, :], bias["bq"][:, :], ACT.Copy, scale=SCALE).then_inc(bqs_ok, 1)
                    act.wait_ge(bqs_ok, 1)
                    for n in range(2 * KD):
                        m, h = n % KD, n // KD
                        act.wait_ge(q_mm, n + 1)
                        act.activation(QT[:, m, h * CK:(h + 1) * CK], bankJ[n % 2][:, :], ACT.Identity,
                                       bias=bqs[:, m:m + 1], scale=SCALE).then_inc(q_ok, 1)

                    def copy_kv(g, b, u):
                        act.wait_ge(j_mm, NP * g + u + 1)
                        if u < KD:
                            act.activation(KT[:, b, u, :], bankJ[u % 2][:, :], ACT.Identity,
                                           bias=bias["bk"][:, u:u + 1]).then_inc(j_cp, 1)
                        else:
                            act.activation(V[:, b, u - KD, :], bankJ[u % 2][:, :], ACT.Copy).then_inc(j_cp, 1)

                    def batch(g, b, nxt, fin=None):
                        for u in range(NP):
                            n = NP * g + u
                            act.wait_ge(s_max, n + 1)
                            act.wait_ge(p_mm, n + 1)
                            act.activation(prob[:, u % 2, :], bankS[u % 2][:, :], ACT.Exp,
                                           bias=nmax[:, b, u:u + 1],
                                           accum_out=rsum[:, b, u:u + 1]).then_inc(s_exp, 1)
                            if nxt:
                                if u == KD:
                                    act.wait_ge(o_mm, NP * g + 2)
                                copy_kv(g + 1, 1 - b, u)
                            if fin is not None and u == 1:
                                finish(fin)

                    def finish(t):
                        act.wait_ge(ct_mm, t + 1)
                        for k in range(KD):
                            act.activation(cnT[:, k, :], bankX[:, k * P:(k + 1) * P], ACT.Identity,
                                           bias=bias["bv"][:, k:k + 1]).then_inc(ct_cp, 1)

                    for u in range(NP):
                        copy_kv(0, 0, u)
                    batch(0, 0, True)
                    batch(1, 1, True)
                    with act.Fori(0, NT - 2) as i:
                        batch(2 * i + 2, 0, True, fin=i)
                        batch(2 * i + 3, 1, True)
                    batch(B - 2, 0, True, fin=NT - 2)
                    batch(B - 1, 1, False)
                    finish(NT - 1)

                @block.vector
                def _(dve):
                    dve.sem_inc(t_cp, 1)
                    dve.sem_inc(p_cp, 1)
                    dve.sem_inc(c_cp, 2)
                    dve.sem_inc(y_add, 1)
                    c = Chain(dve, chain)
                    for e in range(2):
                        dve.memset(head_of[:, e:e + 1], 0.0).then_inc(mask_ok, 1)
                    dve.wait_ge(mask_ok, 2)
                    for hh in range(P // DH):
                        dve.memset(head_of[DH * hh:DH * hh + DH, hh % 2:hh % 2 + 1], 1.0).then_inc(mask_ok, 1)

                    def copy_ctx(g, b, j):
                        if j == 0 and not (isinstance(g, int) and g < 2):
                            dve.wait_ge(j_mm, NP * (g - 1))
                        dve.wait_ge(t_mm, KD * g + j + 1)
                        rows = bankT[:, :, :].rearrange("p a b -> p (a b)")
                        dve.tensor_copy(ctxT[:, b, 0, j, :], rows).then_inc(c_hi, 1)
                        dve.wait_ge(c_hi, KD * g + j + 1)
                        dve.tensor_tensor(ctxT[:, b, 1, j, :], rows, ctxT[:, b, 0, j, :], ALU.subtract).then_inc(t_cp, 1)

                    def row_max(g, b, u):
                        dve.wait_ge(s_mm, NP * g + u + 1)
                        dve.tensor_reduce(nmax[:, b, u:u + 1], bankS[u % 2][:, :], AX.X, ALU.max,
                                          negate=True).then_inc(s_max, 1)

                    def copy_probs(g, u):
                        n = NP * g + u
                        dve.wait_ge(p_mm, 2 + n + 1)
                        dve.wait_ge(o_mm, n + 1)
                        dve.tensor_copy(probT[:, u % 2, :, :], bankP[:, :, :]).then_inc(p_cp, 1)

                    def batch(g, b, nxt2, fin=None):
                        row_max(g, b, 0)
                        for u in range(NP):
                            if u + 1 < NP:
                                row_max(g, b, u + 1)
                            if nxt2 and u % 2 == 0:
                                copy_ctx(g + 2, b, u // 2)
                            copy_probs(g, u)
                            if fin is not None and u == 4:
                                finish(fin)
                        dve.wait_ge(s_exp, 2 + NP * (g + 1))
                        c.link(dve.reciprocal(rinv[:, b, :], rsum[:, b, :]))
                        dve.wait_ge(o_mm, 2 + NP * (g + 1))
                        for h in range(2):
                            r = slice(64 * h, 64 * h + 64)
                            dst = cn[64 * b:64 * b + 64, :].rearrange("p (u e d) -> p u e d", e=2, d=DH)[:, :, h, :]
                            dve.tensor_tensor(dst, bankO[r, :, DH * h:DH * h + DH],
                                              rinv[r, b, :].unsqueeze(2).to_broadcast([64, NP, DH]),
                                              ALU.mult).then_inc(c_cp, 1)

                    def finish(t):
                        dve.wait_ge(y_mm, t + 1)
                        dve.tensor_tensor(xres[:, ds(t, 1), :].rearrange("p a d -> p (a d)"),
                                          xres[:, ds(t, 1), :].rearrange("p a d -> p (a d)"),
                                          bankX[:, :], ALU.add).then_inc(y_add, 1)

                    dve.wait_ge(w_in, 32)
                    for i, (whole_w, split_w) in enumerate(((KT, Wk), (V, Wv))):
                        dve.tensor_copy(split_w[:, 0, :, :], whole_w[:, 1, :, :]).then_inc(w_ok, 1)
                        dve.wait_ge(w_ok, 2 * i + 1)
                        dve.tensor_tensor(split_w[:, 1, :, :], whole_w[:, 1, :, :], split_w[:, 0, :, :],
                                          ALU.subtract).then_inc(w_ok, 1)
                    for j in range(KD):
                        copy_ctx(0, 0, j)
                    for j in range(KD):
                        copy_ctx(1, 1, j)
                    dve.wait_ge(xbo, NT)
                    batch(0, 0, True)
                    batch(1, 1, True)
                    with dve.Fori(0, NT - 2) as i:
                        c.enter(i, 2)
                        batch(2 * i + 2, 0, True, fin=i)
                        batch(2 * i + 3, 1, True)
                        c.leave(NT - 2)
                    batch(B - 2, 0, False, fin=NT - 2)
                    batch(B - 1, 1, False)
                    finish(NT - 1)

        def store_x():
            done = sem0("x_stored")
            with nc.Block() as block:
                @block.sync
                def _(sp):
                    sp.dma_start(out_d.rearrange("(t p) d -> p t d", p=P), xres[:, :, :]).then_inc(done, 16)
                    sp.wait_ge(done, 16)

        if debug == "attention":
            return store_x()
        norm_phase("n2_")
        with ExitStack() as st:
            sb, ps, sem = pool(st)
            NQ = 4
            QT = TOK // NQ
            QB = B // NQ
            TQ = QT // P
            NY = 3
            Win = sb("Win", [P, 2, 2, KD, P])
            Wx = sb("Wx", [P, JD, R + 2 * N])
            Wdt = sb("Wdt", [R, JD, P])
            Wout = sb("Wout", [P, JD, D])
            CD, CT, CB, CW = N, N + 1, N + 2, N + 3
            chan = sb("channel_params", [P, JD, N + 7])
            BC = sb("BC_rows", [P, 2, 2, N, QT])
            xc = sb("xc", [P, 2, JD, QT])
            yz = sb("yz", [P, NY, JD, QT])
            delta = sb("delta", [P, 2, JD, QT])
            xdbl = sb("x_dbl", [R + 2 * N, 2, QT])
            xpad = sb("x_padded", [P, 2, QB, S + 3])
            acc = sb("conv_sum", [P, 2, QT])
            prod = sb("tap_product", [P, 2, QT])
            th = sb("tanh", [P, 2, QT])
            gsum = sb("y_sum", [P, QT])
            spc = sb("log_rest", [P, QT])
            NA = 3
            dA = sb("dA", [P, NA, QT])
            hs = sb("state", [P, 4, QT])
            hc = sb("state_C", [P, 4, QT])
            bc_d = nc.dram_tensor("bc_scratch", (NQ, 2 * N, QT), F32).ap()
            bank_x, bank_d = (ps("bank_" + n, [P, D]) for n in ("x", "dt"))
            bank_z = [ps(f"bank_z{i}", [P, D]) for i in range(2)]
            bankY = [ps(f"bankY{i}", [P, D]) for i in range(2)]
            NX = 3
            bank_dx = [ps(f"bank_dx{i}", [P, 2, QT]) for i in range(2)]
            dx, bx = bank_dx[0][:, 0, :], [bank_dx[(i + 1) // 2][:, (i + 1) % 2, :] for i in range(NX)]

            p_in, wx_in, wdt_in, wo_in = sem("params_in"), sem("wx_in"), sem("wdt_in"), sem("wout_in")
            win_in = [sem(f"win_in{i}") for i in range(2)]
            bc_out = sem("bc_stored")
            bc_in = [sem(f"bc_in{i}") for i in range(N // 4)]
            neg_ok = sem("A_exp_ready")
            x_mm = sem("x_done")
            x_cp = sem("x_copied")
            z_mm = sem("z_done")
            pad_ok, tap = sem("pads_zeroed"), sem("tap_ready")
            TAPS = 3
            added = sem("tap_added")
            z_th, x_th = sem("tanh_z_done"), sem("tanh_x_done")
            zg, xs = sem("gate_done"), sem("xc_done")
            bc_mm, bc_cp = sem("x_dbl_done"), sem("x_dbl_copied")
            d_mm = sem("dt_done")
            abs_ok = sem("abs_ready")
            d_rd = sem("dt_read")
            u_ok = sem("exp_done")
            part_ok, ln_ok = sem("delta_part_ready"), sem("log_done")
            dl_ok = sem("delta_ready")
            da_ok, sc = sem("dA_ready"), sem("state_ready")
            hc_ok = sem("state_C_ready")
            y_mm = sem("y_summed")
            yo = sem("y_gated")
            o_mm, o_ad = sem("out_done"), sem("out_added")
            chain = sem("m_dve_chain")

            def cols(bank, m=P):
                return bank[0:m, 0:QT]

            def uq(q):
                return yz[:, (q + 1) % NY]

            def batches(v):
                return v.rearrange("p (g s) -> p g s", s=S)

            def quarters(slot, step):
                for q in range(NQ + 1):
                    for j in range(JD):
                        for n in range(N):
                            if q < NQ:
                                slot(q, N * j + n)
                            if q > 0:
                                step(q - 1, j, n)

            UNIT, XMM, ZMM, PAD, TAP, ADD = 8, (0, 1, 2, 3), (4, 5, 6, 7), 8, (9, 10, 11, 13), (11, 12, 14)
            TANH_Z, GATE_Z, TANH_X, GATE_X = 13, 14, 17, 19
            XDBL, XCP, D0, DUNIT, LOG, SUM = 76, 84, 86, 3, 117, 123
            OUT = {6 + 36 * t + 4 * j: (t, j) for t in range(TQ) for j in range(JD)}
            ADD_OUT = {39: 0, 76: 1}

            def units(T, first, every):
                u = (T - first) // every
                return [u] if T == first + every * u and 0 <= u < JD else []

            with nc.Block() as block:
                @block.sync
                def _(sp):
                    for q in range(NQ):
                        with sp.Fori(0, JD // 2) as jj:
                            for b in range(2):
                                sp.wait_ge(z_mm, JD * q + 2 * jj + b + 1)
                                for z in range(2):
                                    sp.dma_start(Win[:, b, z, :, :], a["L0_attn_W_in"][
                                        :, ds(z * DI + (2 * jj + b) * P, P)].rearrange("(k p) n -> p k n", p=P)
                                        ).then_inc(win_in[b], 16)
                        sp.wait_ge(bc_cp, 2 * q + 2)
                        sp.dma_start(bc_d[q], xdbl[R:R + 2 * N, q % 2, :]).then_inc(bc_out, 16)
                        sp.wait_ge(bc_out, 16 * q + 16)
                        if q >= 2:
                            sp.wait_ge(yo, 2 + JD * (q - 1))
                        for c4 in range(N // 4):
                            src = bc_d[q].rearrange("(s n) t -> s n t", s=2)[:, 4 * c4:4 * c4 + 4, :]
                            sp.dma_start(BC[:, q % 2, :, 4 * c4:4 * c4 + 4, :],
                                         src.partition_broadcast(P)).then_inc(bc_in[c4], 16)

                @block.gpsimd
                def _(pl):
                    with nc.allow_non_contiguous_dma("channel parameters"):
                        for lo, src in ((0, a["L0_attn_A_log"].rearrange("(j p) n -> p j n", p=P)),
                                        (CD, a["L0_attn_D"].rearrange("(j p o) -> p j o", p=P, o=1)),
                                        (CT, a["L0_attn_b_dt"].rearrange("(j p o) -> p j o", p=P, o=1)),
                                        (CB, a["L0_attn_conv_b"].rearrange("(j p o) -> p j o", p=P, o=1)),
                                        (CW, a["L0_attn_conv_w"].rearrange("(j p) o k -> p j (o k)", p=P))):
                            pl.dma_start(chan[:, :, lo:lo + src.shape[2]], src).then_inc(p_in, 16)
                    pl.dma_start(Wx[:, :, :], a["L0_attn_W_x"].rearrange("(j p) n -> p j n", p=P)).then_inc(wx_in, 16)
                    pl.dma_start(Wdt[:, :, :], a["L0_attn_W_dt"].rearrange("r (j p) -> r j p", p=P)).then_inc(wdt_in, 16)
                    pl.dma_start(Wout[:, :, :], a["L0_attn_W_out"].rearrange("(j p) n -> p j n", p=P)).then_inc(wo_in, 16)
                    pl.sem_inc(hc_ok, 4)
                    pl.sem_inc(added, 2 * TAPS)
                    pl.memset(xpad[:, :, :, 0:3], 0.0).then_inc(pad_ok, 1)

                    def add_tap(q, u, k):
                        m = TAPS * (JD * q + u) + k
                        pl.wait_ge(tap, m + JD * q + u + 2)
                        pl.wait_ge(added, 2 * TAPS + m)
                        pl.tensor_tensor(acc[:, u % 2, :], acc[:, u % 2, :], prod[:, m % 2, :],
                                         ALU.add).then_inc(added, 1)

                    def slot(q, T):
                        for k in range(TAPS):
                            for u in units(T, ADD[k], UNIT):
                                add_tap(q, u, k)

                    def step(q, j, n):
                        i = (q * JD + j) * N + n
                        if j == 0 and n == 0:
                            for c4 in range(N // 4):
                                pl.wait_ge(bc_in[c4], 16 * q + 16)
                        pl.wait_ge(sc, NA + i + 1)
                        pl.wait_ge(y_mm, i + 1)
                        pl.tensor_tensor(hc[:, n % 4, :], hs[:, n % 4, :], BC[:, q % 2, 1, n, :],
                                         ALU.mult).then_inc(hc_ok, 1)

                    quarters(slot, step)

                @block.tensor
                def _(pe):
                    for s, v in ((z_mm, 2), (y_mm, 4)):
                        pe.sem_inc(s, v)

                    def project(q, u, z, k):
                        U, w = JD * q + u, u % 2
                        if k == 0 and z == 0:
                            pe.wait_ge(win_in[w], 16 * (U - w) + 32)
                            pe.wait_ge(x_cp, U + 1)
                        elif k == 0:
                            pe.wait_ge(zg, U + 1)
                        mm = pe.matmul(cols((bank_x, bank_z[w])[z]), Win[:, w, z, k, :],
                                       xnT[:, k, q * QT:(q + 1) * QT], start=(k == 0), stop=(k == KD - 1))
                        if k == KD - 1:
                            mm.then_inc((x_mm, z_mm)[z], 1)

                    def x_dbl(q, js):
                        if js[0] == 0:
                            pe.wait_ge(xs, 2 + JD * (q + 1))
                            pe.wait_ge(x_cp, 1 + JD * (q + 1))
                            pe.wait_ge(wx_in, 16)
                        for j in js:
                            mm = pe.matmul(cols(bank_x, R + 2 * N), Wx[:, j, :], xc[:, q % 2, j, :],
                                           start=(j == 0), stop=(j == JD - 1))
                        if js[-1] == JD - 1:
                            mm.then_inc(bc_mm, 1)

                    def slot(q, T):
                        for z, places in enumerate((XMM, ZMM)):
                            for k, first in enumerate(places):
                                for u in units(T, first, UNIT):
                                    project(q, u, z, k)
                        if 0 <= T - XDBL < JD // 2:
                            x_dbl(q, (2 * (T - XDBL), 2 * (T - XDBL) + 1))
                        for u in units(T, D0, DUNIT):
                            if u == 0:
                                pe.wait_ge(bc_cp, 2 * q + 2)
                                pe.wait_ge(wdt_in, 16)
                                if q > 1:
                                    pe.wait_ge(o_ad, TQ * (q - 1))
                            pe.wait_ge(d_rd, JD * q + u + 1)
                            pe.matmul(cols(bank_d), Wdt[:, u, :], xdbl[0:R, q % 2, :],
                                      start=True, stop=True).then_inc(d_mm, 1)

                    def last_out(j, banks=(bank_x, bank_z[0])):
                        pe.wait_ge(yo, 2 + JD * (NQ - 1) + j + 1)
                        for t in range(TQ):
                            mm = pe.matmul(banks[t][:, :], yz[:, (NQ - 1) % NY, j, t * P:(t + 1) * P], Wout[:, j, :],
                                           start=(j == 0), stop=(j == JD - 1))
                            if j == JD - 1:
                                mm.then_inc(o_mm, 1)

                    def out_part(q, t, js):
                        if js[0] == 0:
                            pe.wait_ge(yo, 2 + JD * (q + 1))
                            pe.wait_ge(wo_in, 16)
                            if TQ * q + t:
                                pe.wait_ge(o_ad, TQ * q + t)
                            if q + 1 < NQ:
                                pe.wait_ge(d_rd, 1 + JD * (q + 2))
                        for j in js:
                            mm = pe.matmul(bank_d[:, :], yz[:, q % NY, j, t * P:(t + 1) * P], Wout[:, j, :],
                                           start=(j == 0), stop=(j == JD - 1))
                        if js[-1] == JD - 1:
                            mm.then_inc(o_mm, 1)

                    def step(q, j, n):
                        J = JD * q + j
                        if n == 0:
                            pe.wait_ge(yo, J + 1)
                        pe.wait_ge(hc_ok, 4 + J * N + n + 1)
                        pe.matmul(bankY[j % 2][:, 0:QT], ident[:, :], hc[:, n % 4, :],
                                  start=(n == 0), stop=(n == N - 1)).then_inc(y_mm, 1)
                        if q > 0 and N * j + n in OUT:
                            t, jo = OUT[N * j + n]
                            out_part(q - 1, t, (jo,))
                        if q == NQ - 1 and j > 0 and n == N - 4:
                            last_out(j - 1)

                    quarters(slot, step)
                    last_out(JD - 1)

                @block.scalar
                def _(act):
                    act.sem_inc(x_cp, 1)
                    act.sem_inc(d_rd, 1)
                    act.wait_ge(p_in, 16 * 5)
                    act.activation(chan[:, :, 0:N], chan[:, :, 0:N], ACT.Exp).then_inc(neg_ok, 1)

                    def pad_x(q, u, k):
                        U, w = JD * q + u, u % 2
                        act.wait_ge(x_mm, U + 1)
                        act.wait_ge(added, TAPS * (U + 1))
                        act.activation(xpad[:, w, :, 3:S + 3], batches(cols(bank_x)), ACT.Copy).then_inc(x_cp, 1)

                    def conv(q, u, k):
                        U, w = JD * q + u, u % 2
                        row, w_k = xpad[:, w, :, k:k + S], chan[:, u, CW + k:CW + k + 1]
                        if k == 0:
                            act.wait_ge(x_cp, 1 + U + 1)
                            act.wait_ge(pad_ok, 1)
                            act.wait_ge(neg_ok, 2)
                            act.wait_ge(xs, U + 1)
                            act.activation(batches(acc[:, w, :]), row, ACT.Identity, bias=chan[:, u, CB:CB + 1],
                                           scale=w_k).then_inc(tap, 1)
                        else:
                            m = TAPS * U + k - 1
                            act.wait_ge(added, 2 * TAPS + m - 1)
                            act.activation(batches(prod[:, m % 2, :]), row, ACT.Copy, scale=w_k).then_inc(tap, 1)

                    def tanh_z(q, u, k):
                        U = JD * q + u
                        act.wait_ge(z_mm, 2 + U + 1)
                        act.wait_ge(zg, 2 + U)
                        act.activation(th[:, 1, :], cols(bank_z[u % 2]), ACT.Tanh, scale=0.5).then_inc(z_th, 1)

                    def tanh_x(q, u, k):
                        U = JD * q + u
                        act.wait_ge(added, 2 * TAPS + TAPS * (U + 1))
                        act.wait_ge(xs, 2 + U)
                        act.activation(th[:, 0, :], acc[:, u % 2, :], ACT.Tanh).then_inc(x_th, 1)

                    def rectify(q, u, k):
                        act.wait_ge(d_mm, JD * q + u + 1)
                        if q > 1 and u == 0:
                            act.wait_ge(o_mm, TQ * (q - 1))
                        v, b = cols(bank_d), chan[:, u, CT:CT + 1]
                        act.activation(uq(q)[:, u, :], v, ACT.Abs, bias=b).then_inc(abs_ok, 1)
                        act.activation(delta[:, q % 2, u, :], v, ACT.Relu, bias=b).then_inc(d_rd, 1)

                    def exp_abs(q, u, k):
                        act.wait_ge(abs_ok, JD * q + u + 1)
                        act.activation(uq(q)[:, u, :], uq(q)[:, u, :], ACT.Exp, scale=-1.0).then_inc(u_ok, 1)

                    def slot(q, T):
                        for what, every, places in (
                                (pad_x, UNIT, (PAD,)), (conv, UNIT, TAP), (tanh_z, UNIT, (TANH_Z,)), (tanh_x, UNIT, (TANH_X,)),
                                (rectify, DUNIT, (D0 + 3,)), (exp_abs, DUNIT, (D0 + 4,))):
                            for k, first in enumerate(places):
                                for u in units(T, first, every):
                                    what(q, u, k)
                        if T == XCP:
                            act.wait_ge(bc_mm, q + 1)
                            for r in (slice(0, R), slice(R, R + 2 * N)):
                                act.activation(xdbl[r, q % 2, :], bank_x[r, 0:QT], ACT.Copy).then_inc(bc_cp, 1)
                        if T == LOG:
                            act.wait_ge(part_ok, 1 + JD * (q + 1))
                            act.activation(uq(q), uq(q), ACT.Ln, bias=1.0).then_inc(ln_ok, 1)

                    def step(q, j, n):
                        i = (JD * q + j) * N + n
                        if j in (0, JD // 2) and n == 0:
                            act.wait_ge(dl_ok, 2 * q + 1 + (j > 0))
                            act.wait_ge(neg_ok, 2)
                        act.wait_ge(sc, i + 1)
                        act.activation(batches(dA[:, i % NA, :])[:, :, 1:S], batches(delta[:, q % 2, j, :])[:, :, 1:S],
                                       ACT.Exp, scale=chan[:, j, n:n + 1]).then_inc(da_ok, 1)

                    quarters(slot, step)

                @block.vector
                def _(dve):
                    for s, v in ((xs, 2), (zg, 2), (part_ok, 1), (sc, NA), (yo, 2)):
                        dve.sem_inc(s, v)
                    c = Chain(dve, chain)
                    for n in range(NA):
                        c.count(dve.memset(batches(dA[:, n, :])[:, :, 0:1], 0.0))
                    dve.wait_ge(neg_ok, 1)
                    c.link(dve.tensor_scalar(chan[:, :, CB:], chan[:, :, CB:], 0.5, None, ALU.mult))
                    dve.tensor_scalar(chan[:, :, 0:N], chan[:, :, 0:N], -1.0, None, ALU.mult).then_inc(neg_ok, 1)
                    last = {"bx": {}}

                    def gate_x(q, u, part):
                        dve.wait_ge(x_th, JD * q + u + 1)
                        dve.scalar_tensor_tensor(xc[:, q % 2, u, :], th[:, 0, :], 1.0, acc[:, u % 2, :],
                                                 ALU.add, ALU.mult).then_inc(xs, 1)

                    def gate_z(q, u, part):
                        dve.wait_ge(z_th, JD * q + u + 1)
                        dve.scalar_tensor_tensor(yz[:, q % NY, u, :], th[:, 1, :], 1.0, cols(bank_z[u % 2]),
                                                 ALU.add, ALU.mult).then_inc(zg, 1)

                    def log_rest(q, u, part):
                        U, uu, dl = JD * q + u, uq(q)[:, u, :], delta[:, q % 2, u, :]
                        if part == 0:
                            dve.wait_ge(u_ok, U + 1)
                            dve.wait_ge(part_ok, U + 1)
                            last["rest"] = c.count(dve.tensor_scalar(spc[:, :], uu, 1.0, -1.0, ALU.add, ALU.add))
                        elif part == 1:
                            dve.wait_ge(chain, last["rest"])
                            last["rest"] = c.count(dve.tensor_tensor(spc[:, :], uu, spc[:, :], ALU.subtract))
                        else:
                            dve.wait_ge(chain, last["rest"])
                            dve.tensor_tensor(dl, dl, spc[:, :], ALU.add).then_inc(part_ok, 1)

                    def slot(q, T):
                        for what, first, every, parts in ((gate_z, GATE_Z, UNIT, 1), (gate_x, GATE_X, UNIT, 1), (log_rest, D0 + 6, DUNIT, 3)):
                            for part in range(parts):
                                for u in units(T, first + part, every):
                                    what(q, u, part)
                        if T in (SUM, SUM + 1):
                            dve.wait_ge(ln_ok, q + 1)
                            h = slice(0, JD // 2) if T == SUM else slice(JD // 2, JD)
                            dl = delta[:, q % 2, h, :]
                            dve.tensor_tensor(dl, dl, uq(q)[:, h, :], ALU.add).then_inc(dl_ok, 1)

                    def prepare(q, j):
                        if JD * q + j:
                            dve.wait_ge(chain, last["bx"][N - 1])
                        if j == 0:
                            dve.wait_ge(dl_ok, 2 * q + 2)
                            for c4 in range(N // 4):
                                dve.wait_ge(bc_in[c4], 16 * q + 16)
                        last["dx"] = c.count(dve.tensor_tensor(dx, delta[:, q % 2, j, :],
                                                               xc[:, q % 2, j, :], ALU.mult))

                    def drive(q, j, n):
                        i = (JD * q + j) * N + n
                        if n == 0:
                            dve.wait_ge(chain, last["dx"])
                        if i >= NX:
                            dve.wait_ge(sc, NA + i - NX + 1)
                        last["bx"][n] = c.count(dve.tensor_tensor(bx[i % NX], dx,
                                                                  BC[:, q % 2, 0, n, :], ALU.mult))

                    def gate_y(q, j, part):
                        if part == 0:
                            dve.wait_ge(y_mm, 4 + N * (JD * q + j + 1))
                            dve.wait_ge(yo, 2 + JD * q + j)
                            last["gate"] = c.count(dve.scalar_tensor_tensor(
                                gsum[:, :], xc[:, q % 2, j, :], chan[:, j, CD:CD + 1], bankY[j % 2][:, 0:QT],
                                ALU.mult, ALU.add))
                        else:
                            dve.wait_ge(chain, last["gate"])
                            g = yz[:, q % NY, j, :]
                            dve.scalar_tensor_tensor(g, gsum[:, :], 0.5, g, ALU.mult, ALU.mult).then_inc(yo, 1)

                    def add_out(q, t):
                        dve.wait_ge(o_mm, TQ * q + t + 1)
                        xr = xres[:, TQ * q + t, :]
                        bank = bank_d if q < NQ - 1 else (bank_x, bank_z[0])[t]
                        dve.tensor_tensor(xr, xr, bank[:, :], ALU.add).then_inc(o_ad, 1)

                    def step(q, j, n):
                        i = (JD * q + j) * N + n
                        if i == 0:
                            prepare(0, 0)
                            drive(0, 0, 0)
                        need = last["bx"][n]
                        before, after = divmod(JD * q + j - 1, JD), divmod(JD * q + j + 1, JD)
                        if i >= N and n in (5, 6):
                            gate_y(*before, n - 5)
                        if q > 0 and N * j + n in ADD_OUT:
                            add_out(q - 1, ADD_OUT[N * j + n])
                        if n < N - 1:
                            drive(q, j, n + 1)
                        elif after[0] < NQ:
                            prepare(*after)
                            drive(*after, 0)
                        dve.wait_ge(chain, need)
                        dve.wait_ge(da_ok, i + 1)
                        dve.wait_ge(hc_ok, i + 1)
                        dve.tensor_tensor_scan(hs[:, n % 4, :], dA[:, i % NA, :], bx[i % NX],
                                               0.0, ALU.mult, ALU.add).then_inc(sc, 1)

                    quarters(slot, step)
                    for part in range(2):
                        gate_y(NQ - 1, JD - 1, part)
                    for t in range(TQ):
                        add_out(NQ - 1, t)
        if debug == "mamba":
            return store_x()

        pos = sb0("slot_of_choice", [P, 2, NT], I32)
        prob2 = sb0("choice_prob", [P, 2, NT])
        eid = sb0("expert_of_slot_tile", [P, NS], I32)
        wbuf = sb0("weight_buffer_of_slot_tile", [P, NS], I32)
        with ExitStack() as st:
            sb, ps, sem = pool(st)
            xrow = sb("xn_rows", [P, NT, D])
            rw = sb("router_wT", [P, KD, E])
            rb = sb("router_b", [P, E])
            bankL = ps("bankL", [P, 512])
            r_in, l_mm = sem("router_in"), sem("logits_done")

            def load_router(sp):
                with nc.allow_non_contiguous_dma("router weights by model dimension"):
                    for k in range(KD):
                        sp.dma_start(rw[:, k, :], a["L0_ffn_router_w"][:, k * P:(k + 1) * P].rearrange("e p -> p e"),
                                     allow_slow_non_contiguous=True).then_inc(r_in, 16)
                sp.dma_start(rb[:, :], a["L0_ffn_router_b"].partition_broadcast(P)).then_inc(r_in, 16)
                sp.wait_ge(r_in, 16 * (KD + 1))

            def logits(pe, t):
                if t == 0:
                    pe.wait_ge(r_in, 16 * (KD + 1))
                for k in range(KD):
                    mm = pe.matmul(bankL[:, t * E:(t + 1) * E], xnT[:, k, t * P:(t + 1) * P], rw[:, k, :],
                                   start=(k == 0), stop=(k == KD - 1))
                if t == NT - 1:
                    mm.then_inc(l_mm, 1)
            norm_phase("n3_", keep=xrow, load=load_router, use=logits)
            ones, before = sb("ones", [P, P]), sb("rows_before", [P, P])
            iE, iJ, iS = sb("iota_e_minus_E", [P, E]), sb("iota_tile_rows", [P, NT]), sb("iota_slot_tile", [P, NS])
            names = ("logits", "masked", "eq", "cand", "one1", "one2", "sel", "where_", "q1", "q2")
            lg, lg2, eq, cand, one1, one2, sel, where, q1, q2 = (sb("r_" + n, [P, NT, E]) for n in names)
            csel = sb("sel_of_tiles_before", [P, NT + 1, E])
            m1, m2, i1, i2, dif, e2, den, p1f, p2f = (sb("r_m%d" % n, [P, NT]) for n in range(9))
            cnt, ntile = sb("expert_count", [P, E]), sb("expert_tiles", [P, E])
            ends = sb("expert_tile_starts", [P, E + 1])
            rows0 = sb("expert_first_row", [P, E])
            more = sb("tile_needed", [P, E, NT])
            past = sb("expert_is_past", [P, NS, E])
            pastn = sb("experts_past", [P, NS])
            change, hold, parity = (sb(n, [P, NS]) for n in ("expert_change", "one_minus_2_change", "change_parity"))
            bankR, bankC = (ps("bank" + n, [P, 512]) for n in "RC")
            io_ok, bf_ok = sem("iota_ready"), sem("rows_before_ready")
            one_ok = sem("ones_ready")
            sel_ok, r_mm = sem("choices_ready"), sem("ranks_done")
            dif_ok, e2_ok = sem("logit_gap_ready"), sem("gap_exp_ready")
            pos_ok, sc_done, chain = sem("slots_ready"), sem("rows_scattered"), sem("r_dve_chain")

            def tE(v):
                return v.unsqueeze(2).to_broadcast([P, NT, E])

            def eT(v):
                return v.unsqueeze(1).to_broadcast([P, NT, E])

            with nc.Block() as block:
                @block.gpsimd
                def _(pl):
                    for v, base, step in ((iE, -E, 1), (iJ, 0, P), (iS, 0, 1)):
                        pl.iota(v[:, :], pattern=[[step, v.shape[1]]], base=base, channel_multiplier=0,
                                allow_small_or_imprecise_dtypes=True).then_inc(io_ok, 1)
                    pl.memset(ones[:, :], 1.0).then_inc(one_ok, 1)
                    pl.wait_ge(one_ok, 1)
                    pl.affine_select(out=before[:, :], in_=ones[:, :], compare_op=ALU.is_gt, fill=0.0,
                                     base=0, pattern=[[1, P]], channel_multiplier=-1).then_inc(bf_ok, 1)
                    pl.wait_ge(xs_zero, 16)
                    pl.wait_ge(pos_ok, 2)
                    for k in range(2):
                        for t in range(NT):
                            pl.indirect_dma_start(xs_d, bass.IndirectOffsetOnAxis(ap=pos[:, k, t:t + 1], axis=0),
                                                  xrow[:, t, :], None).then_inc(sc_done, 16)
                    pl.wait_ge(sc_done, 16 * 2 * NT)

                @block.tensor
                def _(pe):
                    pe.wait_ge(bf_ok, 1)
                    pe.wait_ge(sel_ok, 1)
                    pe.matmul(bankR[:, 0:NT * E], before[:, :], sel[:, :, :].rearrange("p t e -> p (t e)"),
                              start=True, stop=False)
                    pe.matmul(bankR[:, 0:NT * E], ones[:, :], csel[:, 0:NT, :].rearrange("p t e -> p (t e)"),
                              start=False, stop=True).then_inc(r_mm, 1)
                    pe.matmul(bankC[:, 0:E], ones[:, :], csel[:, NT, :], start=True, stop=True).then_inc(r_mm, 1)

                @block.scalar
                def _(act):
                    act.wait_ge(dif_ok, 1)
                    act.activation(e2[:, :], dif[:, :], ACT.Exp).then_inc(e2_ok, 1)

                @block.vector
                def _(dve):
                    c = Chain(dve, chain)

                    def tt(o, x, y, op):
                        c.link(dve.tensor_tensor(o, x, y, op))

                    def first_max(src, m, i, one):
                        c.link(dve.tensor_reduce(m[:, :], src[:, :, :], AX.X, ALU.max))
                        tt(eq[:, :, :], src[:, :, :], tE(m[:, :]), ALU.is_equal)
                        tt(cand[:, :, :], eq[:, :, :], eT(iE[:, :]), ALU.mult)
                        c.link(dve.tensor_reduce(i[:, :], cand[:, :, :], AX.X, ALU.min))
                        tt(one[:, :, :], eT(iE[:, :]), tE(i[:, :]), ALU.is_equal)

                    dve.wait_ge(l_mm, 1)
                    dve.wait_ge(io_ok, 3)
                    tt(lg[:, :, :], bankL[:, 0:NT * E].rearrange("p (t e) -> p t e", e=E), eT(rb[:, :]), ALU.add)
                    first_max(lg, m1, i1, one1)
                    c.link(dve.scalar_tensor_tensor(lg2[:, :, :], one1[:, :, :], -3e38, lg[:, :, :], ALU.mult, ALU.add))
                    first_max(lg2, m2, i2, one2)
                    dve.tensor_tensor(dif[:, :], m2[:, :], m1[:, :], ALU.subtract).then_inc(dif_ok, 1)
                    tt(sel[:, :, :], one1[:, :, :], one2[:, :, :], ALU.add)
                    c.link(dve.memset(csel[:, 0, :], 0.0))
                    for t in range(NT):
                        ins = dve.tensor_tensor(csel[:, t + 1, :], csel[:, t, :], sel[:, t, :], ALU.add)
                        if t + 1 < NT:
                            c.link(ins)
                    ins.then_inc(sel_ok, 1)
                    dve.wait_ge(e2_ok, 1)
                    c.link(dve.tensor_scalar(den[:, :], e2[:, :], 1.0, None, ALU.add))
                    c.link(dve.reciprocal(prob2[:, 0, :], den[:, :]))
                    tt(prob2[:, 1, :], prob2[:, 0, :], e2[:, :], ALU.mult)
                    dve.wait_ge(r_mm, 2)
                    c.link(dve.tensor_copy(cnt[:, :], bankC[:, 0:E]))
                    tt(more[:, :, :], cnt[:, :].unsqueeze(2).to_broadcast([P, E, NT]),
                       iJ[:, :].unsqueeze(1).to_broadcast([P, E, NT]), ALU.is_gt)
                    c.link(dve.tensor_reduce(ntile[:, :], more[:, :, :], AX.X, ALU.add))
                    c.link(dve.memset(ends[:, 0:1], 0.0))
                    for e in range(E):
                        tt(ends[:, e + 1:e + 2], ends[:, e:e + 1], ntile[:, e:e + 1], ALU.add)
                    c.link(dve.tensor_scalar(rows0[:, :], ends[:, 0:E], float(P), None, ALU.mult))
                    tt(where[:, :, :], bankR[:, 0:NT * E].rearrange("p (t e) -> p t e", e=E), eT(rows0[:, :]), ALU.add)
                    for k, (one, q, f) in enumerate(((one1, q1, p1f), (one2, q2, p2f))):
                        tt(q[:, :, :], one[:, :, :], where[:, :, :], ALU.mult)
                        c.link(dve.tensor_reduce(f[:, :], q[:, :, :], AX.X, ALU.add))
                        dve.tensor_copy(pos[:, k, :], f[:, :]).then_inc(pos_ok, 1)
                    tt(past[:, :, :], ends[:, 1:E + 1].unsqueeze(1).to_broadcast([P, NS, E]),
                       iS[:, :].unsqueeze(2).to_broadcast([P, NS, E]), ALU.is_le)
                    c.link(dve.tensor_reduce(pastn[:, :], past[:, :, :], AX.X, ALU.add))
                    c.link(dve.tensor_scalar(pastn[:, :], pastn[:, :], float(E - 1), None, ALU.min))
                    c.link(dve.tensor_copy(eid[:, :], pastn[:, :]))
                    c.link(dve.memset(change[:, 0:1], 0.0))
                    tt(change[:, 1:NS], pastn[:, 1:NS], pastn[:, 0:NS - 1], ALU.is_gt)
                    c.link(dve.tensor_scalar(hold[:, :], change[:, :], -2.0, 1.0, ALU.mult, ALU.add))
                    c.link(dve.tensor_tensor_scan(parity[:, :], hold[:, :], change[:, :], 0.0, ALU.mult, ALU.add))
                    c.link(dve.tensor_copy(wbuf[:, :], parity[:, :]))

        with ExitStack() as st:
            sb, ps, sem = pool(st)
            V_, W_, O_ = range(3)
            PCS = 4
            PER = 3 * PCS
            COLS = KD * FH // PCS
            w_all = [sb(n, [P, 2, PCS, COLS]) for n in ("Ve", "We", "Woe")]
            ring = sb("weight_pieces_HL", [P, PCS, 2, COLS], F32R)
            xs = sb("slot_rows", [P, 2, D])
            xT = sb("slot_rowsT_HL", [P, 2, 2, KD, P], F32R)
            gate_ = sb("silu_b", [P, 2, 512])
            y = sb("hidden", [P, JF, P])
            yT = sb("hiddenT_HL", [P, 2, JF, P], F32R)
            osb = sb("slot_out", [P, 2, D])
            bankA = [ps(f"bankA{i}", [P, 512]) for i in range(2)]
            bankB = [ps(f"bankB{i}", [P, 512]) for i in range(2)]
            bankT = [ps(f"bankYT{i}", [P, KD, P]) for i in range(2)]
            bankX, bankO = ps("bankXT", [P, KD, P]), ps("bankOut", [P, D])
            in_ = [[sem(f"{n}_in{i}") for i in range(2)] for n in ("ve", "we", "woe")]
            x_in2 = [sem(f"slot_in{i}") for i in range(2)]
            hi, lo = sem("piece_H_ready"), sem("piece_L_ready")
            HEAD = 2 * PER
            used = sem("piece_used")
            x_tr = sem("slot_rows_turned")
            x_hi, x_cp = sem("slot_rowsT_H_ready"), sem("slot_rowsT_ready")
            g_ok = sem("silu_ready")
            y_ok = sem("hidden_ready")
            y_tr, y_hi = sem("hidden_turned"), sem("hiddenT_H_ready")
            y_cp = sem("hiddenT_ready")
            o_cp = sem("slot_out_copied")
            o_st = [sem(f"slot_out_stored{i}") for i in range(2)]
            last = NS - 1

            def tiles(eng, first, step):
                pairs = (last - 1 - first) // 2
                with eng.Fori(0, pairs) as i:
                    for h in range(2):
                        step(2 * i + first + h, (first + h) % 2)
                for s in range(first + 2 * pairs, last + 1):
                    step(s, s % 2)

            def use(s, b):
                return (s - b) * 8 + 16

            def piece(s, m, k):
                if isinstance(s, int) and s in (0, last + 1):
                    return PER * s - (PCS if s else 0) + PCS * (m if s == 0 else 0) + k
                return PER * s + (PCS * (m - 1) + k)

            def buffer_of(eng, s):
                return eng.value_load(wbuf[0:1, ds(s, 1)], min_val=0, max_val=1)

            def whole_piece(m, buf, k):
                return w_all[m][:, ds(buf, 1), k, :].rearrange("p b n -> p (b n)")

            def out_piece(s):
                return piece(s + 1, O_, PCS - 1)

            with nc.Block() as block:
                @block.sync
                def _(sp):
                    def step(s, b):
                        e = sp.value_load(eid[0:1, ds(s, 1)], min_val=0, max_val=E - 1)
                        new, buf = 1, buffer_of(sp, s)
                        if not (isinstance(s, int) and s < 1):
                            new = e != sp.value_load(eid[0:1, ds(s - 1, 1)], min_val=0, max_val=E - 1)
                        sp.wait_ge(x_tr, s + 1)
                        plain(sp)
                        sp.dma_start(xs[:, b, :], xs_d[ds(s * P, P), :]).then_inc(x_in2[b], 16)
                        for m, name in ((V_, "V"), (W_, "W"), (O_, "W_out")):
                            sp.wait_ge(lo, PER * s + (PCS, 2 * PCS, HEAD - PCS)[m])
                            plain(sp)
                            sp.dma_start(w_all[m][:, ds(buf, 1), :, :].rearrange("p b c n -> p (b c n)").rearrange(
                                "p (k f) -> p k f", f=(FH, FH, D)[m]), a["L0_ffn_" + name][ds(e, 1)].rearrange(
                                "e (k p) f -> p (e k) f", p=P), cond=new).then_inc(in_[m][b], 16)
                    step(0, 0)
                    step(1, 1)
                    tiles(sp, 2, step)

                @block.gpsimd
                def _(pl):
                    def step(s, b):
                        pl.wait_ge(o_cp, 1 + s + 1)
                        plain(pl)
                        pl.dma_start(ys_d[ds(s * P, P), :], osb[:, b, :]).then_inc(o_st[b], 16)
                    tiles(pl, 0, step)
                    pl.wait_ge(o_st[0], 16 * ((NS + 1) // 2))
                    pl.wait_ge(o_st[1], 16 * (NS // 2))

                @block.tensor
                def _(pe):
                    for s, v in ((used, PCS), (x_tr, 2)):
                        pe.sem_inc(s, v)

                    def turn_x(s, b):
                        pe.wait_ge(x_in2[b], use(s, b))
                        pe.wait_ge(x_cp, s + 1)
                        for k in range(KD):
                            mm = pe.transpose(bankX[:, k, :], xs[:, b, k * P:(k + 1) * P], ident[:, :])
                        mm.then_inc(x_tr, 1)

                    def up(s, b, m, bank, free):
                        pe.wait_ge(free, 2 * s + 2)
                        for k in range(KD):
                            pe.wait_ge(lo, HEAD + piece(s, m, k) + 1)
                            for l, r in ((0, 0), (0, 1), (1, 0)):
                                for h in range(2):
                                    mm = pe.matmul(bank[h][:, :], xT[:, b, l, k, :],
                                                   ring[:, k, r, 512 * h:512 * h + 512],
                                                   start=(k == l == r == 0), stop=(k == KD - 1 and l == 1))
                            mm.then_inc(used, 1)

                    def turn_y(s):
                        for h in range(2):
                            pe.wait_ge(y_ok, 2 + 2 * s + h + 1)
                            pe.wait_ge(y_cp, 2 * s + h + 1)
                            for k in range(KD):
                                mm = pe.transpose(bankT[h][:, k, :], y[:, KD * h + k, :], ident[:, :])
                            mm.then_inc(y_tr, 1)

                    def down(s, nxt):
                        pe.wait_ge(o_cp, s + 1)
                        pe.wait_ge(y_cp, 2 + 2 * s + 2)
                        for c in range(PCS):
                            pe.wait_ge(lo, HEAD + piece(nxt, O_, c) + 1)
                            for h in range(2):
                                j = 2 * c + h
                                for l, r in ((0, 0), (0, 1), (1, 0)):
                                    mm = pe.matmul(bankO[:, :], yT[:, l, j, :], ring[:, c, r, 512 * h:512 * h + 512],
                                                   start=(j == l == r == 0), stop=(j == JF - 1 and l == 1))
                            mm.then_inc(used, 1)

                    def step(s, b, first=False):
                        pe.wait_ge(x_cp, 1 + s + 1)
                        up(s, b, V_, bankB, g_ok)
                        up(s, b, W_, bankA, y_ok)
                        if not (isinstance(s, int) and s == last):
                            turn_x(s + 1, 1 - b)
                        if not first:
                            down(s - 1, s)
                        turn_y(s)
                    turn_x(0, 0)
                    step(0, 0, first=True)
                    tiles(pe, 1, step)
                    down(last, last + 1)

                @block.scalar
                def _(act):
                    act.sem_inc(g_ok, 2)
                    act.sem_inc(o_cp, 1)

                    def split(s, b, m, k, buf):
                        n = piece(s, m, k)
                        if k == 0:
                            act.wait_ge(in_[m][b], use(s if m != O_ else s - 1, b))
                        act.wait_ge(used, n + 1)
                        plain(act)
                        act.activation(ring[:, k, 0, :], whole_piece(m, buf[m == O_], k), ACT.Copy).then_inc(hi, 1)

                    def x_high(s, b):
                        act.wait_ge(x_tr, 2 + s + 1)
                        act.activation(xT[:, b, 0, :, :], bankX[:, :, :], ACT.Copy).then_inc(x_hi, 1)

                    def copy_out(s, b, stored=True):
                        act.wait_ge(used, PCS + out_piece(s) + 1)
                        if stored:
                            act.wait_ge(o_st[b], (s - b) * 8)
                        act.activation(osb[:, b, :], bankO[:, :], ACT.Copy).then_inc(o_cp, 1)

                    def y_high(s):
                        for h in range(2):
                            act.wait_ge(y_tr, 2 * s + h + 1)
                            act.activation(yT[:, 0, KD * h:KD * h + KD, :], bankT[h][:, :, :], ACT.Copy).then_inc(y_hi, 1)

                    def step(s, b, first=False):
                        buf = (buffer_of(act, s), 0 if first else buffer_of(act, s - 1))
                        for k in range(PCS):
                            split(s, b, V_, k, buf)
                        if not first:
                            y_high(s - 1)
                            if not (isinstance(s, int) and s < 2):
                                copy_out(s - 2, b, stored=not (isinstance(s, int) and s < 4))
                        for k in range(PCS):
                            split(s, b, W_, k, buf)
                        act.wait_ge(used, PCS + piece(s, V_, PCS - 1) + 1)
                        act.wait_ge(y_ok, 2 * s + 2)
                        for h in range(2):
                            act.activation(gate_[:, h, :], bankB[h][:, :], ACT.Silu).then_inc(g_ok, 1)
                        if not first:
                            for k in range(PCS - 1):
                                split(s, 1 - b, O_, k, buf)
                        if not (isinstance(s, int) and s == last):
                            x_high(s + 1, 1 - b)
                        if not first:
                            split(s, 1 - b, O_, PCS - 1, buf)
                    x_high(0, 0)
                    for s in range(4):
                        step(s, s % 2, first=(s == 0))
                    tiles(act, 4, step)
                    y_high(last)
                    copy_out(last - 1, (last - 1) % 2)
                    for k in range(PCS):
                        split(last + 1, last % 2, O_, k, (0, buffer_of(act, last)))
                    copy_out(last, last % 2)

                @block.vector
                def _(dve):
                    dve.sem_inc(lo, HEAD)
                    dve.sem_inc(x_cp, 1)
                    dve.sem_inc(y_ok, 2)
                    dve.sem_inc(y_cp, 2)

                    def rest(s, m, k, buf):
                        dve.wait_ge(hi, piece(s, m, k) + 1)
                        dve.tensor_tensor(ring[:, k, 1, :], whole_piece(m, buf[m == O_], k), ring[:, k, 0, :],
                                          ALU.subtract).then_inc(lo, 1)

                    def x_low(s, b):
                        dve.wait_ge(x_hi, s + 1)
                        dve.tensor_tensor(xT[:, b, 1, :, :], bankX[:, :, :], xT[:, b, 0, :, :],
                                          ALU.subtract).then_inc(x_cp, 1)

                    def y_low(s):
                        for h in range(2):
                            r = slice(KD * h, KD * h + KD)
                            dve.wait_ge(y_hi, 2 * s + h + 1)
                            dve.tensor_tensor(yT[:, 1, r, :], bankT[h][:, :, :], yT[:, 0, r, :],
                                              ALU.subtract).then_inc(y_cp, 1)

                    def step(s, b, first=False):
                        buf = (buffer_of(dve, s), 0 if first else buffer_of(dve, s - 1))
                        for k in range(PCS):
                            rest(s, V_, k, buf)
                        if not first:
                            y_low(s - 1)
                        for k in range(PCS):
                            rest(s, W_, k, buf)
                        if not first:
                            for k in range(PCS - 1):
                                rest(s, O_, k, buf)
                        dve.wait_ge(used, PCS + piece(s, W_, PCS - 1) + 1)
                        if not first:
                            dve.wait_ge(y_tr, 2 * s)
                        for h in range(2):
                            dve.wait_ge(g_ok, 2 + 2 * s + h + 1)
                            dve.tensor_tensor(y[:, KD * h:KD * h + KD, :].rearrange("p k q -> p (k q)"),
                                              bankA[h][:, :], gate_[:, h, :], ALU.mult).then_inc(y_ok, 1)
                        if not (isinstance(s, int) and s == last):
                            x_low(s + 1, 1 - b)
                        if not first:
                            rest(s, O_, PCS - 1, buf)
                    x_low(0, 0)
                    step(0, 0, first=True)
                    tiles(dve, 1, step)
                    y_low(last)
                    for k in range(PCS):
                        rest(last + 1, O_, k, (0, buffer_of(dve, last)))

        with ExitStack() as st:
            sb, ps, sem = pool(st)
            got = sb("expert_rows", [P, 2, NT, D])
            g_in = [sem(f"expert_rows_in{i}") for i in range(NT)]
            chain, done = sem("c_dve_chain"), sem("out_stored")
            f_ok = sem("x_final")
            with nc.Block() as block:
                @block.gpsimd
                def _(pl):
                    for t in range(NT):
                        for k in range(2):
                            pl.indirect_dma_start(got[:, k, t, :], None, ys_d,
                                                  bass.IndirectOffsetOnAxis(ap=pos[:, k, t:t + 1], axis=0)
                                                  ).then_inc(g_in[t], 16)

                @block.vector
                def _(dve):
                    c = Chain(dve, chain)
                    for t in range(NT):
                        dve.wait_ge(g_in[t], 32)
                        for k in range(2):
                            ins = dve.scalar_tensor_tensor(xres[:, t, :], got[:, k, t, :], prob2[:, k, t:t + 1],
                                                           xres[:, t, :], ALU.mult, ALU.add)
                            if k == 0:
                                c.link(ins)
                        ins.then_inc(f_ok, 1)

                @block.sync
                def _(sp):
                    for t in range(NT):
                        sp.wait_ge(f_ok, t + 1)
                        sp.dma_start(out_d[t * P:(t + 1) * P, :], xres[:, t, :]).then_inc(done, 16)
                    sp.wait_ge(done, 16 * NT)


DEBUG = None


def kernel(**inputs):
    import numpy as _np
    import concourse.bacc as _bacc
    from concourse import mybir as _mybir
    from concourse.bass_utils import run_bass_kernel_spmd as _run

    nc = _bacc.Bacc("TRN2", target_bir_lowering=False, num_devices=1)
    arrays, args = {}, {}
    for name, v in inputs.items():
        v = _np.ascontiguousarray(v)
        arrays[f"in_{name}"] = v
        args[name] = nc.dram_tensor(f"in_{name}", v.shape, _mybir.dt.from_np(v.dtype), kind="ExternalInput").ap()
    shape = arrays["in_x"].shape
    out = nc.dram_tensor("out_0", shape, F32, kind="ExternalOutput").ap()
    build(nc, args, out, DEBUG)
    r = _run(nc, [arrays], core_ids=[0])
    return r.results[0]["out_0"]
```
